# Optimizing a Trainium2 kernel written in Bass

```python
import numpy as np
import jax
import jax.numpy as jnp

def _softmax(x, axis=-1):
    return jax.nn.softmax(x, axis=axis)

def _gelu(x):
    return jax.nn.gelu(x, approximate=True)

def _silu(x):
    return jax.nn.silu(x)

def _sigmoid(x):
    return jax.nn.sigmoid(x)

def _layernorm(x, axis=-1, eps=1e-05):
    m = jnp.mean(x, axis=axis, keepdims=True)
    v = jnp.var(x, axis=axis, keepdims=True)
    return (x - m) / jnp.sqrt(v + eps)

def _scatter_add(tgt, idx, src, axis=0):
    return tgt.at[idx].add(src)

def _segment_sum(src, seg, n):
    return jax.ops.segment_sum(src, seg, n)
kernel_name = 'mk_vit_tower_d1_tok_img512_r4_bfeb8d'

def setup_inputs(seed: int=0):
    np.random.seed(seed)
    _w = jnp.asarray

    def _rec_inputs():
        import jax
        import jax.numpy as jnp
        _rk = jax.random.key(seed)
        x = -0.000392918 + 0.999932 * jax.random.normal(jax.random.fold_in(_rk, 1), (64, 1, 128, 128), jnp.float32)
        return x
    x = _rec_inputs()

    def _L0_tok_setup():
        import math
        import jax, jax.numpy as jnp
        import numpy as np
        PW = PH = 16
        EMB = 128
        HID = 128
        B, H, W = (64, 128, 128)
        L = H // PW * (W // PH)
        SIGMA_ZERO = 0.1

        def _f_noise(x):
            return jnp.sign(x) * jnp.sqrt(jnp.abs(x))

        def _noisy_linear(x, w, b, sw, sb, eps_in, eps_out):
            ei = _f_noise(eps_in)
            eo = _f_noise(eps_out)
            w_n = w + sw * (eo[:, None] * ei[None, :])
            b_n = b + sb * eo
            return x @ w_n.T + b_n

        def _unfold_patches(x):
            b = x.shape[0]
            p = x.reshape(b, H // PW, PW, W // PH, PH)
            p = p.transpose(0, 1, 3, 2, 4)
            return p.reshape(b, L, PW * PH)

        def _pos_encoding(x):
            pos = jnp.arange(L, dtype=jnp.float32)[:, None]
            div = jnp.exp(jnp.arange(0, EMB, 2, dtype=jnp.float32) * (-math.log(10000.0) / EMB))
            ang = pos * div
            pe = jnp.stack([jnp.sin(ang), jnp.cos(ang)], axis=-1).reshape(L, EMB)
            return x + pe[None, :, :]
        key = jax.random.key(seed)
        ks = jax.random.split(key, 12)
        in_f = PW * PH
        sig = SIGMA_ZERO / math.sqrt(in_f)
        bnd1 = 1.0 / math.sqrt(in_f)
        bnd3 = 1.0 / math.sqrt(HID)
        u = lambda k, shape, bnd: jax.random.uniform(k, shape, jnp.float32, -bnd, bnd)
        return {'inputs': jax.random.normal(ks[0], (B, 1, H, W), jnp.float32), 'W1_w': u(ks[1], (HID, in_f), bnd1), 'W1_b': u(ks[2], (HID,), bnd1), 'W1_sw': jnp.full((HID, in_f), sig, jnp.float32), 'W1_sb': jnp.full((HID,), sig, jnp.float32), 'W2_w': u(ks[3], (HID, in_f), bnd1), 'W2_b': u(ks[4], (HID,), bnd1), 'W2_sw': jnp.full((HID, in_f), sig, jnp.float32), 'W2_sb': jnp.full((HID,), sig, jnp.float32), 'W3_w': u(ks[5], (EMB, HID), bnd3), 'W3_b': u(ks[6], (EMB,), bnd3), 'eps_in1': jax.random.normal(ks[7], (in_f,), jnp.float32), 'eps_out1': jax.random.normal(ks[8], (HID,), jnp.float32), 'eps_in2': jax.random.normal(ks[9], (in_f,), jnp.float32), 'eps_out2': jax.random.normal(ks[10], (HID,), jnp.float32)}
    _L0_tok_all = _L0_tok_setup()
    _L0_tok_in = {k: v for k, v in _L0_tok_all.items() if k in ('W1_w', 'W1_b', 'W1_sw', 'W1_sb', 'W2_w', 'W2_b', 'W2_sw', 'W2_sb', 'W3_w', 'W3_b', 'eps_in1', 'eps_out1', 'eps_in2', 'eps_out2')}
    del _L0_tok_all

    def _L0_attn_setup():
        import jax, jax.numpy as jnp
        import numpy as np
        B, T, DIM = (4, 512, 128)
        H = 8
        HD = DIM // H
        ALPHA = 100.0
        EPS = 1e-10
        key = jax.random.key(seed)
        k1, k2, k3, k4 = jax.random.split(key, 4)
        x = jax.random.normal(k1, (B, T, DIM), dtype=jnp.float32)
        W_qkv = jax.random.normal(k2, (DIM, 2 * DIM), dtype=jnp.float32) * DIM ** (-0.5)
        W_proj = jax.random.normal(k3, (DIM, DIM), dtype=jnp.float32) * DIM ** (-0.5)
        b_proj = jax.random.normal(k4, (DIM,), dtype=jnp.float32) * 0.01
        return {'x': x, 'W_qkv': W_qkv, 'W_proj': W_proj, 'b_proj': b_proj}
    _L0_attn_all = _L0_attn_setup()
    _L0_attn_in = {k: v for k, v in _L0_attn_all.items() if k in ('W_qkv', 'W_proj', 'b_proj')}
    del _L0_attn_all

    def _L0_ffn_setup():
        import jax, jax.numpy as jnp
        import numpy as np
        TOP_K = 2
        key = jax.random.key(seed)
        k1, k2, k3, k4 = jax.random.split(key, 4)
        B, S, d = (4, 512, 128)
        E, H = (32, 128)
        x = jax.random.normal(k1, (B, S, d), dtype=jnp.float32)
        expert_sel = jax.random.normal(k2, (E, d), dtype=jnp.float32) / np.sqrt(d).astype(np.float32)
        keys = jax.random.normal(k3, (E, d, H), dtype=jnp.float32) / np.sqrt(d).astype(np.float32)
        values = jax.random.normal(k4, (E, H, d), dtype=jnp.float32) / np.sqrt(E * H).astype(np.float32)
        return {'x': x, 'expert_sel': expert_sel, 'keys': keys, 'values': values}
    _L0_ffn_all = _L0_ffn_setup()
    _L0_ffn_in = {k: v for k, v in _L0_ffn_all.items() if k in ('expert_sel', 'keys', 'values')}
    del _L0_ffn_all
    return {'x': x, 'L0_tok_W1_w': _L0_tok_in['W1_w'], 'L0_tok_W1_b': _L0_tok_in['W1_b'], 'L0_tok_W1_sw': _L0_tok_in['W1_sw'], 'L0_tok_W1_sb': _L0_tok_in['W1_sb'], 'L0_tok_W2_w': _L0_tok_in['W2_w'], 'L0_tok_W2_b': _L0_tok_in['W2_b'], 'L0_tok_W2_sw': _L0_tok_in['W2_sw'], 'L0_tok_W2_sb': _L0_tok_in['W2_sb'], 'L0_tok_W3_w': _L0_tok_in['W3_w'], 'L0_tok_W3_b': _L0_tok_in['W3_b'], 'L0_tok_eps_in1': _L0_tok_in['eps_in1'], 'L0_tok_eps_out1': _L0_tok_in['eps_out1'], 'L0_tok_eps_in2': _L0_tok_in['eps_in2'], 'L0_tok_eps_out2': _L0_tok_in['eps_out2'], 'L0_attn_W_qkv': _L0_attn_in['W_qkv'], 'L0_attn_W_proj': _L0_attn_in['W_proj'], 'L0_attn_b_proj': _L0_attn_in['b_proj'], 'L0_ffn_expert_sel': _L0_ffn_in['expert_sel'], 'L0_ffn_keys': _L0_ffn_in['keys'], 'L0_ffn_values': _L0_ffn_in['values']}

def reference(x, L0_tok_W1_w, L0_tok_W1_b, L0_tok_W1_sw, L0_tok_W1_sb, L0_tok_W2_w, L0_tok_W2_b, L0_tok_W2_sw, L0_tok_W2_sb, L0_tok_W3_w, L0_tok_W3_b, L0_tok_eps_in1, L0_tok_eps_out1, L0_tok_eps_in2, L0_tok_eps_out2, L0_attn_W_qkv, L0_attn_W_proj, L0_attn_b_proj, L0_ffn_expert_sel, L0_ffn_keys, L0_ffn_values):
    import jax
    import jax.numpy as jnp

    def _L0_tok_ref(inputs, W1_w, W1_b, W1_sw, W1_sb, W2_w, W2_b, W2_sw, W2_sb, W3_w, W3_b, eps_in1, eps_out1, eps_in2, eps_out2):
        import math
        import jax, jax.numpy as jnp
        import numpy as np
        PW = PH = 16
        EMB = 128
        HID = 128
        B, H, W = (64, 128, 128)
        L = H // PW * (W // PH)
        SIGMA_ZERO = 0.1

        def _f_noise(x):
            return jnp.sign(x) * jnp.sqrt(jnp.abs(x))

        def _noisy_linear(x, w, b, sw, sb, eps_in, eps_out):
            ei = _f_noise(eps_in)
            eo = _f_noise(eps_out)
            w_n = w + sw * (eo[:, None] * ei[None, :])
            b_n = b + sb * eo
            return x @ w_n.T + b_n

        def _unfold_patches(x):
            b = x.shape[0]
            p = x.reshape(b, H // PW, PW, W // PH, PH)
            p = p.transpose(0, 1, 3, 2, 4)
            return p.reshape(b, L, PW * PH)

        def _pos_encoding(x):
            pos = jnp.arange(L, dtype=jnp.float32)[:, None]
            div = jnp.exp(jnp.arange(0, EMB, 2, dtype=jnp.float32) * (-math.log(10000.0) / EMB))
            ang = pos * div
            pe = jnp.stack([jnp.sin(ang), jnp.cos(ang)], axis=-1).reshape(L, EMB)
            return x + pe[None, :, :]
        x = _unfold_patches(inputs)
        g = _noisy_linear(x, W1_w, W1_b, W1_sw, W1_sb, eps_in1, eps_out1)
        x_gate = g * jnp.tanh(jax.nn.softplus(g))
        x_inner = _noisy_linear(x, W2_w, W2_b, W2_sw, W2_sb, eps_in2, eps_out2)
        x = x_gate * x_inner
        x = x @ W3_w.T + W3_b
        return _pos_encoding(x)

    def _L0_attn_ref(x, W_qkv, W_proj, b_proj):
        import jax, jax.numpy as jnp
        import numpy as np
        B, T, DIM = (4, 512, 128)
        H = 8
        HD = DIM // H
        ALPHA = 100.0
        EPS = 1e-10
        b, t, dim = x.shape
        qkv = x @ W_qkv
        qkv = qkv.reshape(b, t, HD, 2, H)
        qk = jnp.transpose(qkv[:, :, :, 0, :], (0, 3, 1, 2))
        v = jnp.transpose(qkv[:, :, :, 1, :], (0, 3, 1, 2))
        q = qk
        qsq = jnp.sum(q * q, axis=-1)
        dots = jnp.einsum('bhtd,bhsd->bhts', q, q)
        score = -(qsq[..., :, None] + qsq[..., None, :] - 2.0 * dots)
        a = jnp.sqrt(jnp.sum(q * q, axis=(2, 3), keepdims=True))
        x_norm = jnp.sqrt(jnp.sum(x * x, axis=-1))
        bmax = jnp.max(x_norm, axis=1).reshape(b, 1, 1, 1)
        scale = 1.0 / (a * bmax + EPS)
        attn = jax.nn.softmax(ALPHA * score * scale, axis=-1)
        out = jnp.einsum('bhts,bhsd->bhtd', attn, v)
        out = jnp.transpose(out, (0, 2, 1, 3)).reshape(b, t, dim)
        return out @ W_proj + b_proj

    def _L0_ffn_ref(x, expert_sel, keys, values):
        import jax, jax.numpy as jnp
        import numpy as np
        TOP_K = 2
        B, S, d = x.shape
        E = keys.shape[0]
        xt = x.reshape(-1, d)
        T = xt.shape[0]
        sel = jax.nn.sigmoid(xt @ expert_sel.T)
        sel_val, sel_idx = jax.lax.top_k(sel, TOP_K)
        w = jnp.zeros((T, E), dtype=xt.dtype).at[jnp.arange(T)[:, None], sel_idx].add(sel_val)
        h = jax.nn.relu(jnp.einsum('td,edh->teh', xt, keys))
        out = jnp.einsum('teh,te,ehv->tv', h, w, values)
        return out.reshape(B, S, -1)
    h = _L0_tok_ref(x, L0_tok_W1_w, L0_tok_W1_b, L0_tok_W1_sw, L0_tok_W1_sb, L0_tok_W2_w, L0_tok_W2_b, L0_tok_W2_sw, L0_tok_W2_sb, L0_tok_W3_w, L0_tok_W3_b, L0_tok_eps_in1, L0_tok_eps_out1, L0_tok_eps_in2, L0_tok_eps_out2)
    h = h + _L0_attn_ref(_layernorm(h, axis=-1), L0_attn_W_qkv, L0_attn_W_proj, L0_attn_b_proj)
    h = h + _L0_ffn_ref(_layernorm(h, axis=-1), L0_ffn_expert_sel, L0_ffn_keys, L0_ffn_values)
    return h

_drawn_inputs = setup_inputs


def setup_inputs(seed=0):
    import zlib

    import numpy as np

    out = dict(_drawn_inputs(seed))
    spreads = {'L0_tok_W1_sw': (0.0062500000931322575, 0.6),
     'L0_tok_W1_sb': (0.0062500000931322575, 0.6),
     'L0_tok_W2_sw': (0.0062500000931322575, 0.6),
     'L0_tok_W2_sb': (0.0062500000931322575, 0.6)}
    factors = {'L0_tok_W1_b': 3.285, 'L0_tok_W2_b': 3.159, 'L0_attn_b_proj': 3.294}
    for name, (base, spread) in spreads.items():
        noise = np.random.default_rng([zlib.crc32(name.encode()), seed]).standard_normal(out[name].shape)
        drawn = base * np.exp(spread * noise) if base else spread * noise
        out[name] = jnp.asarray(drawn.astype(out[name].dtype))
    for name, factor in factors.items():
        out[name] = (out[name] * factor).astype(out[name].dtype)
    return out
```

```python
from contextlib import ExitStack

import concourse.bass as bass
from concourse import mybir

F32 = mybir.dt.float32
BF16 = mybir.dt.bfloat16
I32 = mybir.dt.int32
U32 = mybir.dt.uint32
ALU = mybir.AluOpType
ACT = mybir.ActivationFunctionType
AX_X = mybir.AxisListType.X

P = 128


def vit_tower_kernel(nc, x_t, w_t, sw_t, w_cols, eo_rows, w3_t, bias_rows, w_qv, w_out, sel_t, keys, values,
                     pos, out):
    HALVES, _, T = x_t.shape
    SEQS, L, D = out.shape
    HID = w_t.shape[-1]
    HEADS, HD = 8, D // 8
    E = keys.shape[1]
    TILES = T // P
    GT = 4
    GROUPS = TILES // GT
    GTOK = GT * P
    GSEQ = GTOK // L
    BLOCKS = 2
    BT = TILES // BLOCKS
    BG = BT // GT
    SLOT_TILES = -(-(2 * BT + E - 1) // GT) * GT
    SCH = SLOT_TILES // GT
    HP = 32
    VW = HD + 1
    VROW = 3 * 2 * VW + 64
    assert L == 64 and D == 128 and HID == 128 and HALVES == 2
    EPS = 1e-5

    ROWS = SLOT_TILES * P
    xg_dram = [nc.dram_tensor(f"xg_rows{b}", [ROWS, D], F32, kind="Internal").ap() for b in range(BLOCKS)]
    y_dram = [nc.dram_tensor(f"y_rows{b}", [ROWS, D], F32, kind="Internal").ap() for b in range(BLOCKS)]

    with ExitStack() as ctx:
        def sb(name, shape, dt=F32):
            return ctx.enter_context(nc.sbuf_tensor(name, shape, dt))

        def sem(name):
            return ctx.enter_context(nc.semaphore(name))

        banks = [ctx.enter_context(nc.psum_tensor(f"bank{i}", [P, 512], F32)) for i in range(8)]

        keys_sb = sb("keys_sb", [P, E, HID])
        values_sb = sb("values_sb", [P, E, D])
        h = sb("h", [P, TILES, D])
        xn = sb("xn", [P, TILES, D])
        ident = sb("ident", [P, P])
        seq_ones = sb("seq_ones", [P, P])
        tri = sb("tri", [P, P], BF16)
        ones_bf = sb("ones_bf", [P, P], BF16)
        head_mask = sb("head_mask", [P, GT])
        iota_e = sb("iota_e", [P, E])
        thr = sb("thr", [P, BT])
        part_no = sb("part_no", [P, 1])
        scan_keep = sb("scan_keep", [P, E, BT])
        onesE = sb("onesE", [P, E])
        half = sb("half", [P, 256])
        mhalf = sb("mhalf", [P, TILES])
        zeros = sb("zeros", [P, GT * D])
        wn_t = sb("wn_t", [P, 2, 2, HID])
        swn_t = sb("swn_t", [P, 2, 2, HID])
        cols = sb("cols", [P, 10])
        f_abs = sb("f_abs", [P, 6])
        f_sgn = sb("f_sgn", [P, 6])
        r_eo = sb("r_eo", [P, 2, HID])
        r_abs = sb("r_abs", [P, 2, HID])
        sb_eo = sb("sb_eo", [P, 2])
        bn_col = sb("bn_col", [P, 2])
        w3T = sb("w3T", [P, D])
        base = sb("base", [P, D])
        bias_b = sb("bias_b", [P, 2, D])
        wqv = sb("wqv", [P, 2 * D])
        wp2 = sb("wp2", [P, 2, D])
        selT = sb("selT", [P, E])
        hot = sb("hot", [P, 2, E, TILES])
        topw = sb("topw", [P, TILES, 2])
        pos_u = sb("pos_u", [P, 2, TILES], U32)
        etab = sb("etab", [1, BLOCKS, P], I32)
        n2 = sb("n2", [P, TILES])
        bmax = sb("bmax", [P, TILES])
        seqmax = sb("seqmax", [TILES, 2])
        seqmax_b = sb("seqmax_b", [TILES, P])

        XS = 2 * T
        arena_a = sb("arena_a", [P, XS])
        xT = arena_a[:, :].rearrange("p (f t) -> p f t", f=2)
        RW = GSEQ * GT * L
        rdiag = arena_a[:, :].rearrange("p (u f s h t) -> p u f s h t", u=2, f=2, s=GSEQ, h=GT)
        assert XS == 2 * 2 * RW

        arena_b = sb("arena_b", [P, 10 * 1024 + 512])
        mish = arena_b[:, 0:2 * 6 * GTOK].rearrange("p (u k t) -> p u k t", u=2, k=6)
        o = 0
        xg = arena_b[:, o:o + 2 * GTOK].rearrange("p (u t d) -> p u t d", u=2, t=GT)
        o += 2 * GTOK
        xgT = arena_b[:, o:o + 2 * GTOK].rearrange("p (u t) -> p u t", u=2)
        o += 2 * GTOK
        keyc = arena_b[:, o:o + 2 * GTOK].rearrange("p (u t d) -> p u t d", u=2, t=GT)
        o += 2 * GTOK
        hexT = arena_b[:, o:o + 2 * GTOK].rearrange("p (u t) -> p u t", u=2)
        o += 2 * GTOK
        yb = arena_b[:, o:o + 2 * GTOK].rearrange("p (u t d) -> p u t d", u=2, t=GT)

        o = 0

        def part(n):
            nonlocal o
            o += n
            return arena_b[:, o - n:o]
        xnT = part(2 * GTOK).rearrange("p (u t) -> p u t", u=2)
        probs = part(2 * 512).rearrange("p (u t) -> p u t", u=2)
        vbd = part(2 * GT * 2 * VROW).rearrange("p (u t b v) -> p u t b v", u=2, t=GT, b=2)
        sq = part(GTOK)
        aT = part(2 * 2 * GTOK).rearrange("p (u f t) -> p u f t", u=2, f=2)
        o_sb = part(2 * GTOK).rearrange("p (u t b j d) -> p u t b j d", u=2, t=GT, b=2, j=4)
        x2T = part(2 * GTOK).rearrange("p (u t) -> p u t", u=2)
        oT = x2T
        a_tok = sb("a_tok", [P, 2, GT, HEADS, HP])
        b_tok = sb("b_tok", [P, 2, GT, HEADS, HP])
        v8 = sb("v8", [P, 2, GT * HEADS])
        c8 = sb("c8", [P, 2, 3, GT * HEADS])
        rden = sb("rden", [P, 2, 16])
        stats = sb("stats", [P, GT, 6])
        mv = sb("mv", [P, 2, GT, 2])
        veps = sb("veps", [P, 2, GT])
        rstd = sb("rstd", [P, 2, GT])
        all_mv = sb("all_mv", [P, TILES, 2])
        sel = sb("sel", [P, 3, GT, E])
        m8 = sb("m8", [P, GT, 8])
        i8 = sb("i8", [P, GT, 8], U32)
        idxf = sb("idxf", [P, GT, 2])
        rt = sb("rt", [P, 3, E, BT])
        mb = sb("mb", [P, E, BT], BF16)
        cnt = sb("cnt", [P, 4, E])
        posf = sb("posf", [P, 2, BT])
        ecol = sb("ecol", [P, 1])
        yg = arena_a[:, 0:8 * D].rearrange("p (r k d) -> p r k d", r=4, k=2)
        ob = arena_a[:, 8 * D:16 * D].rearrange("p (u t d) -> p u t d", u=2, t=GT)

        names = ("ld_small ld_w ld_rows ld_attn ld_exp ld_x0 ld_x1 ld_x2 ld_x3 ld_x4 ld_x5 ld_x6 ld_x7 zero_done "
                 "c_pool c_dve "
                 "s_prep s_ones s_bg s_abs s_powed s_wn "
                 "lin_ps m_gate m_inner m_min m_exp m_num m_den m_rec m_gi m_gin m_u w3_ps "
                 "h_done ln_stat ln_mv ln_eps ln_rstd ln_xn hb_done "
                 "n2_s n2_ps bm_s bm_ps bm_done "
                 "pX aXT pQ aAq aSq aV dV dAv pA2 gA dC dB pAT aAT pBT dR0 aR1 pS aP pO dRd dO "
                 "pOT aOT pY dH dSt dMv dEp gR dXn pX2 aX2 pL aE dS1 dSel dTop dIx dIf dHot "
                 "r_m r_tt r_dve r_r1 r_pos r_et r_etab "
                 "scat0 scat1 xg_l0 xg_l1 f_tp f_xT f_key f_m1 f_h f_m2 f_y y_st0 y_st1 "
                 "gat0 gat1 gat2 gat3 c_t c_o out_st0 out_st1").split()
        S = {n: sem(n) for n in names}

        block = ctx.enter_context(nc.Block())

        @block.sync
        def _(sp):
            def patches(n):
                ts = slice(GTOK * n, GTOK * n + GTOK)
                sp.dma_start(xT[:, :, ts], x_t[:, :, ts].rearrange("f p t -> p f t")).then_inc(S[f"ld_x{n}"], 16)
            sp.dma_start(cols[:, :], w_cols).then_inc(S["ld_small"], 16)
            sp.dma_start(r_eo[:, :, :], eo_rows.partition_broadcast(P)).then_inc(S["ld_small"], 16)
            sp.dma_start(wn_t[:, :, :, :], w_t.rearrange("a f p o -> p a f o")).then_inc(S["ld_w"], 16)
            sp.dma_start(swn_t[:, :, :, :], sw_t.rearrange("a f p o -> p a f o")).then_inc(S["ld_w"], 16)
            patches(0)
            sp.dma_start(w3T[:, :], w3_t).then_inc(S["ld_rows"], 16)
            sp.dma_start(base[:, :], pos).then_inc(S["ld_rows"], 16)
            sp.dma_start(bias_b[:, :, :], bias_rows.partition_broadcast(P)).then_inc(S["ld_rows"], 16)
            for n in range(1, GROUPS):
                patches(n)
            sp.dma_start(wqv[:, :], w_qv).then_inc(S["ld_attn"], 16)
            sp.dma_start(selT[:, :], sel_t).then_inc(S["ld_attn"], 16)
            for b in range(2):
                sp.dma_start(wp2[L * b:L * b + L, :, :], w_out).then_inc(S["ld_attn"], 16)
            sp.dma_start(keys_sb[:, :, :], keys).then_inc(S["ld_exp"], 16)
            sp.dma_start(values_sb[:, :, :], values).then_inc(S["ld_exp"], 16)
            sp.wait_ge(S["c_dve"], 1)
            for c in range(BLOCKS * SCH):
                r = c % SCH * GTOK
                sp.dma_start(xg_dram[c // SCH][r:r + GTOK, :].rearrange("(p t) d -> p (t d)", p=P), zeros[:, :]).then_inc(S["zero_done"], 16)

            def load_chunk(b, c):
                n = b * SCH + c
                if n == 0 or c == 0:
                    sp.wait_ge(S[f"scat{b}"], 2 * BT * 16)
                if n == 0:
                    sp.wait_ge(S["dXn"], TILES)
                if n >= 2:
                    sp.wait_ge(S["f_tp"], n - 1)
                sp.dma_start(xg[:, n % 2], xg_dram[b][c * GTOK:(c + 1) * GTOK, :].rearrange("(t p) d -> p t d", p=P))\
                  .then_inc(S[f"xg_l{n % 2}"], 16)

            def store_chunk(b, c):
                n = b * SCH + c
                sp.wait_ge(S["f_y"], n + 1)
                sp.dma_start(y_dram[b][c * GTOK:(c + 1) * GTOK, :].rearrange("(t p) d -> p t d", p=P), yb[:, n % 2])\
                  .then_inc(S[f"y_st{n % 2}"], 16)
            for b in range(BLOCKS):
                load_chunk(b, 0)
                load_chunk(b, 1)
                for c in range(SCH):
                    if c + 2 < SCH:
                        load_chunk(b, c + 2)
                    store_chunk(b, c)
            for g in range(GROUPS):
                sp.wait_ge(S["c_o"], GT * (g + 1))
                sp.dma_start(out[g * GSEQ:(g + 1) * GSEQ].rearrange("(t b) l d -> (b l) t d", b=2), ob[:, g % 2])\
                  .then_inc(S[f"out_st{g % 2}"], 16)
            sp.wait_ge(S["out_st0"], 16 * GROUPS // 2)
            sp.wait_ge(S["out_st1"], 16 * GROUPS // 2)
            sp.wait_ge(S["y_st0"], 16 * BLOCKS * SCH // 2)
            sp.wait_ge(S["y_st1"], 16 * BLOCKS * SCH // 2)

        @block.gpsimd
        def _(pool):
            pool.memset(ident[:, :], 0.0).then_inc(S["c_pool"], 1)
            pool.memset(ones_bf[:, :], 1.0).then_inc(S["c_pool"], 1)
            pool.memset(half[:, :], 0.5).then_inc(S["c_pool"], 1)
            pool.memset(mhalf[:, :], -0.5).then_inc(S["c_pool"], 1)
            pool.wait_ge(S["c_pool"], 4)
            pool.affine_select(out=ident[:, :], in_=ident[:, :], compare_op=ALU.not_equal, fill=1.0, base=0,
                               pattern=[[-1, P]], channel_multiplier=1).then_inc(S["c_pool"], 1)
            pool.affine_select(out=tri[:, :], in_=ones_bf[:, :], compare_op=ALU.is_gt, fill=0.0, base=0,
                               pattern=[[1, P]], channel_multiplier=-1).then_inc(S["c_pool"], 1)
            pool.iota(iota_e[:, :], pattern=[[1, E]], base=0, channel_multiplier=0,
                      allow_small_or_imprecise_dtypes=True).then_inc(S["c_pool"], 1)
            pool.iota(thr[:, :], pattern=[[P, BT]], base=0, channel_multiplier=0,
                      allow_small_or_imprecise_dtypes=True).then_inc(S["c_pool"], 1)
            pool.iota(part_no[:, :], pattern=[[0, 1]], base=0, channel_multiplier=1,
                      allow_small_or_imprecise_dtypes=True).then_inc(S["c_pool"], 1)
            pool.wait_ge(S["s_abs"], 2)
            rows = r_abs[:, :, :].rearrange("p a o -> p (a o)")
            pool.tensor_tensor(rows, rows, half[:, :], ALU.pow).then_inc(S["s_powed"], 1)
            pool.tensor_tensor(f_abs[:, :], f_abs[:, :], half[:, 0:6], ALU.pow).then_inc(S["s_powed"], 1)

            def gi_product(n):
                u = n % 2
                pool.wait_ge(S["m_gate"], n + 1)
                pool.wait_ge(S["m_inner"], n + 1)
                pool.tensor_tensor(mish[:, u, 1], mish[:, u, 0], mish[:, u, 1], ALU.mult).then_inc(S["m_gi"], 1)

            def gin_product(n):
                u = n % 2
                pool.wait_ge(S["m_num"], n + 1)
                pool.wait_ge(S["m_gi"], n + 1)
                pool.tensor_tensor(mish[:, u, 1], mish[:, u, 1], mish[:, u, 3], ALU.mult).then_inc(S["m_gin"], 1)

            def ln1_rstd(n):
                pool.wait_ge(S["ln_eps"], n + 1)
                pool.tensor_tensor(rstd[:, n % 2], veps[:, n % 2], mhalf[:, 0:GT], ALU.pow).then_inc(S["ln_rstd"], 1)

            def add_bproj(n):
                pool.wait_ge(S["ln_xn"], GT * (n + 1))
                for t in range(GT * n, GT * n + GT):
                    pool.tensor_tensor(h[:, t], h[:, t], bias_b[:, 1], ALU.add).then_inc(S["hb_done"], 1)
            for n in range(GROUPS):
                gi_product(n)
                gin_product(n)
                if n >= 1:
                    ln1_rstd(n - 1)
                    add_bproj(n - 1)
            ln1_rstd(GROUPS - 1)
            add_bproj(GROUPS - 1)
            pool.wait_ge(S["bm_ps"], 1)
            pool.wait_ge(S["bm_s"], 3)
            pool.tensor_tensor(bmax[:, :], bmax[:, :], half[:, 0:TILES], ALU.pow).then_inc(S["bm_done"], 1)

            def scatter(b, t, k):
                pool.indirect_dma_start(
                    xg_dram[b], bass.IndirectOffsetOnAxis(ap=pos_u[:, k, t:t + 1], axis=0),
                    xn[:, t, :], None).then_inc(S[f"scat{b}"], 16)

            def gather(t, k):
                pool.indirect_dma_start(
                    yg[:, t % 4, k, :], None,
                    y_dram[t // BT], bass.IndirectOffsetOnAxis(ap=pos_u[:, k, t:t + 1], axis=0))\
                    .then_inc(S[f"gat{t % 4}"], 16)

            pend = []

            def some(n):
                for _ in range(min(n, len(pend))):
                    scatter(*pend.pop(0))
            for g in range(GROUPS):
                if g == 0:
                    pool.wait_ge(S["dV"], 1)
                    pool.wait_ge(S["pA2"], 1)
                    pool.wait_ge(S["dC"], 1)
                    pool.tensor_tensor(c8[:, 0, 1], c8[:, 0, 0], half[:, 0:GT * HEADS], ALU.pow).then_inc(S["gA"], 1)
                if g + 1 < GROUPS:
                    pool.wait_ge(S["dC"], 4 * (g + 1) + 1)
                    pool.tensor_tensor(c8[:, (g + 1) % 2, 1], c8[:, (g + 1) % 2, 0], half[:, 0:GT * HEADS],
                                       ALU.pow).then_inc(S["gA"], 1)
                some(5)
                pool.wait_ge(S["dEp"], g + 1)
                pool.tensor_tensor(rstd[:, g % 2], veps[:, g % 2], mhalf[:, 0:GT], ALU.pow).then_inc(S["gR"], 1)
                if g == BG:
                    pool.wait_ge(S["r_pos"], 1)
                    pool.wait_ge(S["zero_done"], 16 * BLOCKS * SCH)
                    pend = [(0, t, k) for t in range(BT) for k in range(2)]
                some(5)
            some(len(pend))
            pool.wait_ge(S["r_pos"], 2)
            for t in range(BT, TILES):
                for k in range(2):
                    scatter(1, t, k)
            for t in range(TILES):
                if t % BT == 0:
                    n = (t // BT + 1) * SCH
                    pool.wait_ge(S["y_st0"], 16 * n // 2)
                    pool.wait_ge(S["y_st1"], 16 * n // 2)
                if t >= 4:
                    pool.wait_ge(S["c_o"], t - 3)
                gather(t, 0)
                gather(t, 1)

        @block.scalar
        def _(act):
            def gate_in(n):
                u = n % 2
                act.wait_ge(S["lin_ps"], 2 * n + 1)
                if n >= 2:
                    act.wait_ge(S["m_gi"], n - 1)
                    act.wait_ge(S["m_min"], n - 1)
                act.activation(mish[:, u, 0], banks[2 + 2 * u][:, :], ACT.Identity, bias=bn_col[:, 0:1])\
                   .then_inc(S["m_gate"], 1)
                act.wait_ge(S["lin_ps"], 2 * n + 2)
                if n >= 2:
                    act.wait_ge(S["m_u"], n - 1)
                act.activation(mish[:, u, 1], banks[3 + 2 * u][:, :], ACT.Identity, bias=bn_col[:, 1:2])\
                   .then_inc(S["m_inner"], 1)

            def gate_exp(n):
                u = n % 2
                act.wait_ge(S["m_min"], n + 1)
                act.activation(mish[:, u, 2], mish[:, u, 2], ACT.Exp).then_inc(S["m_exp"], 1)
            act.wait_ge(S["s_wn"], 6)
            for n in range(GROUPS):
                gate_in(n)
                gate_exp(n)

            def e_xT(g):
                act.wait_ge(S["pX"], g + 1)
                if g >= 2:
                    act.wait_ge(S["pQ"], GT * (g - 1))
                act.activation(xnT[:, g % 2], banks[0][:, :], ACT.Copy).then_inc(S["aXT"], 1)

            def e_qv(g):
                u = g % 2
                if g == 0:
                    act.wait_ge(S["s_prep"], 22)
                    act.wait_ge(S["s_bg"], 7)
                if g >= 1:
                    act.wait_ge(S["dV"], g)
                for q in range(2):
                    act.wait_ge(S["pQ"], GT * g + 2 * q + 2)
                    src = banks[1 + q][:, :].rearrange("p (t a h d) -> p t a h d", t=2, a=2, h=HEADS)
                    act.activation(sq[:, 256 * q:256 * q + 256].rearrange("p (t x) -> p t x", t=2),
                                   src[:, :, 0].rearrange("p t h d -> p t (h d)"), ACT.Square).then_inc(S["aSq"], 1)
                    if g >= 2:
                        act.wait_ge(S["pAT"], 2 * (g - 1))
                    for t in range(2):
                        act.activation(a_tok[:, u, 2 * q + t, :, 0:HD], src[:, t, 0], ACT.Copy).then_inc(S["aAq"], 1)
                    if g >= 2:
                        act.wait_ge(S["pO"], GT * (g - 1))
                    for t in range(2):
                        for b in range(2):
                            r = slice(L * b, L * b + L)
                            act.activation(
                                vbd[r, u, 2 * q + t, b, 0:HEADS * VW].rearrange("p (h v) -> p h v", v=VW)[:, :, 0:HD],
                                src[r, t, 1], ACT.Copy).then_inc(S["aV"], 1)

            def e_exp(g, t):
                n = GT * g + t
                act.wait_ge(S["pS"], n + 1)
                if n >= 2:
                    act.wait_ge(S["pO"], n - 1)
                act.activation(probs[:, n % 2], banks[3 + n % 2][:, :], ACT.Exp).then_inc(S["aP"], 1)

            def e_aT(g):
                for f in range(2):
                    act.wait_ge(S["pAT"], 2 * g + f + 1)
                    if g >= 2:
                        act.wait_ge(S["pS"], GT * (g - 1))
                    act.activation(aT[:, g % 2, f], banks[1 + f][:, :], ACT.Copy).then_inc(S["aAT"], 1)

            def e_r1(g):
                act.wait_ge(S["pBT"], 2 * g + 2)
                if g >= 2:
                    act.wait_ge(S["pS"], GT * (g - 1))
                for k in range(GT):
                    r = slice(HP * k, HP * k + HP)
                    act.activation(rdiag[r, g % 2, 1, :, k, :],
                                   banks[1][r, :].rearrange("p (s t) -> p s t", s=GSEQ), ACT.Copy)\
                       .then_inc(S["aR1"], 1)

            def e_oT(g):
                act.wait_ge(S["pOT"], g + 1)
                act.activation(oT[:, 0], banks[7][:, :], ACT.Copy).then_inc(S["aOT"], 1)

            def e_x2(g):
                act.wait_ge(S["pX2"], g + 1)
                act.activation(x2T[:, 1], banks[7][:, :], ACT.Copy).then_inc(S["aX2"], 1)

            def e_sel(g):
                act.wait_ge(S["pL"], g + 1)
                if g >= 1:
                    act.wait_ge(S["dS1"], g)
                act.activation(sel[:, 0].rearrange("p t e -> p (t e)"), banks[7][:, 0:GT * E], ACT.Exp, scale=-1.0)\
                   .then_inc(S["aE"], 1)
            e_xT(0)
            e_qv(0)
            e_aT(0)
            e_r1(0)
            for g in range(GROUPS):
                if g + 1 < GROUPS:
                    e_xT(g + 1)
                e_exp(g, 0)
                e_exp(g, 1)
                if g >= 1:
                    e_x2(g - 1)
                if g + 1 < GROUPS:
                    e_qv(g + 1)
                e_exp(g, 2)
                if g >= 1:
                    e_sel(g - 1)
                e_exp(g, 3)
                if g + 1 < GROUPS:
                    e_aT(g + 1)
                e_oT(g)
                if g + 1 < GROUPS:
                    e_r1(g + 1)
            e_x2(GROUPS - 1)
            e_sel(GROUPS - 1)

            def f_xT(n):
                act.wait_ge(S["f_tp"], n + 1)
                if n >= 2:
                    act.wait_ge(S["f_m1"], n - 1)
                act.activation(xgT[:, n % 2], banks[n % 2][:, :], ACT.Copy).then_inc(S["f_xT"], 1)

            def f_h(n):
                act.wait_ge(S["f_m1"], n + 1)
                if n >= 2:
                    act.wait_ge(S["f_m2"], n - 1)
                act.activation(hexT[:, n % 2], banks[2 + n % 2][:, :], ACT.Relu).then_inc(S["f_h"], 1)
            for b in range(BLOCKS):
                f_xT(b * SCH)
                for c in range(SCH):
                    if c + 1 < SCH:
                        f_xT(b * SCH + c + 1)
                    f_h(b * SCH + c)

        @block.vector
        def _(dve):
            dve.memset(zeros[:, :], 0.0).then_inc(S["c_dve"], 1)
            dve.memset(head_mask[:, :], 0.0).then_inc(S["s_prep"], 1)
            dve.memset(scan_keep[:, :, :], 1.0).then_inc(S["s_prep"], 1)
            dve.memset(onesE[:, :], 1.0).then_inc(S["s_prep"], 1)
            dve.memset(seq_ones[:, :], 0.0).then_inc(S["s_ones"], 1)
            dve.wait_ge(S["s_prep"], 3)
            dve.wait_ge(S["s_ones"], 1)
            for b in range(2):
                dve.memset(seq_ones[L * b:L * (b + 1), L * b:L * (b + 1)], 1.0).then_inc(S["s_ones"], 1)
            dve.memset(scan_keep[:, :, 0:1], 0.0).then_inc(S["s_prep"], 1)
            for k in range(GT):
                dve.memset(head_mask[HP * k:HP * k + HP, k:k + 1], 1.0).then_inc(S["s_prep"], 1)
            dve.wait_ge(S["ld_small"], 32)
            dve.scalar_tensor_tensor(out=r_abs[:, :, :], in0=r_eo[:, :, :], scalar=-1.0, in1=r_eo[:, :, :],
                                     op0=ALU.mult, op1=ALU.max).then_inc(S["s_abs"], 1)
            dve.scalar_tensor_tensor(out=f_abs[:, :], in0=cols[:, 4:10], scalar=-1.0, in1=cols[:, 4:10],
                                     op0=ALU.mult, op1=ALU.max).then_inc(S["s_abs"], 1)
            dve.tensor_scalar(r_eo[:, :, :], r_eo[:, :, :], 0.0, None, ALU.is_lt).then_inc(S["s_prep"], 1)
            dve.tensor_scalar(f_sgn[:, :], cols[:, 4:10], 0.0, None, ALU.is_lt).then_inc(S["s_prep"], 1)
            dve.wait_ge(S["s_prep"], 10)
            dve.tensor_scalar(r_eo[:, :, :], r_eo[:, :, :], -2.0, 1.0, ALU.mult, ALU.add).then_inc(S["s_prep"], 1)
            dve.tensor_scalar(f_sgn[:, :], f_sgn[:, :], -2.0, 1.0, ALU.mult, ALU.add).then_inc(S["s_prep"], 1)
            dve.wait_ge(S["s_prep"], 12)
            dve.wait_ge(S["s_powed"], 2)
            dve.tensor_tensor(r_abs[:, :, :], r_abs[:, :, :], r_eo[:, :, :], ALU.mult).then_inc(S["s_prep"], 1)
            dve.tensor_tensor(f_abs[:, :], f_abs[:, :], f_sgn[:, :], ALU.mult).then_inc(S["s_prep"], 1)
            dve.wait_ge(S["s_prep"], 14)
            dve.wait_ge(S["ld_w"], 32)
            for a in range(2):
                for f in range(2):
                    dve.scalar_tensor_tensor(out=swn_t[:, a, f], in0=r_abs[:, a],
                                             scalar=f_abs[:, 2 + 2 * a + f:3 + 2 * a + f],
                                             in1=swn_t[:, a, f], op0=ALU.mult, op1=ALU.mult).then_inc(S["s_prep"], 1)
            dve.tensor_tensor(sb_eo[:, :], cols[:, 2:4], f_abs[:, 0:2], ALU.mult).then_inc(S["s_prep"], 1)
            dve.wait_ge(S["s_prep"], 19)
            for a in range(2):
                for f in range(2):
                    dve.tensor_tensor(wn_t[:, a, f], swn_t[:, a, f], wn_t[:, a, f], ALU.add).then_inc(S["s_wn"], 1)
            dve.tensor_tensor(bn_col[:, :], sb_eo[:, :], cols[:, 0:2], ALU.add).then_inc(S["s_wn"], 1)
            dve.wait_ge(S["ld_rows"], 16 * 3)
            dve.tensor_tensor(base[:, :], base[:, :], bias_b[:, 0], ALU.add).then_inc(S["s_wn"], 1)
            for t in (a_tok, b_tok):
                dve.memset(t[:, :, :, :, :].rearrange("p u t h x -> p (u t h x)"), 0.0).then_inc(S["s_prep"], 1)
            dve.wait_ge(S["s_prep"], 21)
            dve.memset(a_tok[:, :, :, :, HD + 1:HD + 2].rearrange("p u t h x -> p (u t h) x"), 1.0)\
               .then_inc(S["s_prep"], 1)

            def gate_min(n):
                u = n % 2
                dve.wait_ge(S["m_gate"], n + 1)
                if n >= 2:
                    dve.wait_ge(S["m_num"], n - 1)
                dve.tensor_scalar(mish[:, u, 2], mish[:, u, 0], 20.0, None, ALU.min).then_inc(S["m_min"], 1)

            def gate_tanh(n):
                u = n % 2
                dve.wait_ge(S["m_exp"], n + 1)
                if n >= 2:
                    dve.wait_ge(S["m_gin"], n - 1)
                dve.scalar_tensor_tensor(out=mish[:, u, 3], in0=mish[:, u, 2], scalar=2.0, in1=mish[:, u, 2],
                                         op0=ALU.add, op1=ALU.mult).then_inc(S["m_num"], 1)
                dve.wait_ge(S["m_num"], n + 1)
                dve.tensor_scalar(mish[:, u, 4], mish[:, u, 3], 2.0, None, ALU.add).then_inc(S["m_den"], 1)
                dve.wait_ge(S["m_den"], n + 1)
                dve.reciprocal(mish[:, u, 4], mish[:, u, 4]).then_inc(S["m_rec"], 1)

            def gate_out(n):
                u = n % 2
                dve.wait_ge(S["m_rec"], n + 1)
                dve.wait_ge(S["m_gin"], n + 1)
                if n >= 2:
                    dve.wait_ge(S["w3_ps"], n - 1)
                dve.tensor_tensor(mish[:, u, 5], mish[:, u, 1], mish[:, u, 4], ALU.mult).then_inc(S["m_u"], 1)

            def ln1(n):
                u = n % 2
                ts = slice(GT * n, GT * n + GT)
                dve.wait_ge(S["w3_ps"], n + 1)
                dve.tensor_tensor(h[:, ts], banks[6 + u][:, :].rearrange("p (t d) -> p t d", t=GT),
                                  base[:, :].unsqueeze(1).to_broadcast([P, GT, D]), ALU.add).then_inc(S["h_done"], 1)
                dve.wait_ge(S["h_done"], n + 1)
                for t in range(GT):
                    dve.bn_stats(stats[:, t, :], h[:, GT * n + t, :]).then_inc(S["ln_stat"], 1)
                dve.wait_ge(S["ln_stat"], GT * (n + 1))
                for t in range(GT):
                    dve.bn_aggr(all_mv[:, GT * n + t, :], stats[:, t, :]).then_inc(S["ln_mv"], 1)
                dve.wait_ge(S["ln_mv"], GT * (n + 1))
                if n >= 2:
                    dve.wait_ge(S["ln_rstd"], n - 1)
                dve.tensor_scalar(veps[:, u], all_mv[:, ts, 1:2].rearrange("p t a -> p (t a)"), EPS, None, ALU.add)\
                   .then_inc(S["ln_eps"], 1)

            def ln1_apply(n):
                dve.wait_ge(S["ln_rstd"], n + 1)
                for t in range(GT):
                    dve.tensor_scalar(xn[:, GT * n + t], h[:, GT * n + t], all_mv[:, GT * n + t, 0:1],
                                      rstd[:, n % 2, t:t + 1], ALU.subtract, ALU.mult).then_inc(S["ln_xn"], 1)
                dve.wait_ge(S["ln_mv"], GT * (n + 1))
                ts = slice(GT * n, GT * n + GT)
                dve.tensor_tensor(n2[:, ts], all_mv[:, ts, 1:2].rearrange("p t a -> p (t a)"), rstd[:, n % 2],
                                  ALU.mult).then_inc(S["n2_s"], 1)
                dve.wait_ge(S["n2_s"], 2 * n + 1)
                dve.scalar_tensor_tensor(out=n2[:, ts], in0=n2[:, ts], scalar=float(D), in1=rstd[:, n % 2],
                                         op0=ALU.mult, op1=ALU.mult).then_inc(S["n2_s"], 1)
            gate_min(0)
            gate_tanh(0)
            for n in range(GROUPS):
                gate_out(n)
                if n + 1 < GROUPS:
                    gate_min(n + 1)
                    gate_tanh(n + 1)
                ln1(n)
                if n >= 1:
                    ln1_apply(n - 1)
            ln1_apply(GROUPS - 1)
            dve.wait_ge(S["n2_ps"], 1)
            dve.tensor_reduce(seqmax[:, :], banks[7][0:TILES, 0:P].rearrange("p (b l) -> p b l", b=2), AX_X, ALU.max)\
               .then_inc(S["bm_s"], 1)
            dve.wait_ge(S["bm_s"], 1)
            dve.tensor_copy(seqmax_b[:, :].rearrange("p (b l) -> p b l", b=2),
                            seqmax[:, :].unsqueeze(2).to_broadcast([TILES, 2, L])).then_inc(S["bm_s"], 1)
            dve.wait_ge(S["bm_ps"], 1)
            dve.tensor_copy(bmax[:, :], banks[7][:, 0:TILES]).then_inc(S["bm_s"], 1)
            dve.wait_ge(S["lin_ps"], 2 * GROUPS)
            dve.memset(vbd.rearrange("p u t b v -> p (u t b v)"), 0.0).then_inc(S["s_bg"], 1)
            for u in range(2):
                dve.memset(rdiag[:, u, 1].rearrange("p s h t -> p (s h t)"), 0.0).then_inc(S["s_bg"], 1)
            dve.wait_ge(S["s_bg"], 1)
            for u in range(2):
                for b in range(2):
                    r = slice(L * b, L * b + L)
                    dve.memset(vbd[r, u, :, b, 0:HEADS * VW].rearrange("p t (h v) -> p t h v", v=VW)[:, :, :, HD:VW], 1.0)\
                       .then_inc(S["s_bg"], 1)

            def d_v(g):
                u = g % 2
                dve.wait_ge(S["aSq"], 2 * g + 2)
                if g >= 2:
                    dve.wait_ge(S["pA2"], g - 1)
                dve.tensor_reduce(v8[:, u], sq[:, :].rearrange("p (x d) -> p x d", d=HD), AX_X, ALU.add)\
                   .then_inc(S["dV"], 1)
                dve.wait_ge(S["dV"], g + 1)
                if g >= 2:
                    dve.wait_ge(S["pAT"], 2 * (g - 1))
                dve.tensor_copy(a_tok[:, u, :, :, HD:HD + 1].rearrange("p t h x -> p (t h) x"),
                                v8[:, u].unsqueeze(2)).then_inc(S["dAv"], 1)

            def d_c1(g):
                u = g % 2
                dve.wait_ge(S["pA2"], g + 1)
                dve.tensor_copy(c8[:, u, 0], banks[0][:, 0:GT * HEADS]).then_inc(S["dC"], 1)

            def d_c2(g):
                u = g % 2
                dve.wait_ge(S["gA"], g + 1)
                dve.wait_ge(S["bm_done"], 1)
                dve.tensor_tensor(c8[:, u, 0].rearrange("p (t h) -> p t h", t=GT),
                                  c8[:, u, 1].rearrange("p (t h) -> p t h", t=GT),
                                  bmax[:, GT * g:GT * g + GT].unsqueeze(2).to_broadcast([P, GT, HEADS]),
                                  ALU.mult).then_inc(S["dC"], 1)
                dve.wait_ge(S["dC"], 4 * g + 2)
                dve.tensor_scalar(c8[:, u, 0], c8[:, u, 0], 1e-10, 0.005, ALU.add, ALU.mult).then_inc(S["dC"], 1)
                dve.wait_ge(S["dC"], 4 * g + 3)
                dve.reciprocal(c8[:, u, 2], c8[:, u, 0]).then_inc(S["dC"], 1)
                dve.wait_ge(S["dC"], 4 * g + 4)
                dve.wait_ge(S["aAq"], GT * (g + 1))
                if g >= 2:
                    dve.wait_ge(S["pBT"], 2 * (g - 1))
                dve.tensor_tensor(b_tok[:, u, :, :, 0:HD].rearrange("p t h d -> p (t h) d"),
                                  a_tok[:, u, :, :, 0:HD].rearrange("p t h d -> p (t h) d"),
                                  c8[:, u, 2].unsqueeze(2).to_broadcast([P, GT * HEADS, HD]), ALU.mult)\
                   .then_inc(S["dB"], 1)
                dve.tensor_scalar(b_tok[:, u, :, :, HD:HD + 1].rearrange("p t h x -> p (t h) x"),
                                  c8[:, u, 2].unsqueeze(2), -0.5, None, ALU.mult).then_inc(S["dB"], 1)
                dve.scalar_tensor_tensor(out=b_tok[:, u, :, :, HD + 1:HD + 2].rearrange("p t h x -> p (t h) x"),
                                         in0=c8[:, u, 2].unsqueeze(2), scalar=-0.5, in1=v8[:, u].unsqueeze(2),
                                         op0=ALU.mult, op1=ALU.mult).then_inc(S["dB"], 1)

            def d_r0(g):
                dve.wait_ge(S["pBT"], 2 * g + 1)
                if g >= 2:
                    dve.wait_ge(S["pS"], GT * (g - 1))
                dve.tensor_tensor(
                    rdiag[:, g % 2, 0],
                    banks[0][:, :].rearrange("p (s t) -> p s t", s=GSEQ).unsqueeze(2)
                    .to_broadcast([P, GSEQ, GT, L]),
                    head_mask[:, :].unsqueeze(1).unsqueeze(3).to_broadcast([P, GSEQ, GT, L]), ALU.mult)\
                   .then_inc(S["dR0"], 1)

            def d_o(g, t):
                n = GT * g + t
                dve.wait_ge(S["pO"], n + 1)
                src = banks[5 + n % 2][:, :].rearrange("p (x c) -> p x c", c=64)
                for k in range(2):
                    r = slice(L * k, L * k + L)
                    dve.reciprocal(rden[r, n % 2, 0:8], src[r, :, VW * k + HD]).then_inc(S["dRd"], 1)
                dve.wait_ge(S["dRd"], 2 * (n + 1))
                if g >= 2:
                    dve.wait_ge(S["pOT"], g - 1)
                for k in range(2):
                    r = slice(L * k, L * k + L)
                    dve.tensor_tensor(o_sb[r, g % 2, t].rearrange("p b j d -> p j b d"),
                                      src[r, :, VW * k:VW * k + HD].rearrange("p (j b) d -> p j b d", b=2),
                                      rden[r, n % 2, 0:8].rearrange("p (j b) -> p j b", b=2).unsqueeze(3)
                                      .to_broadcast([L, 4, 2, HD]), ALU.mult).then_inc(S["dO"], 1)

            def d_ln2(g):
                u = g % 2
                ts = slice(GT * g, GT * g + GT)
                dve.wait_ge(S["pY"], g + 1)
                dve.wait_ge(S["hb_done"], GT * (g + 1))
                dve.tensor_tensor(h[:, ts], banks[7][:, :].rearrange("p (t d) -> p t d", t=GT), h[:, ts], ALU.add)\
                   .then_inc(S["dH"], 1)
                dve.wait_ge(S["dH"], g + 1)
                for t in range(GT):
                    dve.bn_stats(stats[:, t, :], h[:, GT * g + t, :]).then_inc(S["dSt"], 1)
                dve.wait_ge(S["dSt"], GT * (g + 1))
                for t in range(GT):
                    dve.bn_aggr(mv[:, u, t, :], stats[:, t, :]).then_inc(S["dMv"], 1)
                dve.wait_ge(S["dMv"], GT * (g + 1))
                dve.tensor_scalar(veps[:, u], mv[:, u, :, 1:2].rearrange("p t a -> p (t a)"), EPS, None, ALU.add)\
                   .then_inc(S["dEp"], 1)

            def d_ln2_apply(g):
                dve.wait_ge(S["gR"], g + 1)
                for t in range(GT):
                    dve.tensor_scalar(xn[:, GT * g + t], h[:, GT * g + t], mv[:, g % 2, t, 0:1],
                                      rstd[:, g % 2, t:t + 1], ALU.subtract, ALU.mult).then_inc(S["dXn"], 1)

            def d_top(g):
                dve.wait_ge(S["aE"], g + 1)
                dve.tensor_scalar(sel[:, 1], sel[:, 0], 1.0, None, ALU.add).then_inc(S["dS1"], 1)
                dve.wait_ge(S["dS1"], g + 1)
                dve.reciprocal(sel[:, 2], sel[:, 1]).then_inc(S["dSel"], 1)
                dve.wait_ge(S["dSel"], g + 1)
                for t in range(GT):
                    dve.max(m8[:, t], sel[:, 2, t]).then_inc(S["dTop"], 1)
                dve.wait_ge(S["dTop"], GT * (g + 1))
                for t in range(GT):
                    dve.max_index(i8[:, t], m8[:, t], sel[:, 2, t]).then_inc(S["dIx"], 1)
                ts = slice(GT * g, GT * g + GT)
                dve.tensor_copy(topw[:, ts], m8[:, :, 0:2]).then_inc(S["dHot"], 1)
                dve.wait_ge(S["dIx"], GT * (g + 1))
                dve.tensor_copy(idxf[:, :, :], i8[:, :, 0:2]).then_inc(S["dIf"], 1)
                dve.wait_ge(S["dIf"], g + 1)
                for k in range(2):
                    dve.tensor_tensor(hot[:, k, :, ts], iota_e[:, :].unsqueeze(2).to_broadcast([P, E, GT]),
                                      idxf[:, :, k].unsqueeze(1).to_broadcast([P, E, GT]), ALU.is_equal)\
                       .then_inc(S["dHot"], 1)

            rd = [0]

            def step(ins):
                rd[0] += 1
                ins.then_inc(S["r_dve"], 1)
                dve.wait_ge(S["r_dve"], rd[0])

            def d_route_mask(b):
                bs = slice(BT * b, BT * b + BT)
                dve.wait_ge(S["dHot"], 3 * BG * (b + 1))
                dve.tensor_tensor(mb[:, :, :], hot[:, 0, :, bs], hot[:, 1, :, bs], ALU.add).then_inc(S["r_m"], 1)

            def d_route(b):
                dve.wait_ge(S["r_tt"], b + 1)
                tt = banks[7][:, :].rearrange("p (e t) -> p e t", e=E)
                flat = "p e t -> p (e t)"
                step(dve.tensor_tensor_scan(rt[:, 0].rearrange(flat), scan_keep[:, :, :].rearrange(flat),
                                            banks[7][:, :], 0.0, ALU.mult, ALU.add))
                step(dve.tensor_tensor(rt[:, 1], rt[:, 0], tt, ALU.subtract))
                step(dve.tensor_tensor(rt[:, 2], rt[:, 0, :, BT - 1:BT].to_broadcast([P, E, BT]),
                                       thr[:, :].unsqueeze(1).to_broadcast([P, E, BT]), ALU.is_gt))
                step(dve.tensor_reduce(cnt[:, 0], rt[:, 2], AX_X, ALU.add))
                if 2 * BT > BT:
                    pass
                step(dve.tensor_tensor_scan(cnt[:, 1], onesE[:, :], cnt[:, 0], 0.0, ALU.mult, ALU.add))
                step(dve.tensor_tensor(cnt[:, 2], cnt[:, 1], cnt[:, 0], ALU.subtract))
                step(dve.scalar_tensor_tensor(out=rt[:, 1], in0=cnt[:, 2].unsqueeze(2).to_broadcast([P, E, BT]),
                                              scalar=float(P), in1=rt[:, 1], op0=ALU.mult, op1=ALU.add))
                step(dve.tensor_scalar(cnt[:, 3], cnt[:, 1], part_no[:, 0:1], None, ALU.is_le))
                dve.tensor_reduce(ecol[:, :], cnt[:, 3], AX_X, ALU.add).then_inc(S["r_et"], 1)

            def d_route_pos(b):
                dve.wait_ge(S["r_r1"], 2 * b + 1)
                step(dve.tensor_tensor(rt[:, 0], banks[7][:, :].rearrange("p (e t) -> p e t", e=E), rt[:, 1], ALU.add))
                bs = slice(BT * b, BT * b + BT)
                for k in range(2):
                    step(dve.tensor_tensor(rt[:, 2], rt[:, 0], hot[:, k, :, bs], ALU.mult))
                    step(dve.tensor_reduce(posf[:, k], rt[:, 2].rearrange("p e t -> p t e"), AX_X, ALU.add))
                dve.tensor_copy(pos_u[:, :, bs], posf[:, :, :])\
                   .then_inc(S["r_pos"], 1)
                dve.wait_ge(S["r_r1"], 2 * b + 2)
                dve.tensor_scalar(etab[0:1, b, :], banks[7][0:1, 0:P], float(E - 1), None, ALU.min)\
                   .then_inc(S["r_etab"], 1)
            d_v(0)
            d_c1(0)
            d_c2(0)
            d_r0(0)
            for g in range(GROUPS):
                if g == BG + 1:
                    d_route_pos(0)
                if g + 1 < GROUPS:
                    d_v(g + 1)
                d_o(g, 0)
                if g >= 1:
                    d_top(g - 1)
                if g == BG:
                    d_route_mask(0)
                d_o(g, 1)
                if g + 1 < GROUPS:
                    d_c1(g + 1)
                    d_c2(g + 1)
                d_o(g, 2)
                d_o(g, 3)
                if g + 1 < GROUPS:
                    d_r0(g + 1)
                d_ln2(g)
                d_ln2_apply(g)
                if g == BG:
                    d_route(0)
            d_top(GROUPS - 1)
            d_route_mask(1)
            d_route(1)
            d_route_pos(1)

            def key_copy(n, reg):
                b, c = divmod(n, SCH)
                if n >= 2:
                    dve.wait_ge(S["f_m1"], n - 1)
                for t in range(GT):
                    e = dve.value_load(etab[0:1, b, c * GT + t:c * GT + t + 1], min_val=0, max_val=E - 1)
                    dve.tensor_copy(keyc[:, n % 2, t:t + 1, :], keys_sb[:, bass.ds(e, 1), :]).then_inc(S["f_key"], 1)

            def f_y(n):
                dve.wait_ge(S["f_m2"], n + 1)
                if n >= 2:
                    dve.wait_ge(S[f"y_st{n % 2}"], 16 * (n // 2))
                dve.tensor_copy(yb[:, n % 2].rearrange("p t d -> p (t d)"), banks[4 + n % 2][:, :])\
                   .then_inc(S["f_y"], 1)
            dve.wait_ge(S["ld_exp"], 32)
            for b in range(BLOCKS):
                dve.wait_ge(S["r_etab"], b + 1)
                key_copy(b * SCH, None)
                for c in range(SCH):
                    if c + 1 < SCH:
                        key_copy(b * SCH + c + 1, None)
                    f_y(b * SCH + c)

            for t in range(TILES):
                g = t // GT
                dve.wait_ge(S[f"gat{t % 4}"], 32 * (t // 4 + 1))
                if t % GT == 0 and g >= 2:
                    dve.wait_ge(S[f"out_st{g % 2}"], 16 * (g // 2))
                dve.scalar_tensor_tensor(out=h[:, t], in0=yg[:, t % 4, 0], scalar=topw[:, t, 0:1], in1=h[:, t],
                                         op0=ALU.mult, op1=ALU.add).then_inc(S["c_t"], 1)
                dve.wait_ge(S["c_t"], t + 1)
                dve.scalar_tensor_tensor(out=ob[:, g % 2, t % GT], in0=yg[:, t % 4, 1], scalar=topw[:, t, 1:2],
                                         in1=h[:, t], op0=ALU.mult, op1=ALU.add).then_inc(S["c_o"], 1)

        @block.tensor
        def _(pe):
            def linear(n):
                u = n % 2
                pe.wait_ge(S[f"ld_x{n}"], 16)
                for a in range(2):
                    if n >= 2:
                        pe.wait_ge(S["m_gate" if a == 0 else "m_inner"], n - 1)
                    for f in range(2):
                        mm = pe.matmul(banks[2 + 2 * u + a][:, :], wn_t[:, a, f, :],
                                       xT[:, f, GTOK * n:GTOK * n + GTOK], start=(f == 0), stop=(f == 1))
                    mm.then_inc(S["lin_ps"], 1)

            def embed(n):
                u = n % 2
                pe.wait_ge(S["m_u"], n + 1)
                if n >= 2:
                    pe.wait_ge(S["h_done"], n - 1)
                for t in range(GT):
                    mm = pe.matmul(banks[6 + u][:, D * t:D * t + D], mish[:, u, 5, P * t:P * t + P], w3T[:, :],
                                   start=True, stop=True)
                mm.then_inc(S["w3_ps"], 1)
            pe.wait_ge(S["c_pool"], 9)
            pe.wait_ge(S["s_wn"], 6)
            for n in range(GROUPS):
                linear(n)
                if n >= 1:
                    embed(n - 1)
            embed(GROUPS - 1)
            pe.wait_ge(S["n2_s"], 2 * GROUPS)
            pe.wait_ge(S["h_done"], GROUPS)
            pe.transpose(banks[7][0:TILES, 0:P], n2[:, :], ident[:, :]).then_inc(S["n2_ps"], 1)
            pe.wait_ge(S["bm_s"], 2)
            pe.transpose(banks[7][:, 0:TILES], seqmax_b[:, :], ident[0:TILES, 0:TILES]).then_inc(S["bm_ps"], 1)

            def t_x(g):
                pe.wait_ge(S["ln_xn"], GT * (g + 1))
                if g >= 1:
                    pe.wait_ge(S["dR0"], g)
                for t in range(GT):
                    mm = pe.transpose(banks[0][:, P * t:P * t + P], xn[:, GT * g + t], ident[:, :])
                mm.then_inc(S["pX"], 1)

            def t_qv(g):
                pe.wait_ge(S["aXT"], g + 1)
                pe.wait_ge(S["ld_attn"], 16 * 4)
                if g >= 1:
                    pe.wait_ge(S["aR1"], GT * g)
                    pe.wait_ge(S["aAT"], 2 * g)
                for t in range(GT):
                    pe.matmul(banks[1 + t // 2][:, 256 * (t % 2):256 * (t % 2) + 256], xnT[:, g % 2, P * t:P * t + P],
                              wqv[:, :], start=True, stop=True)\
                      .then_inc(S["pQ"], 1)

            def t_a2(g):
                pe.wait_ge(S["dV"], g + 1)
                pe.wait_ge(S["aXT"], g + 1)
                pe.matmul(banks[0][:, 0:GT * HEADS], seq_ones[:, :], v8[:, g % 2], start=True, stop=True)\
                  .then_inc(S["pA2"], 1)

            def t_at(g):
                pe.wait_ge(S["dAv"], g + 1)
                pe.wait_ge(S["aAq"], GT * (g + 1))
                pe.wait_ge(S["aV"], 2 * GT * (g + 1))
                for f in range(2):
                    for t in range(GT):
                        mm = pe.transpose(banks[1 + f][:, P * t:P * t + P],
                                          a_tok[:, g % 2, t, 4 * f:4 * f + 4, :].rearrange("p h x -> p (h x)"),
                                          ident[:, :])
                    mm.then_inc(S["pAT"], 1)

            def t_bt(g):
                pe.wait_ge(S["dB"], 3 * (g + 1))
                for f in range(2):
                    pe.wait_ge(S["aAT"], 2 * g + 1)
                    for t in range(GT):
                        mm = pe.transpose(banks[f][:, P * t:P * t + P],
                                          b_tok[:, g % 2, t, 4 * f:4 * f + 4, :].rearrange("p h x -> p (h x)"),
                                          ident[:, :])
                    mm.then_inc(S["pBT"], 1)

            def t_s(g, t):
                n = GT * g + t
                if t == 0:
                    pe.wait_ge(S["dR0"], g + 1)
                    pe.wait_ge(S["aR1"], GT * (g + 1))
                    pe.wait_ge(S["aAT"], 2 * (g + 1))
                if n >= 2:
                    pe.wait_ge(S["aP"], n - 1)
                for f in range(2):
                    for b in range(2):
                        s = 2 * t + b
                        mm = pe.matmul(banks[3 + n % 2][L * b:L * b + L, 256 * f:256 * f + 256],
                                       aT[:, g % 2, f, L * s:L * s + L],
                                       rdiag[:, g % 2, f, s].rearrange("p h t -> p (h t)"), start=True, stop=True)
                mm.then_inc(S["pS"], 1)

            def t_o(g, t):
                n = GT * g + t
                pe.wait_ge(S["aP"], n + 1)
                if t == 0:
                    pe.wait_ge(S["aV"], 2 * GT * (g + 1))
                if n >= 2:
                    pe.wait_ge(S["dO"], 2 * (n - 1))
                for j in range(4):
                    mm = pe.matmul(banks[5 + n % 2][:, P * j:P * j + P], probs[:, n % 2, P * j:P * j + P],
                                   vbd[:, g % 2, t, :, 2 * VW * j:2 * VW * j + 64], start=True, stop=True)
                mm.then_inc(S["pO"], 1)

            def t_ot(g):
                pe.wait_ge(S["dO"], 2 * GT * (g + 1))
                if g >= 1:
                    pe.wait_ge(S["aE"], g)
                for t in range(GT):
                    mm = pe.transpose(banks[7][:, P * t:P * t + P],
                                      o_sb[:, g % 2, t].rearrange("p b j d -> p (b j d)"), ident[:, :])
                mm.then_inc(S["pOT"], 1)

            def t_y(g):
                pe.wait_ge(S["aOT"], g + 1)
                for t in range(GT):
                    for k in range(2):
                        for b in range(2):
                            r = slice(L * b, L * b + L)
                            c = P * t + L * k
                            mm = pe.matmul(banks[7][r, D * t:D * t + D], oT[r, 0, c:c + L], wp2[r, k, :],
                                           start=(k == 0), stop=(k == 1))
                mm.then_inc(S["pY"], 1)

            def t_x2(g):
                pe.wait_ge(S["dXn"], GT * (g + 1))
                for t in range(GT):
                    mm = pe.transpose(banks[7][:, P * t:P * t + P], xn[:, GT * g + t], ident[:, :])
                mm.then_inc(S["pX2"], 1)

            def t_l(g):
                pe.wait_ge(S["aX2"], g + 1)
                for t in range(GT):
                    mm = pe.matmul(banks[7][:, E * t:E * t + E], x2T[:, 1, P * t:P * t + P], selT[:, :],
                                   start=True, stop=True)
                mm.then_inc(S["pL"], 1)

            def t_tt(b):
                pe.wait_ge(S["r_m"], b + 1)
                pe.wait_ge(S["aE"], BG if b == 0 else GROUPS)
                pe.wait_ge(S["dH"], BG + 1)
                pe.matmul(banks[7][:, :], ones_bf[:, :], mb[:, :, :].rearrange("p e t -> p (e t)"),
                          start=True, stop=True).then_inc(S["r_tt"], 1)

            def t_r1(b):
                pe.wait_ge(S["r_et"], b + 1)
                pe.matmul(banks[7][:, :], tri[:, :], mb[:, :, :].rearrange("p e t -> p (e t)"),
                          start=True, stop=True).then_inc(S["r_r1"], 1)
                pe.wait_ge(S["r_pos"], b + 1)
                pe.matmul(banks[7][0:1, 0:P], ecol[:, 0:1], ident[:, :], start=True, stop=True)\
                  .then_inc(S["r_r1"], 1)
            t_x(0)
            t_qv(0)
            t_a2(0)
            t_at(0)
            t_bt(0)
            for g in range(GROUPS):
                if g == BG + 1:
                    t_r1(0)
                if g + 1 < GROUPS:
                    t_x(g + 1)
                t_s(g, 0)
                t_s(g, 1)
                if g >= 1:
                    if g == BG + 1:
                        pe.wait_ge(S["r_etab"], 1)
                    t_x2(g - 1)
                if g + 1 < GROUPS:
                    t_qv(g + 1)
                t_o(g, 0)
                t_s(g, 2)
                if g >= 1:
                    t_l(g - 1)
                t_o(g, 1)
                t_s(g, 3)
                if g + 1 < GROUPS:
                    t_a2(g + 1)
                    t_at(g + 1)
                t_o(g, 2)
                t_o(g, 3)
                if g + 1 < GROUPS:
                    t_bt(g + 1)
                t_ot(g)
                t_y(g)
                if g == BG:
                    t_tt(0)
            t_x2(GROUPS - 1)
            t_l(GROUPS - 1)
            t_tt(1)
            t_r1(1)

            def f_tp(n):
                pe.wait_ge(S[f"xg_l{n % 2}"], 16 * (n // 2 + 1))
                if n >= 2:
                    pe.wait_ge(S["f_xT"], n - 1)
                for t in range(GT):
                    mm = pe.transpose(banks[n % 2][:, P * t:P * t + P], xg[:, n % 2, t], ident[:, :])
                mm.then_inc(S["f_tp"], 1)

            def f_m1(n):
                pe.wait_ge(S["f_xT"], n + 1)
                pe.wait_ge(S["f_key"], GT * (n + 1))
                if n >= 2:
                    pe.wait_ge(S["f_h"], n - 1)
                for t in range(GT):
                    mm = pe.matmul(banks[2 + n % 2][:, P * t:P * t + P], keyc[:, n % 2, t], xgT[:, n % 2, P * t:P * t + P],
                                   start=True, stop=True)
                mm.then_inc(S["f_m1"], 1)

            def f_m2(n):
                b, c = divmod(n, SCH)
                pe.wait_ge(S["f_h"], n + 1)
                if n >= 2:
                    pe.wait_ge(S["f_y"], n - 1)
                for t in range(GT):
                    e = pe.value_load(etab[0:1, b, c * GT + t:c * GT + t + 1], min_val=0, max_val=E - 1)
                    mm = pe.matmul(banks[4 + n % 2][:, P * t:P * t + P], hexT[:, n % 2, P * t:P * t + P],
                                   values_sb[:, bass.ds(e, 1), :].rearrange("p a d -> p (a d)"),
                                   start=True, stop=True)
                mm.then_inc(S["f_m2"], 1)
            pe.wait_ge(S["ld_exp"], 32)
            for b in range(BLOCKS):
                pe.wait_ge(S["r_etab"], b + 1)
                n0 = b * SCH
                f_tp(n0)
                f_tp(n0 + 1)
                f_m1(n0)
                for c in range(1, SCH):
                    if c + 1 < SCH:
                        f_tp(n0 + c + 1)
                    f_m1(n0 + c)
                    f_m2(n0 + c - 1)
                f_m2(n0 + SCH - 1)


def kernel(**inputs):
    import numpy as np
    import concourse.bacc as bacc
    from concourse.bass_utils import run_bass_kernel_spmd

    a = {k.removeprefix("L0_"): np.asarray(v) for k, v in inputs.items()}
    seqs, _, high, wide = a["x"].shape
    emb = a["tok_W3_w"].shape[0]
    patch, heads = 16, 8
    hi, wi = high // patch, wide // patch
    tokens, hd, part = hi * wi, emb // heads, 128
    halves = patch * patch // part

    def layer(n, what):
        return a[f"tok_W{n}_{what}"].T.reshape(halves, part, -1)

    qkv = a["attn_W_qkv"].reshape(emb, hd, 2, heads)
    arrays = {
        "patches_t": a["x"].reshape(seqs, hi, patch, wi, patch).transpose(2, 4, 0, 1, 3)
        .reshape(halves, part, seqs * tokens),
        "noisy_w_t": np.stack([layer(1, "w"), layer(2, "w")]),
        "noisy_sw_t": np.stack([layer(1, "sw"), layer(2, "sw")]),
        "noisy_cols": np.stack([a["tok_W1_b"], a["tok_W2_b"], a["tok_W1_sb"], a["tok_W2_sb"],
                                a["tok_eps_out1"], a["tok_eps_out2"],
                                *a["tok_eps_in1"].reshape(halves, part), *a["tok_eps_in2"].reshape(halves, part)],
                               axis=1),
        "eps_out_rows": np.stack([a["tok_eps_out1"], a["tok_eps_out2"]]),
        "w3_t": a["tok_W3_w"].T,
        "bias_rows": np.stack([a["tok_W3_b"], a["attn_b_proj"]]),
        "w_qv": qkv.transpose(0, 2, 3, 1).reshape(emb, 2 * emb),
        "w_out": a["attn_W_proj"].reshape(heads // 2, 2, hd, emb).transpose(0, 2, 1, 3).reshape(emb // 2, 2, emb),
        "sel_t": a["ffn_expert_sel"].T,
        "keys_t": a["ffn_keys"].transpose(1, 0, 2),
        "values_t": a["ffn_values"].transpose(1, 0, 2),
    }
    at = np.arange(tokens, dtype=np.float32)[:, None]
    div = np.exp(np.arange(0, emb, 2, dtype=np.float32) * np.float32(-np.log(10000.0) / emb))
    ang = (at * div).astype(np.float32)
    code = np.stack([np.sin(ang), np.cos(ang)], axis=-1).reshape(tokens, emb).astype(np.float32)
    arrays["position_code"] = np.concatenate([code, code], axis=0)
    arrays = {k: np.ascontiguousarray(v) for k, v in arrays.items()}

    nc = bacc.Bacc("TRN2", target_bir_lowering=False, num_devices=1)
    args = [nc.dram_tensor(k, v.shape, mybir.dt.from_np(v.dtype), kind="ExternalInput").ap()
            for k, v in arrays.items()]
    args.append(nc.dram_tensor("tokens_out", (seqs, tokens, emb), F32, kind="ExternalOutput").ap())
    vit_tower_kernel(nc, *args)
    r = run_bass_kernel_spmd(nc, [arrays], core_ids=[0])
    return r.results[0]["tokens_out"]
```

```python
from contextlib import ExitStack

import concourse.bass as bass
from concourse import mybir

F32 = mybir.dt.float32
BF16 = mybir.dt.bfloat16
I32 = mybir.dt.int32
U32 = mybir.dt.uint32
ALU = mybir.AluOpType
ACT = mybir.ActivationFunctionType
AX_X = mybir.AxisListType.X

P = 128


def vit_tower_kernel(nc, x_t, w_t, sw_t, w_cols, w3_t, bias_rows, w_qv, w_out, sel_t, keys, values,
                     pos, out):
    HALVES, _, T = x_t.shape
    SEQS, L, D = out.shape
    HID = w_t.shape[-1]
    HEADS, HD = 8, D // 8
    E = keys.shape[1]
    TILES = T // P
    GT = 4
    GROUPS = TILES // GT
    GTOK = GT * P
    GSEQ = GTOK // L
    BLOCKS = 2
    RG = GROUPS * 5 // 8
    BT = (RG * GT, TILES - RG * GT)
    BTM = max(BT)
    FIRST = (0, BT[0])
    SCH = tuple(-(-(2 * bt + E - 1) // GT) for bt in BT)
    CHUNKS = sum(SCH)
    HP = 32
    VW = HD + 1
    VROW = 3 * 2 * VW + 64
    assert L == 64 and D == 128 and HID == 128 and HALVES == 2
    EPS = 1e-5
    ROW_AT = 3
    H0 = E * BT[0] // 2
    ROUTE_PARTS = (((0, 7, slice(0, H0)), (0, 2, slice(H0, 2 * H0)), (1, 7, slice(0, H0)), (1, 2, slice(H0, 2 * H0))),
                   ((0, 6, slice(0, E * BT[1])), (1, 7, slice(0, E * BT[1]))))
    assert H0 <= 512 and E * BT[1] <= 512


    def block_chunk(n):
        return (0, n) if n < SCH[0] else (1, n - SCH[0])
    xg_dram = [nc.dram_tensor(f"xg_rows{b}", [SCH[b] * GTOK, D], F32, kind="Internal").ap()
               for b in range(BLOCKS)]
    y_dram = [nc.dram_tensor(f"y_rows{b}", [SCH[b] * GTOK, D], F32, kind="Internal").ap()
               for b in range(BLOCKS)]

    with ExitStack() as ctx:
        def sb(name, shape, dt=F32):
            return ctx.enter_context(nc.sbuf_tensor(name, shape, dt))

        def sem(name):
            return ctx.enter_context(nc.semaphore(name))

        banks = [ctx.enter_context(nc.psum_tensor(f"bank{i}", [P, 512], F32)) for i in range(8)]

        keys_sb = sb("keys_sb", [P, E, HID])
        values_sb = sb("values_sb", [P, E, D])
        h = sb("h", [P, TILES, D])
        xn = sb("xn", [P, TILES, D])
        ident = sb("ident", [P, P])
        seq_ones = sb("seq_ones", [P, P])
        tri = sb("tri", [P, P], BF16)
        ones_bf = sb("ones_bf", [P, P], BF16)
        head_mask = sb("head_mask", [P, GT])
        iota_e = sb("iota_e", [P, E])
        thr = sb("thr", [P, BTM])
        part_no = sb("part_no", [P, 1])
        scan_keep = sb("scan_keep", [P, E * TILES])
        onesE = sb("onesE", [P, E])
        half = sb("half", [P, 6])
        mhalf = sb("mhalf", [P, TILES])
        zeros = sb("zeros", [P, GT * D])
        wn_t = sb("wn_t", [P, 2, 2, HID])
        swn_t = sb("swn_t", [P, 2, 2, HID])
        cols = sb("cols", [P, 10])
        f_abs = sb("f_abs", [P, 6])
        f_sgn = sb("f_sgn", [P, 6])
        eo_diag = sb("eo_diag", [P, 2, HID])
        ones_f = sb("ones_f", [P, P])
        tiny = sb("tiny", [P, 1])
        two = sb("two", [P, 1])
        sb_eo = sb("sb_eo", [P, 2])
        bn_col = sb("bn_col", [P, 2])
        w3T = sb("w3T", [P, D])
        base = sb("base", [P, D])
        bias_b = sb("bias_b", [P, 2, D])
        wqv = sb("wqv", [P, 2 * D])
        wp2 = sb("wp2", [P, 2, D])
        selT = sb("selT", [P, E])
        hot = sb("hot", [P, 2, E, TILES])
        topw = sb("topw", [P, TILES, 2])
        pos_u = sb("pos_u", [P, 2, TILES], U32)
        etab = sb("etab", [1, BLOCKS, P], I32)
        n2 = sb("n2", [P, TILES])
        bmax = sb("bmax", [P, TILES])
        bmaxh = sb("bmaxh", [P, TILES])
        seqmax = sb("seqmax", [TILES, 2])
        seqmax_b = sb("seqmax_b", [TILES, P])

        XS = 2 * T
        arena_a = sb("arena_a", [P, XS])
        xT = arena_a[:, :].rearrange("p (f t) -> p f t", f=2)
        RW = GSEQ * GT * L
        rdiag = arena_a[:, :].rearrange("p (u f s h t) -> p u f s h t", u=2, f=2, s=GSEQ, h=GT)
        assert XS == 2 * 2 * RW

        arena_b = sb("arena_b", [P, 10 * 1024 + 512])
        mish = arena_b[:, 0:2 * 6 * GTOK].rearrange("p (u k t) -> p u k t", u=2, k=6)
        o = 0
        XR = 6
        xg = arena_b[:, o:o + XR * GTOK].rearrange("p (u t d) -> p u t d", u=XR, t=GT)
        o += XR * GTOK
        xgT = arena_b[:, o:o + 2 * GTOK].rearrange("p (u t) -> p u t", u=2)
        o += 2 * GTOK
        experts_low = o
        o = 11 * GTOK
        keyc = arena_b[:, o:o + 2 * GTOK].rearrange("p (u t d) -> p u t d", u=2, t=GT)
        o += 2 * GTOK
        hexT = arena_b[:, o:o + 2 * GTOK].rearrange("p (u t) -> p u t", u=2)
        o += 2 * GTOK
        yb = arena_b[:, o:o + 2 * GTOK].rearrange("p (u t d) -> p u t d", u=2, t=GT)
        experts_end = o + 2 * GTOK

        o = 0

        def part(n):
            nonlocal o
            o += n
            return arena_b[:, o - n:o]
        xnT = part(2 * GTOK).rearrange("p (u t) -> p u t", u=2)
        probs = part(2 * 512).rearrange("p (u t) -> p u t", u=2)
        sq = part(GTOK)
        aT = part(2 * 2 * GTOK).rearrange("p (u f t) -> p u f t", u=2, f=2)
        assert o >= experts_low
        o_sb = part(2 * GTOK).rearrange("p (u t b j d) -> p u t b j d", u=2, t=GT, b=2, j=4)
        assert o <= 11 * GTOK <= 2 * 6 * GTOK
        o = 2 * 6 * GTOK
        vbd = part(2 * GT * 2 * VROW).rearrange("p (u t b v) -> p u t b v", u=2, t=GT, b=2)
        assert o >= experts_end
        x2T = part(2 * GTOK).rearrange("p (u t) -> p u t", u=2)
        oT = x2T
        a_tok = sb("a_tok", [P, 2, GT, HEADS, HP])
        b_tok = sb("b_tok", [P, 2, GT, HEADS, HP])
        v8 = sb("v8", [P, 2, GT * HEADS])
        c8 = sb("c8", [P, 2, 3, GT * HEADS])
        rden = sb("rden", [P, 2, 16])
        stats = sb("stats", [P, GT, 6])
        mv = sb("mv", [P, 2, GT, 2])
        veps = sb("veps", [P, 2, GT])
        rstd = sb("rstd", [P, 2, GT])
        all_mv = sb("all_mv", [P, TILES, 2])
        sel = sb("sel", [P, 3, GT, E])
        m8 = sb("m8", [P, GT, 8])
        i8 = sb("i8", [P, GT, 8], U32)
        idxf = sb("idxf", [P, GT, 2])
        rt_all = sb("rt", [P, 4, E * BTM])
        mb_all = sb("mb", [P, E * BTM], BF16)
        cnt = sb("cnt", [P, 4, E])
        posf = sb("posf", [P, 2, BTM])
        ecol = sb("ecol", [P, 1])
        YR, OR = 8, 4
        yg = arena_a[:, 0:YR * 2 * D].rearrange("p (r k d) -> p r k d", r=YR, k=2)
        ob = arena_a[:, YR * 2 * D:(YR * 2 + OR * GT) * D].rearrange("p (u t d) -> p u t d", u=OR, t=GT)

        names = ("ld_small ld_w ld_rows ld_attn ld_exp ld_x0 ld_x1 ld_x2 ld_x3 ld_x4 ld_x5 ld_x6 ld_x7 zero_done "
                 "c_pool c_dve "
                 "s_prep s_ones s_bg s_abs s_powed s_diag s_eo_ps s_wn "
                 "lin_ps m_gate m_inner m_min m_exp m_num m_log m_rec0 m_rec m_gi m_gin m_u w3_ps "
                 "h_done ln_stat ln_mv ln_eps ln_rstd ln_xn hb_done "
                 "n2_s n2_ps bm_s bm_ps bm_log bm_dve bm_done "
                 "pX aXT pQ aAq aSq aV dV dAv pA2 gA dC dB pAT aAT pBT dR0 aR1 pS aP pO dRd dO "
                 "pOT aOT pY dH dSt dMv dEp gR dXn pX2 aX2 pL aE dS1 dSel dTop dIx dIf dHot "
                 "r_m r_tt r_ld r_dve r_pos r_et r_row r_etab "
                 "scat0 scat1 xg_l0 xg_l1 xg_l2 xg_l3 f_tp f_xT f_key f_m1 f_h f_m2 f_y y_st0 y_st1 "
                 "gat0 gat1 gat2 gat3 gat4 gat5 gat6 gat7 xg_l4 xg_l5 c_t c_o "
                 "out_st0 out_st1 out_st2 out_st3").split()
        S = {n: sem(n) for n in names}

        block = ctx.enter_context(nc.Block())

        @block.sync
        def _(sp):
            def patches(n):
                ts = slice(GTOK * n, GTOK * n + GTOK)
                sp.dma_start(xT[:, :, ts], x_t[:, :, ts].rearrange("f p t -> p f t")).then_inc(S[f"ld_x{n}"], 16)
            sp.dma_start(cols[:, :], w_cols).then_inc(S["ld_small"], 16)
            sp.dma_start(wn_t[:, :, :, :], w_t.rearrange("a f p o -> p a f o")).then_inc(S["ld_w"], 16)
            sp.dma_start(swn_t[:, :, :, :], sw_t.rearrange("a f p o -> p a f o")).then_inc(S["ld_w"], 16)
            patches(0)
            sp.dma_start(w3T[:, :], w3_t).then_inc(S["ld_rows"], 16)
            sp.dma_start(base[:, :], pos).then_inc(S["ld_rows"], 16)
            sp.dma_start(bias_b[:, :, :], bias_rows.partition_broadcast(P)).then_inc(S["ld_rows"], 16)
            for n in range(1, GROUPS):
                patches(n)
            sp.dma_start(wqv[:, :], w_qv).then_inc(S["ld_attn"], 16)
            sp.dma_start(selT[:, :], sel_t).then_inc(S["ld_attn"], 16)
            for b in range(2):
                sp.dma_start(wp2[L * b:L * b + L, :, :], w_out).then_inc(S["ld_attn"], 16)
            sp.dma_start(keys_sb[:, :, :], keys).then_inc(S["ld_exp"], 16)
            sp.dma_start(values_sb[:, :, :], values).then_inc(S["ld_exp"], 16)
            sp.wait_ge(S["c_dve"], 1)
            for b in range(BLOCKS):
                rows = xg_dram[b].rearrange("(c p t) d -> c p (t d)", p=P, t=GT)
                with sp.Fori(0, SCH[b]) as c:
                    sp.dma_start(rows[bass.ds(c, 1)].rearrange("a p x -> p (a x)"), zeros[:, :])\
                      .then_inc(S["zero_done"], 16)

            def load_chunk(n):
                b, c = block_chunk(n)
                if c == 0:
                    sp.wait_ge(S[f"scat{b}"], 2 * BT[b] * 16)
                if n == 0:
                    sp.wait_ge(S["pO"], TILES)
                if n >= XR:
                    sp.wait_ge(S["f_tp"], n - XR + 1)
                sp.dma_start(xg[:, n % XR], xg_dram[b][c * GTOK:(c + 1) * GTOK, :].rearrange("(t p) d -> p t d", p=P))\
                  .then_inc(S[f"xg_l{n % XR}"], 16)

            def store_out(g):
                sp.wait_ge(S["c_o"], GT * (g + 1))
                sp.dma_start(out[g * GSEQ:(g + 1) * GSEQ].rearrange("(t b) l d -> (b l) t d", b=2), ob[:, g % OR])\
                  .then_inc(S[f"out_st{g % OR}"], 16)

            for n in range(CHUNKS):
                load_chunk(n)
            for g in range(GROUPS):
                store_out(g)
            for r in range(OR):
                sp.wait_ge(S[f"out_st{r}"], 16 * GROUPS // OR)
            sp.wait_ge(S["y_st0"], 16 * CHUNKS // 2)
            sp.wait_ge(S["y_st1"], 16 * CHUNKS // 2)

        @block.gpsimd
        def _(pool):
            pool.memset(ident[:, :], 0.0).then_inc(S["c_pool"], 1)
            pool.memset(ones_bf[:, :], 1.0).then_inc(S["c_pool"], 1)
            pool.memset(half[:, :], 0.5).then_inc(S["c_pool"], 1)
            pool.memset(mhalf[:, :], -0.5).then_inc(S["c_pool"], 1)
            pool.wait_ge(S["c_pool"], 4)
            pool.affine_select(out=ident[:, :], in_=ident[:, :], compare_op=ALU.not_equal, fill=1.0, base=0,
                               pattern=[[-1, P]], channel_multiplier=1).then_inc(S["c_pool"], 1)
            pool.affine_select(out=tri[:, :], in_=ones_bf[:, :], compare_op=ALU.is_gt, fill=0.0, base=0,
                               pattern=[[1, P]], channel_multiplier=-1).then_inc(S["c_pool"], 1)
            pool.iota(iota_e[:, :], pattern=[[1, E]], base=0, channel_multiplier=0,
                      allow_small_or_imprecise_dtypes=True).then_inc(S["c_pool"], 1)
            pool.iota(thr[:, :], pattern=[[P, BTM]], base=0, channel_multiplier=0,
                      allow_small_or_imprecise_dtypes=True).then_inc(S["c_pool"], 1)
            pool.iota(part_no[:, :], pattern=[[0, 1]], base=0, channel_multiplier=1,
                      allow_small_or_imprecise_dtypes=True).then_inc(S["c_pool"], 1)
            pool.wait_ge(S["s_abs"], 1)
            pool.tensor_tensor(f_abs[:, :], f_abs[:, :], half[:, 0:6], ALU.pow).then_inc(S["s_powed"], 1)

            pool.memset(vbd.rearrange("p u t b v -> p (u t b v)"), 0.0).then_inc(S["s_bg"], 1)
            for u in range(2):
                for b in range(2):
                    r = slice(L * b, L * b + L)
                    pool.wait_ge(S["s_bg"], 1 + 2 * u + b)
                    pool.memset(vbd[r, u, :, b, 0:HEADS * VW].rearrange("p t (h v) -> p t h v", v=VW)[:, :, :, HD:VW],
                                1.0).then_inc(S["s_bg"], 1)
            pool.wait_ge(S["s_bg"], 5)

            def gi_product(n):
                u = n % 2
                pool.wait_ge(S["m_gate"], n + 1)
                pool.wait_ge(S["m_inner"], n + 1)
                pool.tensor_tensor(mish[:, u, 1], mish[:, u, 0], mish[:, u, 1], ALU.mult).then_inc(S["m_gi"], 1)

            def gin_product(n):
                u = n % 2
                pool.wait_ge(S["m_num"], n + 1)
                pool.wait_ge(S["m_gi"], n + 1)
                pool.tensor_tensor(mish[:, u, 1], mish[:, u, 1], mish[:, u, 3], ALU.mult).then_inc(S["m_gin"], 1)

            def ln1_rstd(n):
                pool.wait_ge(S["ln_eps"], n + 1)
                pool.tensor_tensor(rstd[:, n % 2], veps[:, n % 2], mhalf[:, 0:GT], ALU.pow).then_inc(S["ln_rstd"], 1)

            def add_bproj(n):
                pool.wait_ge(S["ln_xn"], GT * (n + 1))
                for t in range(GT * n, GT * n + GT):
                    pool.tensor_tensor(h[:, t], h[:, t], bias_b[:, 1], ALU.add).then_inc(S["hb_done"], 1)
            for n in range(GROUPS + 3):
                if n < GROUPS:
                    gi_product(n)
                    gin_product(n)
                if n >= 3:
                    ln1_rstd(n - 3)
                if n == GROUPS:
                    pool.wait_ge(S["lin_ps"], 2 * GROUPS)
                    for u in range(2):
                        pool.memset(rdiag[:, u, 1].rearrange("p s h t -> p (s h t)"), 0.0).then_inc(S["s_bg"], 1)

            def scatter(b, t, k):
                pool.indirect_dma_start(
                    xg_dram[b], bass.IndirectOffsetOnAxis(ap=pos_u[:, k, t:t + 1], axis=0),
                    xn[:, t, :], None).then_inc(S[f"scat{b}"], 16)

            def gather(t, k):
                pool.indirect_dma_start(
                    yg[:, t % YR, k, :], None,
                    y_dram[int(t >= BT[0])], bass.IndirectOffsetOnAxis(ap=pos_u[:, k, t:t + 1], axis=0))\
                    .then_inc(S[f"gat{t % YR}"], 16)

            pend = []

            def some(n):
                for _ in range(min(n, len(pend))):
                    scatter(*pend.pop(0))
            add_bproj(0)
            for g in range(GROUPS):
                if g == RG:
                    pool.wait_ge(S["r_pos"], 1)
                    pool.wait_ge(S["zero_done"], 16 * CHUNKS)
                    pend = [(0, t, k) for t in range(BT[0]) for k in range(2)]
                    some(2)
                pool.wait_ge(S["dEp"], g + 1)
                pool.tensor_tensor(rstd[:, g % 2], veps[:, g % 2], mhalf[:, 0:GT], ALU.pow).then_inc(S["gR"], 1)
                for n in range(2 * g + 1, min(2 * g + 3, GROUPS)):
                    add_bproj(n)
                some(20 if g < GROUPS - 2 else 11 if g < GROUPS - 1 else len(pend))
            pool.wait_ge(S["r_pos"], 2)
            for t in range(BT[0], TILES):
                for k in range(2):
                    scatter(1, t, k)
            for t in range(TILES):
                if t in FIRST:
                    n = SCH[0] if t == 0 else CHUNKS
                    pool.wait_ge(S["y_st0"], 16 * -(-n // 2))
                    pool.wait_ge(S["y_st1"], 16 * (n // 2))
                if t >= YR:
                    pool.wait_ge(S["c_o"], t - YR + 1)
                gather(t, 0)
                gather(t, 1)

        @block.scalar
        def _(act):
            def gate_in(n):
                u = n % 2
                act.wait_ge(S["lin_ps"], 2 * n + 1)
                if n >= 2:
                    act.wait_ge(S["m_gi"], n - 1)
                    act.wait_ge(S["m_min"], n - 1)
                act.activation(mish[:, u, 0], banks[2 + 2 * u][:, :], ACT.Identity, bias=bn_col[:, 0:1])\
                   .then_inc(S["m_gate"], 1)
                act.wait_ge(S["lin_ps"], 2 * n + 2)
                if n >= 2:
                    act.wait_ge(S["m_u"], n - 1)
                act.activation(mish[:, u, 1], banks[3 + 2 * u][:, :], ACT.Identity, bias=bn_col[:, 1:2], scale=-1.0)\
                   .then_inc(S["m_inner"], 1)

            def gate_exp(n):
                u = n % 2
                act.wait_ge(S["m_min"], n + 1)
                act.activation(mish[:, u, 2], mish[:, u, 2], ACT.Exp).then_inc(S["m_exp"], 1)

            def gate_recip(n):
                u = n % 2
                act.wait_ge(S["m_num"], n + 1)
                if n >= 2:
                    act.wait_ge(S["m_rec"], 2 * (n - 1))
                act.activation(mish[:, u, 4], mish[:, u, 3], ACT.Ln, bias=two[:, 0:1]).then_inc(S["m_log"], 1)
                act.wait_ge(S["m_log"], n + 1)
                act.activation(mish[:, u, 4], mish[:, u, 4], ACT.Exp, scale=-1.0).then_inc(S["m_rec0"], 1)
            act.preload_act_table_set("natural_log_exp_and_others")
            act.wait_ge(S["s_ones"], 4)
            act.wait_ge(S["s_wn"], 7)
            for n in range(GROUPS + 1):
                if n < GROUPS:
                    gate_in(n)
                if n >= 1:
                    gate_recip(n - 1)
                if n < GROUPS:
                    gate_exp(n)
            def e_xT(g):
                act.wait_ge(S["pX"], g + 1)
                if g >= 2:
                    act.wait_ge(S["pQ"], GT * (g - 1))
                act.activation(xnT[:, g % 2], banks[0][:, :], ACT.Copy).then_inc(S["aXT"], 1)

            def e_qv(g):
                u = g % 2
                if g == 0:
                    act.wait_ge(S["s_prep"], 20)
                    act.wait_ge(S["s_bg"], 5)
                if g >= 1:
                    act.wait_ge(S["dV"], g)
                for q in range(2):
                    act.wait_ge(S["pQ"], GT * g + 2 * q + 2)
                    src = banks[1 + q][:, :].rearrange("p (t a h d) -> p t a h d", t=2, a=2, h=HEADS)
                    act.activation(sq[:, 256 * q:256 * q + 256].rearrange("p (t x) -> p t x", t=2),
                                   src[:, :, 0].rearrange("p t h d -> p t (h d)"), ACT.Square).then_inc(S["aSq"], 1)
                    if g >= 2:
                        act.wait_ge(S["pAT"], 2 * (g - 1))
                    act.activation(a_tok[:, u, 2 * q:2 * q + 2, :, 0:HD], src[:, :, 0], ACT.Copy).then_inc(S["aAq"], 1)
                    if g >= 2:
                        act.wait_ge(S["pO"], GT * (g - 1))
                    for b in range(2):
                        r = slice(L * b, L * b + L)
                        act.activation(
                            vbd[r, u, 2 * q:2 * q + 2, b, 0:HEADS * VW]
                            .rearrange("p t (h v) -> p t h v", v=VW)[:, :, :, 0:HD],
                            src[r, :, 1], ACT.Copy).then_inc(S["aV"], 1)

            def e_a(g):
                u = g % 2
                act.wait_ge(S["pA2"], g + 1)
                act.activation(c8[:, u, 1], banks[0][:, 0:GT * HEADS], ACT.Ln, bias=tiny[:, 0:1]).then_inc(S["gA"], 1)
                act.wait_ge(S["gA"], 2 * g + 1)
                act.activation(c8[:, u, 1], c8[:, u, 1], ACT.Exp, scale=0.5).then_inc(S["gA"], 1)

            def e_exp(g, t):
                n = GT * g + t
                act.wait_ge(S["pS"], n + 1)
                if n >= 2:
                    act.wait_ge(S["pO"], n - 1)
                act.activation(probs[:, n % 2], banks[3 + n % 2][:, :], ACT.Exp).then_inc(S["aP"], 1)

            def e_aT(g):
                for f in range(2):
                    act.wait_ge(S["pAT"], 2 * g + f + 1)
                    if g >= 2:
                        act.wait_ge(S["pS"], GT * (g - 1))
                    act.activation(aT[:, g % 2, f], banks[1 + f][:, :], ACT.Copy).then_inc(S["aAT"], 1)

            def e_r1(g):
                act.wait_ge(S["pBT"], 2 * g + 2)
                if g == 0:
                    act.wait_ge(S["s_bg"], 7)
                if g >= 2:
                    act.wait_ge(S["pS"], GT * (g - 1))
                for k in range(GT):
                    r = slice(HP * k, HP * k + HP)
                    act.activation(rdiag[r, g % 2, 1, :, k, :],
                                   banks[1][r, :].rearrange("p (s t) -> p s t", s=GSEQ), ACT.Copy)\
                       .then_inc(S["aR1"], 1)

            def e_oT(g):
                act.wait_ge(S["pOT"], g + 1)
                act.activation(oT[:, 0], banks[7][:, :], ACT.Copy).then_inc(S["aOT"], 1)

            def e_x2(g):
                act.wait_ge(S["pX2"], g + 1)
                act.activation(x2T[:, 1], banks[7][:, :], ACT.Copy).then_inc(S["aX2"], 1)

            def e_sel(g):
                act.wait_ge(S["pL"], g + 1)
                if g >= 1:
                    act.wait_ge(S["dS1"], g)
                act.activation(sel[:, 0].rearrange("p t e -> p (t e)"), banks[7][:, 0:GT * E], ACT.Exp, scale=-1.0)\
                   .then_inc(S["aE"], 1)
            act.wait_ge(S["m_u"], GROUPS - 1)
            e_xT(0)
            e_qv(0)
            e_a(0)
            e_aT(0)
            act.wait_ge(S["bm_ps"], 1)
            act.activation(bmax[:, :], banks[7][:, 0:TILES], ACT.Ln, bias=tiny[:, 0:1]).then_inc(S["bm_log"], 1)
            act.wait_ge(S["bm_log"], 1)
            act.activation(bmax[:, :], bmax[:, :], ACT.Exp, scale=0.5).then_inc(S["bm_log"], 1)

            e_r1(0)
            for g in range(GROUPS):
                nxt, old = g + 1 < GROUPS, g >= 1
                if nxt:
                    e_xT(g + 1)
                e_exp(g, 0)
                if g == RG + 1:
                    e_exp(g, 1)
                    e_qv(g + 1)
                    e_oT(g - 1)
                else:
                    if old:
                        e_oT(g - 1)
                    if nxt:
                        e_qv(g + 1)
                    e_exp(g, 1)
                if nxt:
                    e_a(g + 1)
                e_exp(g, 2)
                if nxt:
                    e_aT(g + 1)
                e_exp(g, 3)
                if nxt:
                    e_r1(g + 1)
                if old:
                    e_x2(g - 1)
                    e_sel(g - 1)

            def f_xT(n):
                act.wait_ge(S["f_tp"], n + 1)
                if n >= 2:
                    act.wait_ge(S["f_m1"], n - 1)
                act.activation(xgT[:, n % 2], banks[n % 2][:, :], ACT.Copy).then_inc(S["f_xT"], 1)

            def f_h(n):
                act.wait_ge(S["f_m1"], n + 1)
                if n >= 2:
                    act.wait_ge(S["f_m2"], n - 1)
                act.activation(hexT[:, n % 2], banks[2 + n % 2][:, :], ACT.Relu).then_inc(S["f_h"], 1)

            def f_y(n):
                act.wait_ge(S["f_m2"], n + 1)
                if n >= 2:
                    act.wait_ge(S[f"y_st{n % 2}"], 16 * (n // 2))
                act.activation(yb[:, n % 2].rearrange("p t d -> p (t d)"), banks[4 + n % 2][:, :], ACT.Copy)\
                   .then_inc(S["f_y"], 1)

            def store_chunk(n):
                b, c = block_chunk(n)
                act.wait_ge(S["f_y"], n + 1)
                act.dma_start(y_dram[b][c * GTOK:(c + 1) * GTOK, :].rearrange("(t p) d -> p t d", p=P), yb[:, n % 2])\
                   .then_inc(S[f"y_st{n % 2}"], 16)
            e_oT(GROUPS - 1)
            e_x2(GROUPS - 1)
            e_sel(GROUPS - 1)
            f_xT(0)
            for n in range(CHUNKS):
                if n + 1 < CHUNKS:
                    f_xT(n + 1)
                f_h(n)
                if n >= 1:
                    f_y(n - 1)
                    store_chunk(n - 1)
            f_y(CHUNKS - 1)
            store_chunk(CHUNKS - 1)

        @block.vector
        def _(dve):
            dve.memset(zeros[:, :], 0.0).then_inc(S["c_dve"], 1)
            dve.memset(head_mask[:, :], 0.0).then_inc(S["s_prep"], 1)
            dve.memset(scan_keep[:, :], 1.0).then_inc(S["s_prep"], 1)
            dve.memset(onesE[:, :], 1.0).then_inc(S["s_prep"], 1)
            dve.memset(seq_ones[:, :], 0.0).then_inc(S["s_ones"], 1)
            dve.memset(ones_f[:, :], 1.0).then_inc(S["s_ones"], 1)
            dve.memset(tiny[:, :], 1e-37).then_inc(S["s_ones"], 1)
            dve.memset(two[:, :], 2.0).then_inc(S["s_ones"], 1)
            dve.wait_ge(S["s_prep"], 3)
            dve.wait_ge(S["s_ones"], 4)
            for b in range(2):
                dve.memset(seq_ones[L * b:L * (b + 1), L * b:L * (b + 1)], 1.0).then_inc(S["s_ones"], 1)
            dve.memset(scan_keep[:, 0:E * BT[0]].rearrange("p (e t) -> p e t", e=E)[:, :, 0:1], 0.0)\
               .then_inc(S["s_prep"], 1)
            dve.memset(scan_keep[:, E * BT[0]:E * TILES].rearrange("p (e t) -> p e t", e=E)[:, :, 0:1], 0.0)\
               .then_inc(S["s_prep"], 1)
            for k in range(GT):
                dve.memset(head_mask[HP * k:HP * k + HP, k:k + 1], 1.0).then_inc(S["s_prep"], 1)
            dve.wait_ge(S["ld_small"], 16)
            dve.scalar_tensor_tensor(out=f_abs[:, :], in0=cols[:, 4:10], scalar=-1.0, in1=cols[:, 4:10],
                                     op0=ALU.mult, op1=ALU.max).then_inc(S["s_abs"], 1)
            dve.tensor_scalar(f_sgn[:, :], cols[:, 4:10], 0.0, None, ALU.is_lt).then_inc(S["s_prep"], 1)
            dve.wait_ge(S["s_prep"], 10)
            dve.tensor_scalar(f_sgn[:, :], f_sgn[:, :], -2.0, 1.0, ALU.mult, ALU.add).then_inc(S["s_prep"], 1)
            dve.wait_ge(S["s_prep"], 11)
            dve.wait_ge(S["s_powed"], 1)
            dve.tensor_tensor(f_abs[:, :], f_abs[:, :], f_sgn[:, :], ALU.mult).then_inc(S["s_prep"], 1)
            dve.wait_ge(S["s_prep"], 12)
            dve.wait_ge(S["c_pool"], 9)
            for a in range(2):
                dve.tensor_scalar(eo_diag[:, a], ident[:, :], f_abs[:, a:a + 1], None, ALU.mult)\
                   .then_inc(S["s_diag"], 1)
            dve.wait_ge(S["s_eo_ps"], 1)
            dve.wait_ge(S["ld_w"], 32)
            for a in range(2):
                for f in range(2):
                    dve.scalar_tensor_tensor(out=swn_t[:, a, f], in0=banks[7][:, HID * a:HID * a + HID],
                                             scalar=f_abs[:, 2 + 2 * a + f:3 + 2 * a + f],
                                             in1=swn_t[:, a, f], op0=ALU.mult, op1=ALU.mult).then_inc(S["s_prep"], 1)
            dve.tensor_tensor(sb_eo[:, :], cols[:, 2:4], f_abs[:, 0:2], ALU.mult).then_inc(S["s_prep"], 1)
            dve.wait_ge(S["s_prep"], 17)
            for a in range(2):
                for f in range(2):
                    dve.tensor_tensor(wn_t[:, a, f], swn_t[:, a, f], wn_t[:, a, f], ALU.add).then_inc(S["s_wn"], 1)
            dve.tensor_tensor(bn_col[:, :], sb_eo[:, :], cols[:, 0:2], ALU.add).then_inc(S["s_wn"], 1)
            dve.wait_ge(S["s_wn"], 5)
            dve.tensor_scalar(bn_col[:, 1:2], bn_col[:, 1:2], -1.0, None, ALU.mult).then_inc(S["s_wn"], 1)
            dve.wait_ge(S["ld_rows"], 16 * 3)
            dve.tensor_tensor(base[:, :], base[:, :], bias_b[:, 0], ALU.add).then_inc(S["s_wn"], 1)
            for t in (a_tok, b_tok):
                dve.memset(t[:, :, :, :, :].rearrange("p u t h x -> p (u t h x)"), 0.0).then_inc(S["s_prep"], 1)
            dve.wait_ge(S["s_prep"], 19)
            dve.memset(a_tok[:, :, :, :, HD + 1:HD + 2].rearrange("p u t h x -> p (u t h) x"), 1.0)\
               .then_inc(S["s_prep"], 1)

            def gate_min(n):
                u = n % 2
                dve.wait_ge(S["m_gate"], n + 1)
                dve.tensor_scalar(mish[:, u, 2], mish[:, u, 0], 20.0, None, ALU.min).then_inc(S["m_min"], 1)

            def gate_tanh(n):
                u = n % 2
                dve.wait_ge(S["m_exp"], n + 1)
                if n >= 2:
                    dve.wait_ge(S["m_gin"], n - 1)
                dve.scalar_tensor_tensor(out=mish[:, u, 3], in0=mish[:, u, 2], scalar=2.0, in1=mish[:, u, 2],
                                         op0=ALU.add, op1=ALU.mult).then_inc(S["m_num"], 1)

            def gate_out(n):
                u = n % 2
                dve.wait_ge(S["m_rec0"], n + 1)
                dve.scalar_tensor_tensor(out=mish[:, u, 2], in0=mish[:, u, 3], scalar=2.0, in1=mish[:, u, 4],
                                         op0=ALU.add, op1=ALU.mult).then_inc(S["m_rec"], 1)
                dve.wait_ge(S["m_rec"], 2 * n + 1)
                dve.scalar_tensor_tensor(out=mish[:, u, 4], in0=mish[:, u, 2], scalar=2.0, in1=mish[:, u, 4],
                                         op0=ALU.subtract, op1=ALU.mult).then_inc(S["m_rec"], 1)
                dve.wait_ge(S["m_rec"], 2 * n + 2)
                dve.wait_ge(S["m_gin"], n + 1)
                if n >= 2:
                    dve.wait_ge(S["w3_ps"], n - 1)
                dve.tensor_tensor(mish[:, u, 5], mish[:, u, 1], mish[:, u, 4], ALU.mult).then_inc(S["m_u"], 1)

            def ln1(n):
                u = n % 2
                ts = slice(GT * n, GT * n + GT)
                dve.wait_ge(S["w3_ps"], n + 1)
                dve.tensor_tensor(h[:, ts], banks[6 + u][:, :].rearrange("p (t d) -> p t d", t=GT),
                                  base[:, :].unsqueeze(1).to_broadcast([P, GT, D]), ALU.add).then_inc(S["h_done"], 1)
                dve.wait_ge(S["h_done"], n + 1)
                for t in range(GT):
                    dve.bn_stats(stats[:, t, :], h[:, GT * n + t, :]).then_inc(S["ln_stat"], 1)
                dve.wait_ge(S["ln_stat"], GT * (n + 1))
                for t in range(GT):
                    dve.bn_aggr(all_mv[:, GT * n + t, :], stats[:, t, :]).then_inc(S["ln_mv"], 1)
                dve.wait_ge(S["ln_mv"], GT * (n + 1))
                if n >= 2:
                    dve.wait_ge(S["ln_rstd"], n - 1)
                dve.tensor_scalar(veps[:, u], all_mv[:, ts, 1:2].rearrange("p t a -> p (t a)"), EPS, None, ALU.add)\
                   .then_inc(S["ln_eps"], 1)

            def ln1_apply(n):
                dve.wait_ge(S["ln_rstd"], n + 1)
                for t in range(GT):
                    dve.tensor_scalar(xn[:, GT * n + t], h[:, GT * n + t], all_mv[:, GT * n + t, 0:1],
                                      rstd[:, n % 2, t:t + 1], ALU.subtract, ALU.mult).then_inc(S["ln_xn"], 1)
                dve.wait_ge(S["ln_mv"], GT * (n + 1))
                ts = slice(GT * n, GT * n + GT)
                dve.tensor_tensor(n2[:, ts], all_mv[:, ts, 1:2].rearrange("p t a -> p (t a)"), rstd[:, n % 2],
                                  ALU.mult).then_inc(S["n2_s"], 1)
                dve.wait_ge(S["n2_s"], 2 * n + 1)
                dve.scalar_tensor_tensor(out=n2[:, ts], in0=n2[:, ts], scalar=float(D), in1=rstd[:, n % 2],
                                         op0=ALU.mult, op1=ALU.mult).then_inc(S["n2_s"], 1)
            def d_v(g):
                u = g % 2
                dve.wait_ge(S["aSq"], 2 * g + 2)
                if g >= 2:
                    dve.wait_ge(S["pA2"], g - 1)
                dve.tensor_reduce(v8[:, u], sq[:, :].rearrange("p (x d) -> p x d", d=HD), AX_X, ALU.add)\
                   .then_inc(S["dV"], 1)
                dve.wait_ge(S["dV"], g + 1)
                if g >= 2:
                    dve.wait_ge(S["pAT"], 2 * (g - 1))
                dve.tensor_copy(a_tok[:, u, :, :, HD:HD + 1].rearrange("p t h x -> p (t h) x"),
                                v8[:, u].unsqueeze(2)).then_inc(S["dAv"], 1)

            for n in range(GROUPS + 4):
                if n < GROUPS:
                    gate_min(n)
                if 1 <= n <= GROUPS:
                    gate_out(n - 1)
                if n < GROUPS:
                    gate_tanh(n)
                if 3 <= n < GROUPS + 3:
                    ln1(n - 3)
                if n == GROUPS + 3:
                    d_v(0)
                if n >= 4:
                    ln1_apply(n - 4)
            dve.wait_ge(S["n2_ps"], 1)
            dve.tensor_reduce(seqmax[:, :], banks[7][0:TILES, 0:P].rearrange("p (b l) -> p b l", b=2), AX_X, ALU.max)\
               .then_inc(S["bm_s"], 1)
            dve.wait_ge(S["bm_s"], 1)
            dve.tensor_copy(seqmax_b[:, :].rearrange("p (b l) -> p b l", b=2),
                            seqmax[:, :].unsqueeze(2).to_broadcast([TILES, 2, L])).then_inc(S["bm_s"], 1)
            dve.wait_ge(S["bm_ps"], 1)
            dve.wait_ge(S["bm_log"], 2)
            dve.reciprocal(bmaxh[:, :], bmax[:, :]).then_inc(S["bm_dve"], 1)
            dve.wait_ge(S["bm_dve"], 1)
            dve.tensor_tensor(bmaxh[:, :], banks[7][:, 0:TILES], bmaxh[:, :], ALU.mult).then_inc(S["bm_dve"], 1)
            dve.wait_ge(S["bm_dve"], 2)
            dve.tensor_tensor(bmaxh[:, :], bmax[:, :], bmaxh[:, :], ALU.add).then_inc(S["bm_dve"], 1)
            dve.wait_ge(S["bm_dve"], 3)
            dve.tensor_scalar(bmaxh[:, :], bmaxh[:, :], 0.25, None, ALU.mult).then_inc(S["bm_dve"], 1)
            def d_c(g):
                u = g % 2
                a0, ta, tb = c8[:, u, 1], c8[:, u, 0], c8[:, u, 2]
                dve.wait_ge(S["gA"], 2 * (g + 1))
                dve.reciprocal(tb, a0).then_inc(S["dC"], 1)
                dve.wait_ge(S["dC"], 6 * g + 1)
                dve.tensor_tensor(ta, banks[0][:, 0:GT * HEADS], tb, ALU.mult).then_inc(S["dC"], 1)
                dve.wait_ge(S["dC"], 6 * g + 2)
                dve.tensor_tensor(ta, ta, a0, ALU.add).then_inc(S["dC"], 1)
                dve.wait_ge(S["dC"], 6 * g + 3)
                if g == 0:
                    dve.wait_ge(S["bm_dve"], 4)
                dve.tensor_tensor(ta.rearrange("p (t h) -> p t h", t=GT), ta.rearrange("p (t h) -> p t h", t=GT),
                                  bmaxh[:, GT * g:GT * g + GT].unsqueeze(2).to_broadcast([P, GT, HEADS]),
                                  ALU.mult).then_inc(S["dC"], 1)
                dve.wait_ge(S["dC"], 6 * g + 4)
                dve.tensor_scalar(ta, ta, 1e-10, 0.005, ALU.add, ALU.mult).then_inc(S["dC"], 1)
                dve.wait_ge(S["dC"], 6 * g + 5)
                dve.reciprocal(tb, ta).then_inc(S["dC"], 1)
                dve.wait_ge(S["dC"], 6 * g + 6)
                dve.wait_ge(S["aAq"], 2 * (g + 1))
                if g >= 2:
                    dve.wait_ge(S["pBT"], 2 * (g - 1))
                dve.tensor_tensor(b_tok[:, u, :, :, 0:HD].rearrange("p t h d -> p (t h) d"),
                                  a_tok[:, u, :, :, 0:HD].rearrange("p t h d -> p (t h) d"),
                                  c8[:, u, 2].unsqueeze(2).to_broadcast([P, GT * HEADS, HD]), ALU.mult)\
                   .then_inc(S["dB"], 1)
                dve.tensor_scalar(b_tok[:, u, :, :, HD:HD + 1].rearrange("p t h x -> p (t h) x"),
                                  c8[:, u, 2].unsqueeze(2), -0.5, None, ALU.mult).then_inc(S["dB"], 1)
                dve.scalar_tensor_tensor(out=b_tok[:, u, :, :, HD + 1:HD + 2].rearrange("p t h x -> p (t h) x"),
                                         in0=c8[:, u, 2].unsqueeze(2), scalar=-0.5, in1=v8[:, u].unsqueeze(2),
                                         op0=ALU.mult, op1=ALU.mult).then_inc(S["dB"], 1)

            def d_r0(g):
                dve.wait_ge(S["pBT"], 2 * g + 1)
                if g >= 2:
                    dve.wait_ge(S["pS"], GT * (g - 1))
                dve.tensor_tensor(
                    rdiag[:, g % 2, 0],
                    banks[0][:, :].rearrange("p (s t) -> p s t", s=GSEQ).unsqueeze(2)
                    .to_broadcast([P, GSEQ, GT, L]),
                    head_mask[:, :].unsqueeze(1).unsqueeze(3).to_broadcast([P, GSEQ, GT, L]), ALU.mult)\
                   .then_inc(S["dR0"], 1)

            def d_o(g, t):
                n = GT * g + t
                dve.wait_ge(S["pO"], n + 1)
                src = banks[5 + n % 2][:, :].rearrange("p (x c) -> p x c", c=64)
                for k in range(2):
                    r = slice(L * k, L * k + L)
                    dve.reciprocal(rden[r, n % 2, 0:8], src[r, :, VW * k + HD]).then_inc(S["dRd"], 1)
                dve.wait_ge(S["dRd"], 2 * (n + 1))
                if g >= 2:
                    dve.wait_ge(S["pOT"], g - 1)
                for k in range(2):
                    r = slice(L * k, L * k + L)
                    dve.tensor_tensor(o_sb[r, g % 2, t].rearrange("p b j d -> p j b d"),
                                      src[r, :, VW * k:VW * k + HD].rearrange("p (j b) d -> p j b d", b=2),
                                      rden[r, n % 2, 0:8].rearrange("p (j b) -> p j b", b=2).unsqueeze(3)
                                      .to_broadcast([L, 4, 2, HD]), ALU.mult).then_inc(S["dO"], 1)

            def d_ln2(g):
                u = g % 2
                ts = slice(GT * g, GT * g + GT)
                dve.wait_ge(S["pY"], g + 1)
                dve.wait_ge(S["hb_done"], GT * (g + 1))
                dve.tensor_tensor(h[:, ts], banks[7][:, :].rearrange("p (t d) -> p t d", t=GT), h[:, ts], ALU.add)\
                   .then_inc(S["dH"], 1)
                dve.wait_ge(S["dH"], g + 1)
                for t in range(GT):
                    dve.bn_stats(stats[:, t, :], h[:, GT * g + t, :]).then_inc(S["dSt"], 1)
                dve.wait_ge(S["dSt"], GT * (g + 1))
                for t in range(GT):
                    dve.bn_aggr(mv[:, u, t, :], stats[:, t, :]).then_inc(S["dMv"], 1)
                dve.wait_ge(S["dMv"], GT * (g + 1))
                dve.tensor_scalar(veps[:, u], mv[:, u, :, 1:2].rearrange("p t a -> p (t a)"), EPS, None, ALU.add)\
                   .then_inc(S["dEp"], 1)

            def d_ln2_apply(g):
                dve.wait_ge(S["gR"], g + 1)
                for t in range(GT):
                    dve.tensor_scalar(xn[:, GT * g + t], h[:, GT * g + t], mv[:, g % 2, t, 0:1],
                                      rstd[:, g % 2, t:t + 1], ALU.subtract, ALU.mult).then_inc(S["dXn"], 1)

            def d_top(g):
                dve.wait_ge(S["aE"], g + 1)
                dve.tensor_scalar(sel[:, 1], sel[:, 0], 1.0, None, ALU.add).then_inc(S["dS1"], 1)
                dve.wait_ge(S["dS1"], g + 1)
                dve.reciprocal(sel[:, 2], sel[:, 1]).then_inc(S["dSel"], 1)
                dve.wait_ge(S["dSel"], g + 1)
                for t in range(GT):
                    dve.max(m8[:, t], sel[:, 2, t]).then_inc(S["dTop"], 1)
                dve.wait_ge(S["dTop"], GT * (g + 1))
                for t in range(GT):
                    dve.max_index(i8[:, t], m8[:, t], sel[:, 2, t]).then_inc(S["dIx"], 1)
                ts = slice(GT * g, GT * g + GT)
                dve.tensor_copy(topw[:, ts], m8[:, :, 0:2]).then_inc(S["dHot"], 1)
                dve.wait_ge(S["dIx"], GT * (g + 1))
                dve.tensor_copy(idxf[:, :, :], i8[:, :, 0:2]).then_inc(S["dIf"], 1)
                dve.wait_ge(S["dIf"], g + 1)
                for k in range(2):
                    dve.tensor_tensor(hot[:, k, :, ts], iota_e[:, :].unsqueeze(2).to_broadcast([P, E, GT]),
                                      idxf[:, :, k].unsqueeze(1).to_broadcast([P, E, GT]), ALU.is_equal)\
                       .then_inc(S["dHot"], 1)

            rd = [0]

            def step(ins):
                rd[0] += 1
                ins.then_inc(S["r_dve"], 1)
                dve.wait_ge(S["r_dve"], rd[0])

            def d_route_mask(b):
                bs = slice(FIRST[b], FIRST[b] + BT[b])
                dve.wait_ge(S["dHot"], 3 * (RG if b == 0 else GROUPS))
                dve.tensor_tensor(mb_all[:, 0:E * BT[b]].rearrange("p (e t) -> p e t", e=E),
                                  hot[:, 0, :, bs], hot[:, 1, :, bs], ALU.add).then_inc(S["r_m"], 1)

            def d_route_load(b):
                for i, (k, bank, part) in enumerate(ROUTE_PARTS[b]):
                    dve.wait_ge(S["r_tt"], len(ROUTE_PARTS[0]) * b + i + 1)
                    dve.tensor_copy(rt_all[:, k, part], banks[bank][:, 0:part.stop - part.start])\
                       .then_inc(S["r_ld"], 1)

            def d_route(b):
                bt, n = BT[b], E * BT[b]
                flat = [rt_all[:, k, 0:n] for k in range(4)]
                rt = [f.rearrange("p (e t) -> p e t", e=E) for f in flat]
                dve.wait_ge(S["r_ld"], len(ROUTE_PARTS[0]) + len(ROUTE_PARTS[1]) * b)
                step(dve.tensor_tensor_scan(flat[2], scan_keep[:, E * FIRST[b]:E * FIRST[b] + n], flat[0], 0.0,
                                            ALU.mult, ALU.add))
                step(dve.tensor_tensor(flat[0], flat[2], flat[0], ALU.subtract))
                step(dve.tensor_tensor(rt[3], rt[2][:, :, bt - 1:bt].to_broadcast([P, E, bt]),
                                       thr[:, 0:bt].unsqueeze(1).to_broadcast([P, E, bt]), ALU.is_gt))
                step(dve.tensor_reduce(cnt[:, 0], rt[3], AX_X, ALU.add))
                step(dve.tensor_tensor_scan(cnt[:, 1], onesE[:, :], cnt[:, 0], 0.0, ALU.mult, ALU.add))
                step(dve.tensor_tensor(cnt[:, 2], cnt[:, 1], cnt[:, 0], ALU.subtract))
                step(dve.tensor_scalar(cnt[:, 3], cnt[:, 1], part_no[:, 0:1], None, ALU.is_le))
                dve.tensor_reduce(ecol[:, :], cnt[:, 3], AX_X, ALU.add).then_inc(S["r_et"], 1)
                step(dve.scalar_tensor_tensor(out=rt[0], in0=cnt[:, 2].unsqueeze(2).to_broadcast([P, E, bt]),
                                              scalar=float(P), in1=rt[0], op0=ALU.mult, op1=ALU.add))
                step(dve.tensor_tensor(flat[0], flat[1], flat[0], ALU.add))
                bs = slice(FIRST[b], FIRST[b] + bt)
                for k in range(2):
                    step(dve.tensor_tensor(rt[2], rt[0], hot[:, k, :, bs], ALU.mult))
                    step(dve.tensor_reduce(posf[:, k, 0:bt], rt[2].rearrange("p e t -> p t e"), AX_X, ALU.add))
                dve.tensor_copy(pos_u[:, :, bs], posf[:, :, 0:bt]).then_inc(S["r_pos"], 1)

            def d_etab(b):
                dve.wait_ge(S["r_row"], b + 1)
                dve.tensor_scalar(etab[0:1, b, :], banks[7][0:1, 0:P], float(E - 1), None, ALU.min)\
                   .then_inc(S["r_etab"], 1)
            d_c(0)
            d_r0(0)
            for g in range(GROUPS):
                nxt, old = g + 1 < GROUPS, g >= 1
                if g == RG + 2:
                    d_etab(0)
                if g == RG + 1:
                    d_route_load(0)
                    d_route(0)
                if nxt:
                    d_v(g + 1)
                if old:
                    d_ln2(g - 1)
                d_o(g, 0)
                if nxt:
                    d_c(g + 1)
                if old:
                    d_ln2_apply(g - 1)
                d_o(g, 1)
                if nxt:
                    d_r0(g + 1)
                d_o(g, 2)
                d_o(g, 3)
                if old:
                    d_top(g - 1)
                if g == RG:
                    d_route_mask(0)

            def key_copy(n):
                b, c = block_chunk(n)
                if n >= 2:
                    dve.wait_ge(S["f_m1"], n - 1)
                _, experts = nc.values_load_multi_w_load_instructions(
                    etab[0:1, b, c * GT:c * GT + GT], engines=[mybir.EngineType.DVE], min_val=0, max_val=E - 1)
                for t, e in enumerate(experts):
                    dve.tensor_copy(keyc[:, n % 2, t:t + 1, :], keys_sb[:, bass.ds(e, 1), :]).then_inc(S["f_key"], 1)

            def combine(t):
                g = t // GT
                dve.wait_ge(S[f"gat{t % YR}"], 32 * (t // YR + 1))
                if t % GT == 0 and g >= OR:
                    dve.wait_ge(S[f"out_st{g % OR}"], 16 * (g // OR))
                dve.scalar_tensor_tensor(out=h[:, t], in0=yg[:, t % YR, 0], scalar=topw[:, t, 0:1], in1=h[:, t],
                                         op0=ALU.mult, op1=ALU.add).then_inc(S["c_t"], 1)
                dve.wait_ge(S["c_t"], t + 1)
                dve.scalar_tensor_tensor(out=ob[:, g % OR, t % GT], in0=yg[:, t % YR, 1], scalar=topw[:, t, 1:2],
                                         in1=h[:, t], op0=ALU.mult, op1=ALU.add).then_inc(S["c_o"], 1)

            d_ln2(GROUPS - 1)
            d_ln2_apply(GROUPS - 1)
            dve.wait_ge(S["ld_exp"], 32)
            dve.wait_ge(S["pO"], TILES)
            key_copy(0)
            key_copy(1)
            d_top(GROUPS - 1)
            d_route_mask(1)
            d_route_load(1)
            d_route(1)
            for n in range(CHUNKS):
                if n == ROW_AT:
                    d_etab(1)
                if n + 2 < CHUNKS:
                    key_copy(n + 2)
                if n >= SCH[0] + 2:
                    combine(n - SCH[0] - 2)
            for t in range(SCH[1] - 2, TILES):
                combine(t)

        @block.tensor
        def _(pe):
            def linear(n):
                u = n % 2
                pe.wait_ge(S[f"ld_x{n}"], 16)
                for a in range(2):
                    if n >= 2:
                        pe.wait_ge(S["m_gate" if a == 0 else "m_inner"], n - 1)
                    for f in range(2):
                        mm = pe.matmul(banks[2 + 2 * u + a][:, :], wn_t[:, a, f, :],
                                       xT[:, f, GTOK * n:GTOK * n + GTOK], start=(f == 0), stop=(f == 1))
                    mm.then_inc(S["lin_ps"], 1)

            def embed(n):
                u = n % 2
                pe.wait_ge(S["m_u"], n + 1)
                if n >= 2:
                    pe.wait_ge(S["h_done"], n - 1)
                for t in range(GT):
                    mm = pe.matmul(banks[6 + u][:, D * t:D * t + D], mish[:, u, 5, P * t:P * t + P], w3T[:, :],
                                   start=True, stop=True)
                mm.then_inc(S["w3_ps"], 1)
            pe.wait_ge(S["c_pool"], 9)
            pe.wait_ge(S["s_ones"], 6)
            pe.wait_ge(S["s_diag"], 2)
            pe.matmul(banks[7][:, 0:2 * HID], ones_f[:, :], eo_diag[:, :, :].rearrange("p a o -> p (a o)"),
                      start=True, stop=True).then_inc(S["s_eo_ps"], 1)
            pe.wait_ge(S["s_wn"], 7)
            def t_x(g):
                pe.wait_ge(S["ln_xn"], GT * (g + 1))
                if g >= 1:
                    pe.wait_ge(S["dR0"], g)
                for t in range(GT):
                    mm = pe.transpose(banks[0][:, P * t:P * t + P], xn[:, GT * g + t], ident[:, :])
                mm.then_inc(S["pX"], 1)

            def t_qv(g):
                pe.wait_ge(S["aXT"], g + 1)
                pe.wait_ge(S["ld_attn"], 16 * 4)
                if g >= 1:
                    pe.wait_ge(S["aR1"], GT * g)
                    pe.wait_ge(S["aAT"], 2 * g)
                for t in range(GT):
                    pe.matmul(banks[1 + t // 2][:, 256 * (t % 2):256 * (t % 2) + 256], xnT[:, g % 2, P * t:P * t + P],
                              wqv[:, :], start=True, stop=True)\
                      .then_inc(S["pQ"], 1)

            def t_a2(g):
                pe.wait_ge(S["dV"], g + 1)
                pe.wait_ge(S["aXT"], g + 1)
                pe.matmul(banks[0][:, 0:GT * HEADS], seq_ones[:, :], v8[:, g % 2], start=True, stop=True)\
                  .then_inc(S["pA2"], 1)

            def t_at(g):
                pe.wait_ge(S["dAv"], g + 1)
                pe.wait_ge(S["aAq"], 2 * (g + 1))
                pe.wait_ge(S["aV"], GT * (g + 1))
                for f in range(2):
                    for t in range(GT):
                        mm = pe.transpose(banks[1 + f][:, P * t:P * t + P],
                                          a_tok[:, g % 2, t, 4 * f:4 * f + 4, :].rearrange("p h x -> p (h x)"),
                                          ident[:, :])
                    mm.then_inc(S["pAT"], 1)

            def t_bt(g):
                pe.wait_ge(S["dB"], 3 * (g + 1))
                for f in range(2):
                    pe.wait_ge(S["aAT"], 2 * g + 1)
                    for t in range(GT):
                        mm = pe.transpose(banks[f][:, P * t:P * t + P],
                                          b_tok[:, g % 2, t, 4 * f:4 * f + 4, :].rearrange("p h x -> p (h x)"),
                                          ident[:, :])
                    mm.then_inc(S["pBT"], 1)

            def t_s(g, t):
                n = GT * g + t
                if t == 0:
                    pe.wait_ge(S["dR0"], g + 1)
                    pe.wait_ge(S["aR1"], GT * (g + 1))
                    pe.wait_ge(S["aAT"], 2 * (g + 1))
                if n >= 2:
                    pe.wait_ge(S["aP"], n - 1)
                for f in range(2):
                    for b in range(2):
                        s = 2 * t + b
                        mm = pe.matmul(banks[3 + n % 2][L * b:L * b + L, 256 * f:256 * f + 256],
                                       aT[:, g % 2, f, L * s:L * s + L],
                                       rdiag[:, g % 2, f, s].rearrange("p h t -> p (h t)"), start=True, stop=True)
                mm.then_inc(S["pS"], 1)

            def t_o(g, t):
                n = GT * g + t
                pe.wait_ge(S["aP"], n + 1)
                if t == 0:
                    pe.wait_ge(S["aV"], GT * (g + 1))
                if n >= 2:
                    pe.wait_ge(S["dO"], 2 * (n - 1))
                for j in range(4):
                    mm = pe.matmul(banks[5 + n % 2][:, P * j:P * j + P], probs[:, n % 2, P * j:P * j + P],
                                   vbd[:, g % 2, t, :, 2 * VW * j:2 * VW * j + 64], start=True, stop=True)
                mm.then_inc(S["pO"], 1)

            def t_ot(g):
                pe.wait_ge(S["dO"], 2 * GT * (g + 1))
                if g >= 1:
                    pe.wait_ge(S["aE"], g)
                if g == RG:
                    pe.wait_ge(S["r_ld"], len(ROUTE_PARTS[0]))
                if g == RG + 1:
                    pe.wait_ge(S["r_etab"], 1)
                for t in range(GT):
                    mm = pe.transpose(banks[7][:, P * t:P * t + P],
                                      o_sb[:, g % 2, t].rearrange("p b j d -> p (b j d)"), ident[:, :])
                mm.then_inc(S["pOT"], 1)

            def t_y(g):
                pe.wait_ge(S["aOT"], g + 1)
                for t in range(GT):
                    for k in range(2):
                        for b in range(2):
                            r = slice(L * b, L * b + L)
                            c = P * t + L * k
                            mm = pe.matmul(banks[7][r, D * t:D * t + D], oT[r, 0, c:c + L], wp2[r, k, :],
                                           start=(k == 0), stop=(k == 1))
                mm.then_inc(S["pY"], 1)

            def t_x2(g):
                pe.wait_ge(S["dXn"], GT * (g + 1))
                for t in range(GT):
                    mm = pe.transpose(banks[7][:, P * t:P * t + P], xn[:, GT * g + t], ident[:, :])
                mm.then_inc(S["pX2"], 1)

            def t_l(g):
                pe.wait_ge(S["aX2"], g + 1)
                for t in range(GT):
                    mm = pe.matmul(banks[7][:, E * t:E * t + E], x2T[:, 1, P * t:P * t + P], selT[:, :],
                                   start=True, stop=True)
                mm.then_inc(S["pL"], 1)

            def t_tt(b, i):
                k, bank, part = ROUTE_PARTS[b][i]
                if i == 0:
                    pe.wait_ge(S["r_m"], b + 1)
                    pe.wait_ge(S["aE"], RG if b == 0 else GROUPS)
                if i >= 2:
                    pe.wait_ge(S["r_ld"], i - 1)
                pe.matmul(banks[bank][:, 0:part.stop - part.start], (ones_bf, tri)[k][:, :], mb_all[:, part],
                          start=True, stop=True).then_inc(S["r_tt"], 1)

            def t_row(b):
                pe.wait_ge(S["r_et"], b + 1)
                pe.wait_ge(S["aE"], RG + 1 if b == 0 else GROUPS)
                pe.matmul(banks[7][0:1, 0:P], ecol[:, 0:1], ident[:, :], start=True, stop=True)\
                  .then_inc(S["r_row"], 1)
            for n in range(GROUPS + 2):
                if n < GROUPS:
                    linear(n)
                if n == GROUPS + 1:
                    t_x(0)
                if n >= 2:
                    embed(n - 2)
            pe.wait_ge(S["m_gate"], GROUPS - 1)
            t_qv(0)
            t_a2(0)
            t_at(0)
            pe.wait_ge(S["n2_s"], 2 * GROUPS)
            pe.wait_ge(S["h_done"], GROUPS)
            pe.transpose(banks[7][0:TILES, 0:P], n2[:, :], ident[:, :]).then_inc(S["n2_ps"], 1)
            pe.wait_ge(S["bm_s"], 2)
            pe.transpose(banks[7][:, 0:TILES], seqmax_b[:, :], ident[0:TILES, 0:TILES]).then_inc(S["bm_ps"], 1)
            t_bt(0)
            for g in range(GROUPS):
                nxt, old = g + 1 < GROUPS, g >= 1
                if nxt:
                    t_x(g + 1)
                t_s(g, 0)
                if g == RG + 1:
                    t_tt(0, 0)
                    t_tt(0, 1)
                    t_s(g, 1)
                    t_tt(0, 2)
                    t_tt(0, 3)
                    pe.wait_ge(S["r_ld"], len(ROUTE_PARTS[0]))
                    t_qv(g + 1)
                    t_ot(g - 1)
                else:
                    if old:
                        t_ot(g - 1)
                    if nxt:
                        t_qv(g + 1)
                    t_s(g, 1)
                if old:
                    t_y(g - 1)
                t_o(g, 0)
                if nxt:
                    t_a2(g + 1)
                t_s(g, 2)
                if nxt:
                    t_at(g + 1)
                t_o(g, 1)
                t_s(g, 3)
                if nxt:
                    t_bt(g + 1)
                t_o(g, 2)
                if old:
                    t_x2(g - 1)
                t_o(g, 3)
                if old:
                    t_l(g - 1)
                if g == RG + 1:
                    t_row(0)

            def f_tp(n):
                pe.wait_ge(S[f"xg_l{n % XR}"], 16 * (n // XR + 1))
                if n >= 2:
                    pe.wait_ge(S["f_xT"], n - 1)
                for t in range(GT):
                    mm = pe.transpose(banks[n % 2][:, P * t:P * t + P], xg[:, n % XR, t], ident[:, :])
                mm.then_inc(S["f_tp"], 1)

            def f_m1(n):
                pe.wait_ge(S["f_xT"], n + 1)
                pe.wait_ge(S["f_key"], GT * (n + 1))
                if n < 2:
                    pe.wait_ge(S["aP"], TILES)
                    pe.wait_ge(S["dO"], 2 * TILES)
                if n >= 2:
                    pe.wait_ge(S["f_h"], n - 1)
                for t in range(GT):
                    mm = pe.matmul(banks[2 + n % 2][:, P * t:P * t + P], keyc[:, n % 2, t], xgT[:, n % 2, P * t:P * t + P],
                                   start=True, stop=True)
                mm.then_inc(S["f_m1"], 1)

            held = {}

            def m2_experts(n):
                b, c = block_chunk(n)
                _, held[n] = nc.values_load_multi_w_load_instructions(
                    etab[0:1, b, c * GT:c * GT + GT], engines=[mybir.EngineType.PE], min_val=0, max_val=E - 1)

            def f_m2(n):
                experts = held.pop(n)
                pe.wait_ge(S["f_h"], n + 1)
                if n >= 2:
                    pe.wait_ge(S["f_y"], n - 1)
                for t, e in enumerate(experts):
                    mm = pe.matmul(banks[4 + n % 2][:, P * t:P * t + P], hexT[:, n % 2, P * t:P * t + P],
                                   values_sb[:, bass.ds(e, 1), :].rearrange("p a d -> p (a d)"),
                                   start=True, stop=True)
                mm.then_inc(S["f_m2"], 1)
            pe.wait_ge(S["ld_exp"], 32)
            t_ot(GROUPS - 1)
            t_y(GROUPS - 1)
            t_x2(GROUPS - 1)
            t_l(GROUPS - 1)
            pe.wait_ge(S["dO"], 2 * TILES)
            for i in range(len(ROUTE_PARTS[1])):
                t_tt(1, i)
            f_tp(0)
            for n in range(CHUNKS):
                if n + 1 < CHUNKS:
                    f_tp(n + 1)
                if n == ROW_AT:
                    t_row(1)
                if n == SCH[0]:
                    pe.wait_ge(S["r_etab"], 2)
                if n >= 1:
                    m2_experts(n - 1)
                f_m1(n)
                if n >= 1:
                    f_m2(n - 1)
            m2_experts(CHUNKS - 1)
            f_m2(CHUNKS - 1)


def kernel(**inputs):
    import numpy as np
    import concourse.bacc as bacc
    from concourse.bass_utils import run_bass_kernel_spmd

    a = {k.removeprefix("L0_"): np.asarray(v) for k, v in inputs.items()}
    seqs, _, high, wide = a["x"].shape
    emb = a["tok_W3_w"].shape[0]
    patch, heads = 16, 8
    hi, wi = high // patch, wide // patch
    tokens, hd, part = hi * wi, emb // heads, 128
    halves = patch * patch // part

    def layer(n, what):
        return a[f"tok_W{n}_{what}"].T.reshape(halves, part, -1)

    qkv = a["attn_W_qkv"].reshape(emb, hd, 2, heads)
    arrays = {
        "patches_t": a["x"].reshape(seqs, hi, patch, wi, patch).transpose(2, 4, 0, 1, 3)
        .reshape(halves, part, seqs * tokens),
        "noisy_w_t": np.stack([layer(1, "w"), layer(2, "w")]),
        "noisy_sw_t": np.stack([layer(1, "sw"), layer(2, "sw")]),
        "noisy_cols": np.stack([a["tok_W1_b"], a["tok_W2_b"], a["tok_W1_sb"], a["tok_W2_sb"],
                                a["tok_eps_out1"], a["tok_eps_out2"],
                                *a["tok_eps_in1"].reshape(halves, part), *a["tok_eps_in2"].reshape(halves, part)],
                               axis=1),
        "w3_t": a["tok_W3_w"].T,
        "bias_rows": np.stack([a["tok_W3_b"], a["attn_b_proj"]]),
        "w_qv": qkv.transpose(0, 2, 3, 1).reshape(emb, 2 * emb),
        "w_out": a["attn_W_proj"].reshape(heads // 2, 2, hd, emb).transpose(0, 2, 1, 3).reshape(emb // 2, 2, emb),
        "sel_t": a["ffn_expert_sel"].T,
        "keys_t": a["ffn_keys"].transpose(1, 0, 2),
        "values_t": a["ffn_values"].transpose(1, 0, 2),
    }
    at = np.arange(tokens, dtype=np.float32)[:, None]
    div = np.exp(np.arange(0, emb, 2, dtype=np.float32) * np.float32(-np.log(10000.0) / emb))
    ang = (at * div).astype(np.float32)
    code = np.stack([np.sin(ang), np.cos(ang)], axis=-1).reshape(tokens, emb).astype(np.float32)
    arrays["position_code"] = np.concatenate([code, code], axis=0)
    arrays = {k: np.ascontiguousarray(v) for k, v in arrays.items()}

    nc = bacc.Bacc("TRN2", target_bir_lowering=False, num_devices=1)
    args = [nc.dram_tensor(k, v.shape, mybir.dt.from_np(v.dtype), kind="ExternalInput").ap()
            for k, v in arrays.items()]
    args.append(nc.dram_tensor("tokens_out", (seqs, tokens, emb), F32, kind="ExternalOutput").ap())
    vit_tower_kernel(nc, *args)
    r = run_bass_kernel_spmd(nc, [arrays], core_ids=[0])
    return r.results[0]["tokens_out"]
```

```python
from contextlib import ExitStack

import concourse.bass as bass
from concourse import mybir

F32 = mybir.dt.float32
BF16 = mybir.dt.bfloat16
I32 = mybir.dt.int32
U32 = mybir.dt.uint32
ALU = mybir.AluOpType
ACT = mybir.ActivationFunctionType
AX_X = mybir.AxisListType.X

P = 128


def vit_tower_kernel(nc, x_t, w_t, sw_t, w_cols, w3_t, bias_rows, w_qv, w_out, sel_t, keys, values,
                     pos, out):
    HALVES, _, T = x_t.shape
    SEQS, L, D = out.shape
    HID = w_t.shape[-1]
    HEADS, HD = 8, D // 8
    E = keys.shape[1]
    TILES = T // P
    GT = 4
    GROUPS = TILES // GT
    GTOK = GT * P
    GSEQ = GTOK // L
    BLOCKS = 2
    RG = GROUPS * 5 // 8
    BT = (RG * GT, TILES - RG * GT)
    BTM = max(BT)
    FIRST = (0, BT[0])
    SCH = tuple(-(-(2 * bt + E - 1) // GT) for bt in BT)
    CHUNKS = sum(SCH)
    HP = 32
    VW = HD + 1
    VROW = 3 * 2 * VW + 64
    assert L == 64 and D == 128 and HID == 128 and HALVES == 2
    EPS = 1e-5
    ROW_AT = 3
    H0 = E * BT[0] // 2
    ROUTE_PARTS = (((0, 7, slice(0, H0)), (0, 2, slice(H0, 2 * H0)), (1, 7, slice(0, H0)), (1, 2, slice(H0, 2 * H0))),
                   ((0, 6, slice(0, E * BT[1])), (1, 7, slice(0, E * BT[1]))))
    assert H0 <= 512 and E * BT[1] <= 512

    def block_chunk(n):
        return (0, n) if n < SCH[0] else (1, n - SCH[0])

    xg_dram = [nc.dram_tensor(f"xg_rows{b}", [SCH[b] * GTOK, D], F32, kind="Internal").ap()
               for b in range(BLOCKS)]
    y_dram = [nc.dram_tensor(f"y_rows{b}", [SCH[b] * GTOK, D], F32, kind="Internal").ap()
               for b in range(BLOCKS)]

    with ExitStack() as ctx:
        def sb(name, shape, dt=F32):
            return ctx.enter_context(nc.sbuf_tensor(name, shape, dt))

        def sem(name):
            return ctx.enter_context(nc.semaphore(name))

        banks = [ctx.enter_context(nc.psum_tensor(f"bank{i}", [P, 512], F32)) for i in range(8)]

        keys_sb = sb("keys_sb", [P, E, HID])
        values_sb = sb("values_sb", [P, E, D])
        h = sb("h", [P, TILES, D])
        xn = sb("xn", [P, TILES, D])
        ident = sb("ident", [P, P])
        seq_ones = sb("seq_ones", [P, P])
        tri = sb("tri", [P, P], BF16)
        ones_bf = sb("ones_bf", [P, P], BF16)
        head_mask = sb("head_mask", [P, GT])
        iota_e = sb("iota_e", [P, E])
        thr = sb("thr", [P, BTM])
        part_no = sb("part_no", [P, 1])
        scan_keep = sb("scan_keep", [P, E * TILES])
        onesE = sb("onesE", [P, E])
        half = sb("half", [P, 6])
        mhalf = sb("mhalf", [P, GT])
        zeros = sb("zeros", [P, GT * D])
        wn_t = sb("wn_t", [P, 2, 2, HID])
        swn_t = sb("swn_t", [P, 2, 2, HID])
        cols = sb("cols", [P, 10])
        f_abs = sb("f_abs", [P, 6])
        f_sgn = sb("f_sgn", [P, 6])
        eo_diag = sb("eo_diag", [P, 2, HID])
        ones_f = sb("ones_f", [P, P])
        tiny = sb("tiny", [P, 1])
        two = sb("two", [P, 1])
        sb_eo = sb("sb_eo", [P, 2])
        bn_col = sb("bn_col", [P, 2])
        w3T = sb("w3T", [P, D])
        base = sb("base", [P, D])
        bias_b = sb("bias_b", [P, 2, D])
        wqv = sb("wqv", [P, 2 * D])
        wp2 = sb("wp2", [P, 2, D])
        selT = sb("selT", [P, E])
        hot = sb("hot", [P, 2, E, TILES])
        topw = sb("topw", [P, TILES, 2])
        pos_u = sb("pos_u", [P, 2, TILES], U32)
        etab = sb("etab", [1, BLOCKS, P], I32)
        n2 = sb("n2", [P, TILES])
        bmax = sb("bmax", [P, TILES])
        bmaxh = sb("bmaxh", [P, TILES])
        seqmax = sb("seqmax", [TILES, 2])
        seqmax_b = sb("seqmax_b", [TILES, P])

        XS = 2 * T
        arena_a = sb("arena_a", [P, XS])
        xT = arena_a[:, :].rearrange("p (f t) -> p f t", f=2)
        RW = GSEQ * GT * L
        rdiag = arena_a[:, :].rearrange("p (u f s h t) -> p u f s h t", u=2, f=2, s=GSEQ, h=GT)
        assert XS == 2 * 2 * RW

        arena_b = sb("arena_b", [P, 10 * 1024 + 512])
        mish = arena_b[:, 0:2 * 6 * GTOK].rearrange("p (u k t) -> p u k t", u=2, k=6)
        o = 0
        XR = 6
        xg = arena_b[:, o:o + XR * GTOK].rearrange("p (u t d) -> p u t d", u=XR, t=GT)
        o += XR * GTOK
        xgT = arena_b[:, o:o + 2 * GTOK].rearrange("p (u t) -> p u t", u=2)
        o += 2 * GTOK
        experts_low = o
        o = 11 * GTOK
        keyc = arena_b[:, o:o + 2 * GTOK].rearrange("p (u t d) -> p u t d", u=2, t=GT)
        o += 2 * GTOK
        hexT = arena_b[:, o:o + 2 * GTOK].rearrange("p (u t) -> p u t", u=2)
        o += 2 * GTOK
        yb = arena_b[:, o:o + 2 * GTOK].rearrange("p (u t d) -> p u t d", u=2, t=GT)
        experts_end = o + 2 * GTOK

        o = 0

        def part(n):
            nonlocal o
            o += n
            return arena_b[:, o - n:o]
        xnT = part(2 * GTOK).rearrange("p (u t) -> p u t", u=2)
        probs = part(2 * 512).rearrange("p (u t) -> p u t", u=2)
        sq = part(GTOK)
        aT = part(2 * 2 * GTOK).rearrange("p (u f t) -> p u f t", u=2, f=2)
        assert o >= experts_low
        o_sb = part(2 * GTOK).rearrange("p (u t b j d) -> p u t b j d", u=2, t=GT, b=2, j=4)
        assert o <= 11 * GTOK <= 2 * 6 * GTOK
        o = 2 * 6 * GTOK
        vbd = part(2 * GT * 2 * VROW).rearrange("p (u t b v) -> p u t b v", u=2, t=GT, b=2)
        assert o >= experts_end
        x2T = part(2 * GTOK).rearrange("p (u t) -> p u t", u=2)
        oT = x2T
        a_tok = sb("a_tok", [P, 2, GT, HEADS, HP])
        b_tok = sb("b_tok", [P, 2, GT, HEADS, HP])
        v8 = sb("v8", [P, 2, GT * HEADS])
        c8 = sb("c8", [P, 2, 3, GT * HEADS])
        rden = sb("rden", [P, 2, 16])
        stats = sb("stats", [P, GT, 6])
        mv = sb("mv", [P, 2, GT, 2])
        veps = sb("veps", [P, 2, GT])
        rstd = sb("rstd", [P, 2, GT])
        all_mv = sb("all_mv", [P, TILES, 2])
        sel = sb("sel", [P, 3, GT, E])
        m8 = sb("m8", [P, GT, 8])
        i8 = sb("i8", [P, GT, 8], U32)
        idxf = sb("idxf", [P, GT, 2])
        rt_all = sb("rt", [P, 4, E * BTM])
        mb_all = sb("mb", [P, E * BTM], BF16)
        cnt = sb("cnt", [P, 4, E])
        posf = sb("posf", [P, 2, BTM])
        ecol = sb("ecol", [P, 1])
        YR, OR = 8, 4
        yg = arena_a[:, 0:YR * 2 * D].rearrange("p (r k d) -> p r k d", r=YR, k=2)
        ob = arena_a[:, YR * 2 * D:(YR * 2 + OR * GT) * D].rearrange("p (u t d) -> p u t d", u=OR, t=GT)

        names = ("ld_small ld_w ld_rows ld_attn ld_exp ld_x0 ld_x1 ld_x2 ld_x3 ld_x4 ld_x5 ld_x6 ld_x7 "
                 "zero_done c_pool c_dve s_prep s_ones s_bg s_abs s_powed s_diag s_eo_ps s_wn lin_ps "
                 "m_gate m_inner m_min m_exp m_num m_log m_rec0 m_rec m_gi m_gin m_u w3_ps h_done ln_stat "
                 "ln_mv ln_eps ln_rstd ln_xn hb_done n2_s n2_ps bm_s bm_ps bm_log bm_dve xT_in_psum "
                 "xT_copied qv_in_psum q_copied q_squared v_copied q_norms q_rows_done seq_norm_ps "
                 "root_first scale_steps b_rows_done aT_in_psum aT_copied bT_in_psum rdiag0_done "
                 "rdiag1_done scores_ready probs_ready heads_in_psum sums_inverted heads_done oT_in_psum "
                 "oT_copied proj_in_psum h_added ln2_stat ln2_mv ln2_eps ln2_rstd ln2_xn x2T_in_psum "
                 "x2T_copied logits_ready sel_exp sel_plus_one sel_sigmoid top_values top_indices "
                 "top_indices_f hot_done mask_done counts_ps counts_copied route_steps slots_done "
                 "tile_expert_col tile_expert_ps tile_expert_done scat0 scat1 xg_l0 xg_l1 xg_l2 xg_l3 "
                 "rowsT_in_psum rowsT_copied keys_copied hidden_ps hidden_done y_in_psum y_copied y_st0 "
                 "y_st1 gat0 gat1 gat2 gat3 gat4 gat5 gat6 gat7 xg_l4 xg_l5 first_added result_done "
                 "out_st0 out_st1 out_st2 out_st3").split()
        S = {n: sem(n) for n in names}

        block = ctx.enter_context(nc.Block())

        @block.sync
        def _(sp):
            def patches(n):
                ts = slice(GTOK * n, GTOK * n + GTOK)
                sp.dma_start(xT[:, :, ts], x_t[:, :, ts].rearrange("f p t -> p f t")).then_inc(S[f"ld_x{n}"], 16)
            sp.dma_start(cols[:, :], w_cols).then_inc(S["ld_small"], 16)
            sp.dma_start(wn_t[:, :, :, :], w_t.rearrange("a f p o -> p a f o")).then_inc(S["ld_w"], 16)
            sp.dma_start(swn_t[:, :, :, :], sw_t.rearrange("a f p o -> p a f o")).then_inc(S["ld_w"], 16)
            patches(0)
            sp.dma_start(w3T[:, :], w3_t).then_inc(S["ld_rows"], 16)
            sp.dma_start(base[:, :], pos).then_inc(S["ld_rows"], 16)
            sp.dma_start(bias_b[:, :, :], bias_rows.partition_broadcast(P)).then_inc(S["ld_rows"], 16)
            for n in range(1, GROUPS):
                patches(n)
            sp.dma_start(wqv[:, :], w_qv).then_inc(S["ld_attn"], 16)
            sp.dma_start(selT[:, :], sel_t).then_inc(S["ld_attn"], 16)
            for b in range(2):
                sp.dma_start(wp2[L * b:L * b + L, :, :], w_out).then_inc(S["ld_attn"], 16)
            sp.dma_start(keys_sb[:, :, :], keys).then_inc(S["ld_exp"], 16)
            sp.dma_start(values_sb[:, :, :], values).then_inc(S["ld_exp"], 16)
            sp.wait_ge(S["c_dve"], 1)
            for b in range(BLOCKS):
                rows = xg_dram[b].rearrange("(c p t) d -> c p (t d)", p=P, t=GT)
                with sp.Fori(0, SCH[b]) as c:
                    sp.dma_start(rows[bass.ds(c, 1)].rearrange("a p x -> p (a x)"), zeros[:, :])\
                      .then_inc(S["zero_done"], 16)

            def load_chunk(n):
                b, c = block_chunk(n)
                if c == 0:
                    sp.wait_ge(S[f"scat{b}"], 2 * BT[b] * 16)
                if n == 0:
                    sp.wait_ge(S["heads_in_psum"], TILES)
                if n >= XR:
                    sp.wait_ge(S["rowsT_in_psum"], n - XR + 1)
                sp.dma_start(xg[:, n % XR], xg_dram[b][c * GTOK:(c + 1) * GTOK, :].rearrange("(t p) d -> p t d", p=P))\
                  .then_inc(S[f"xg_l{n % XR}"], 16)


            def store_out(g):
                sp.wait_ge(S["result_done"], GT * (g + 1))
                sp.dma_start(out[g * GSEQ:(g + 1) * GSEQ].rearrange("(t b) l d -> (b l) t d", b=2), ob[:, g % OR])\
                  .then_inc(S[f"out_st{g % OR}"], 16)

            for n in range(CHUNKS):
                load_chunk(n)
            for g in range(GROUPS):
                store_out(g)
            for r in range(OR):
                sp.wait_ge(S[f"out_st{r}"], 16 * GROUPS // OR)
            sp.wait_ge(S["y_st0"], 16 * CHUNKS // 2)
            sp.wait_ge(S["y_st1"], 16 * CHUNKS // 2)

        @block.gpsimd
        def _(pool):
            pool.memset(ident[:, :], 0.0).then_inc(S["c_pool"], 1)
            pool.memset(ones_bf[:, :], 1.0).then_inc(S["c_pool"], 1)
            pool.memset(half[:, :], 0.5).then_inc(S["c_pool"], 1)
            pool.memset(mhalf[:, :], -0.5).then_inc(S["c_pool"], 1)
            pool.wait_ge(S["c_pool"], 4)
            pool.affine_select(out=ident[:, :], in_=ident[:, :], compare_op=ALU.not_equal, fill=1.0, base=0,
                               pattern=[[-1, P]], channel_multiplier=1).then_inc(S["c_pool"], 1)
            pool.affine_select(out=tri[:, :], in_=ones_bf[:, :], compare_op=ALU.is_gt, fill=0.0, base=0,
                               pattern=[[1, P]], channel_multiplier=-1).then_inc(S["c_pool"], 1)
            pool.iota(iota_e[:, :], pattern=[[1, E]], base=0, channel_multiplier=0,
                      allow_small_or_imprecise_dtypes=True).then_inc(S["c_pool"], 1)
            pool.iota(thr[:, :], pattern=[[P, BTM]], base=0, channel_multiplier=0,
                      allow_small_or_imprecise_dtypes=True).then_inc(S["c_pool"], 1)
            pool.iota(part_no[:, :], pattern=[[0, 1]], base=0, channel_multiplier=1,
                      allow_small_or_imprecise_dtypes=True).then_inc(S["c_pool"], 1)
            pool.wait_ge(S["s_abs"], 1)
            pool.tensor_tensor(f_abs[:, :], f_abs[:, :], half[:, 0:6], ALU.pow).then_inc(S["s_powed"], 1)

            pool.memset(vbd.rearrange("p u t b v -> p (u t b v)"), 0.0).then_inc(S["s_bg"], 1)
            for u in range(2):
                for b in range(2):
                    r = slice(L * b, L * b + L)
                    pool.wait_ge(S["s_bg"], 1 + 2 * u + b)
                    pool.memset(vbd[r, u, :, b, 0:HEADS * VW].rearrange("p t (h v) -> p t h v", v=VW)[:, :, :, HD:VW],
                                1.0).then_inc(S["s_bg"], 1)
            pool.wait_ge(S["s_bg"], 5)

            def gi_product(n):
                u = n % 2
                pool.wait_ge(S["m_gate"], n + 1)
                pool.wait_ge(S["m_inner"], n + 1)
                pool.tensor_tensor(mish[:, u, 1], mish[:, u, 0], mish[:, u, 1], ALU.mult).then_inc(S["m_gi"], 1)

            def gin_product(n):
                u = n % 2
                pool.wait_ge(S["m_num"], n + 1)
                pool.wait_ge(S["m_gi"], n + 1)
                pool.tensor_tensor(mish[:, u, 1], mish[:, u, 1], mish[:, u, 3], ALU.mult).then_inc(S["m_gin"], 1)

            def ln1_rstd(n):
                pool.wait_ge(S["ln_eps"], n + 1)
                pool.tensor_tensor(rstd[:, n % 2], veps[:, n % 2], mhalf[:, :], ALU.pow).then_inc(S["ln_rstd"], 1)

            def add_bproj(n):
                pool.wait_ge(S["ln_xn"], GT * (n + 1))
                for t in range(GT * n, GT * n + GT):
                    pool.tensor_tensor(h[:, t], h[:, t], bias_b[:, 1], ALU.add).then_inc(S["hb_done"], 1)
            for n in range(GROUPS + 3):
                if n < GROUPS:
                    gi_product(n)
                    gin_product(n)
                if n >= 3:
                    ln1_rstd(n - 3)
                if n == GROUPS:
                    pool.wait_ge(S["lin_ps"], 2 * GROUPS)
                    for u in range(2):
                        pool.memset(rdiag[:, u, 1].rearrange("p s h t -> p (s h t)"), 0.0).then_inc(S["s_bg"], 1)


            def scatter(b, t, k):
                pool.indirect_dma_start(
                    xg_dram[b], bass.IndirectOffsetOnAxis(ap=pos_u[:, k, t:t + 1], axis=0),
                    xn[:, t, :], None).then_inc(S[f"scat{b}"], 16)

            def gather(t, k):
                pool.indirect_dma_start(
                    yg[:, t % YR, k, :], None,
                    y_dram[int(t >= BT[0])], bass.IndirectOffsetOnAxis(ap=pos_u[:, k, t:t + 1], axis=0))\
                    .then_inc(S[f"gat{t % YR}"], 16)

            pend = []

            def some(n):
                for _ in range(min(n, len(pend))):
                    scatter(*pend.pop(0))
            add_bproj(0)
            for g in range(GROUPS):
                if g == RG:
                    pool.wait_ge(S["slots_done"], 1)
                    pool.wait_ge(S["zero_done"], 16 * CHUNKS)
                    pend = [(0, t, k) for t in range(BT[0]) for k in range(2)]
                    some(2)
                pool.wait_ge(S["ln2_eps"], g + 1)
                pool.tensor_tensor(rstd[:, g % 2], veps[:, g % 2], mhalf[:, :], ALU.pow).then_inc(S["ln2_rstd"], 1)
                for n in range(2 * g + 1, min(2 * g + 3, GROUPS)):
                    add_bproj(n)
                some(20 if g < GROUPS - 2 else 11 if g < GROUPS - 1 else len(pend))
            pool.wait_ge(S["slots_done"], 2)
            for t in range(BT[0], TILES):
                for k in range(2):
                    scatter(1, t, k)
            for t in range(TILES):
                if t in FIRST:
                    n = SCH[0] if t == 0 else CHUNKS
                    pool.wait_ge(S["y_st0"], 16 * -(-n // 2))
                    pool.wait_ge(S["y_st1"], 16 * (n // 2))
                if t >= YR:
                    pool.wait_ge(S["result_done"], t - YR + 1)
                gather(t, 0)
                gather(t, 1)

        @block.scalar
        def _(act):
            def gate_in(n):
                u = n % 2
                act.wait_ge(S["lin_ps"], 2 * n + 1)
                if n >= 2:
                    act.wait_ge(S["m_gi"], n - 1)
                    act.wait_ge(S["m_min"], n - 1)
                act.activation(mish[:, u, 0], banks[2 + 2 * u][:, :], ACT.Identity, bias=bn_col[:, 0:1])\
                   .then_inc(S["m_gate"], 1)
                act.wait_ge(S["lin_ps"], 2 * n + 2)
                if n >= 2:
                    act.wait_ge(S["m_u"], n - 1)
                act.activation(mish[:, u, 1], banks[3 + 2 * u][:, :], ACT.Identity, bias=bn_col[:, 1:2], scale=-1.0)\
                   .then_inc(S["m_inner"], 1)

            def gate_exp(n):
                u = n % 2
                act.wait_ge(S["m_min"], n + 1)
                act.activation(mish[:, u, 2], mish[:, u, 2], ACT.Exp).then_inc(S["m_exp"], 1)

            def gate_recip(n):
                u = n % 2
                act.wait_ge(S["m_num"], n + 1)
                if n >= 2:
                    act.wait_ge(S["m_rec"], 2 * (n - 1))
                act.activation(mish[:, u, 4], mish[:, u, 3], ACT.Ln, bias=two[:, 0:1]).then_inc(S["m_log"], 1)
                act.wait_ge(S["m_log"], n + 1)
                act.activation(mish[:, u, 4], mish[:, u, 4], ACT.Exp, scale=-1.0).then_inc(S["m_rec0"], 1)
            act.preload_act_table_set("natural_log_exp_and_others")
            act.wait_ge(S["s_ones"], 4)
            act.wait_ge(S["s_wn"], 7)
            for n in range(GROUPS + 1):
                if n < GROUPS:
                    gate_in(n)
                if n >= 1:
                    gate_recip(n - 1)
                if n < GROUPS:
                    gate_exp(n)
            def e_xT(g):
                act.wait_ge(S["xT_in_psum"], g + 1)
                if g >= 2:
                    act.wait_ge(S["qv_in_psum"], GT * (g - 1))
                act.activation(xnT[:, g % 2], banks[0][:, :], ACT.Copy).then_inc(S["xT_copied"], 1)

            def e_qv(g):
                u = g % 2
                if g == 0:
                    act.wait_ge(S["s_prep"], 20)
                    act.wait_ge(S["s_bg"], 5)
                if g >= 1:
                    act.wait_ge(S["q_norms"], g)
                for q in range(2):
                    act.wait_ge(S["qv_in_psum"], GT * g + 2 * q + 2)
                    src = banks[1 + q][:, :].rearrange("p (t a h d) -> p t a h d", t=2, a=2, h=HEADS)
                    act.activation(sq[:, 256 * q:256 * q + 256].rearrange("p (t x) -> p t x", t=2),
                                   src[:, :, 0].rearrange("p t h d -> p t (h d)"), ACT.Square).then_inc(S["q_squared"], 1)
                    if g >= 2:
                        act.wait_ge(S["aT_in_psum"], 2 * (g - 1))
                    act.activation(a_tok[:, u, 2 * q:2 * q + 2, :, 0:HD], src[:, :, 0], ACT.Copy).then_inc(S["q_copied"], 1)
                    if g >= 2:
                        act.wait_ge(S["heads_in_psum"], GT * (g - 1))
                    for b in range(2):
                        r = slice(L * b, L * b + L)
                        act.activation(
                            vbd[r, u, 2 * q:2 * q + 2, b, 0:HEADS * VW]
                            .rearrange("p t (h v) -> p t h v", v=VW)[:, :, :, 0:HD],
                            src[r, :, 1], ACT.Copy).then_inc(S["v_copied"], 1)

            def e_a(g):
                u = g % 2
                act.wait_ge(S["seq_norm_ps"], g + 1)
                act.activation(c8[:, u, 1], banks[0][:, 0:GT * HEADS], ACT.Ln, bias=tiny[:, 0:1]).then_inc(S["root_first"], 1)
                act.wait_ge(S["root_first"], 2 * g + 1)
                act.activation(c8[:, u, 1], c8[:, u, 1], ACT.Exp, scale=0.5).then_inc(S["root_first"], 1)

            def e_exp(g, t):
                n = GT * g + t
                act.wait_ge(S["scores_ready"], n + 1)
                if n >= 2:
                    act.wait_ge(S["heads_in_psum"], n - 1)
                act.activation(probs[:, n % 2], banks[3 + n % 2][:, :], ACT.Exp).then_inc(S["probs_ready"], 1)

            def e_aT(g):
                for f in range(2):
                    act.wait_ge(S["aT_in_psum"], 2 * g + f + 1)
                    if g >= 2:
                        act.wait_ge(S["scores_ready"], GT * (g - 1))
                    act.activation(aT[:, g % 2, f], banks[1 + f][:, :], ACT.Copy).then_inc(S["aT_copied"], 1)

            def e_r1(g):
                act.wait_ge(S["bT_in_psum"], 2 * g + 2)
                if g == 0:
                    act.wait_ge(S["s_bg"], 7)
                if g >= 2:
                    act.wait_ge(S["scores_ready"], GT * (g - 1))
                for k in range(GT):
                    r = slice(HP * k, HP * k + HP)
                    act.activation(rdiag[r, g % 2, 1, :, k, :],
                                   banks[1][r, :].rearrange("p (s t) -> p s t", s=GSEQ), ACT.Copy)\
                       .then_inc(S["rdiag1_done"], 1)

            def e_oT(g):
                act.wait_ge(S["oT_in_psum"], g + 1)
                act.activation(oT[:, 0], banks[7][:, :], ACT.Copy).then_inc(S["oT_copied"], 1)

            def e_x2(g):
                act.wait_ge(S["x2T_in_psum"], g + 1)
                act.activation(x2T[:, 1], banks[7][:, :], ACT.Copy).then_inc(S["x2T_copied"], 1)

            def e_sel(g):
                act.wait_ge(S["logits_ready"], g + 1)
                if g >= 1:
                    act.wait_ge(S["sel_plus_one"], g)
                act.activation(sel[:, 0].rearrange("p t e -> p (t e)"), banks[7][:, 0:GT * E], ACT.Exp, scale=-1.0)\
                   .then_inc(S["sel_exp"], 1)
            act.wait_ge(S["m_u"], GROUPS - 1)
            e_xT(0)
            e_qv(0)
            e_a(0)
            e_aT(0)
            act.wait_ge(S["bm_ps"], 1)
            act.activation(bmax[:, :], banks[7][:, 0:TILES], ACT.Ln, bias=tiny[:, 0:1]).then_inc(S["bm_log"], 1)
            act.wait_ge(S["bm_log"], 1)
            act.activation(bmax[:, :], bmax[:, :], ACT.Exp, scale=0.5).then_inc(S["bm_log"], 1)

            e_r1(0)
            for g in range(GROUPS):
                nxt, old = g + 1 < GROUPS, g >= 1
                if nxt:
                    e_xT(g + 1)
                e_exp(g, 0)
                if g == RG + 1:
                    e_exp(g, 1)
                    e_qv(g + 1)
                    e_oT(g - 1)
                else:
                    if old:
                        e_oT(g - 1)
                    if nxt:
                        e_qv(g + 1)
                    e_exp(g, 1)
                if nxt:
                    e_a(g + 1)
                e_exp(g, 2)
                if nxt:
                    e_aT(g + 1)
                e_exp(g, 3)
                if nxt:
                    e_r1(g + 1)
                if old:
                    e_x2(g - 1)
                    e_sel(g - 1)

            def f_xT(n):
                act.wait_ge(S["rowsT_in_psum"], n + 1)
                if n >= 2:
                    act.wait_ge(S["hidden_ps"], n - 1)
                act.activation(xgT[:, n % 2], banks[n % 2][:, :], ACT.Copy).then_inc(S["rowsT_copied"], 1)

            def f_h(n):
                act.wait_ge(S["hidden_ps"], n + 1)
                if n >= 2:
                    act.wait_ge(S["y_in_psum"], n - 1)
                act.activation(hexT[:, n % 2], banks[2 + n % 2][:, :], ACT.Relu).then_inc(S["hidden_done"], 1)

            def f_y(n):
                act.wait_ge(S["y_in_psum"], n + 1)
                if n >= 2:
                    act.wait_ge(S[f"y_st{n % 2}"], 16 * (n // 2))
                act.activation(yb[:, n % 2].rearrange("p t d -> p (t d)"), banks[4 + n % 2][:, :], ACT.Copy)\
                   .then_inc(S["y_copied"], 1)

            def store_chunk(n):
                b, c = block_chunk(n)
                act.wait_ge(S["y_copied"], n + 1)
                act.dma_start(y_dram[b][c * GTOK:(c + 1) * GTOK, :].rearrange("(t p) d -> p t d", p=P), yb[:, n % 2])\
                   .then_inc(S[f"y_st{n % 2}"], 16)
            e_oT(GROUPS - 1)
            e_x2(GROUPS - 1)
            e_sel(GROUPS - 1)
            f_xT(0)
            for n in range(CHUNKS):
                if n + 1 < CHUNKS:
                    f_xT(n + 1)
                f_h(n)
                if n >= 1:
                    f_y(n - 1)
                    store_chunk(n - 1)
            f_y(CHUNKS - 1)
            store_chunk(CHUNKS - 1)

        @block.vector
        def _(dve):
            dve.memset(zeros[:, :], 0.0).then_inc(S["c_dve"], 1)
            dve.memset(head_mask[:, :], 0.0).then_inc(S["s_prep"], 1)
            dve.memset(scan_keep[:, :], 1.0).then_inc(S["s_prep"], 1)
            dve.memset(onesE[:, :], 1.0).then_inc(S["s_prep"], 1)
            dve.memset(seq_ones[:, :], 0.0).then_inc(S["s_ones"], 1)
            dve.memset(ones_f[:, :], 1.0).then_inc(S["s_ones"], 1)
            dve.memset(tiny[:, :], 1e-37).then_inc(S["s_ones"], 1)
            dve.memset(two[:, :], 2.0).then_inc(S["s_ones"], 1)
            dve.wait_ge(S["s_prep"], 3)
            dve.wait_ge(S["s_ones"], 4)
            for b in range(2):
                dve.memset(seq_ones[L * b:L * (b + 1), L * b:L * (b + 1)], 1.0).then_inc(S["s_ones"], 1)
            dve.memset(scan_keep[:, 0:E * BT[0]].rearrange("p (e t) -> p e t", e=E)[:, :, 0:1], 0.0)\
               .then_inc(S["s_prep"], 1)
            dve.memset(scan_keep[:, E * BT[0]:E * TILES].rearrange("p (e t) -> p e t", e=E)[:, :, 0:1], 0.0)\
               .then_inc(S["s_prep"], 1)
            for k in range(GT):
                dve.memset(head_mask[HP * k:HP * k + HP, k:k + 1], 1.0).then_inc(S["s_prep"], 1)
            dve.wait_ge(S["ld_small"], 16)
            dve.scalar_tensor_tensor(out=f_abs[:, :], in0=cols[:, 4:10], scalar=-1.0, in1=cols[:, 4:10],
                                     op0=ALU.mult, op1=ALU.max).then_inc(S["s_abs"], 1)
            dve.tensor_scalar(f_sgn[:, :], cols[:, 4:10], 0.0, None, ALU.is_lt).then_inc(S["s_prep"], 1)
            dve.wait_ge(S["s_prep"], 10)
            dve.tensor_scalar(f_sgn[:, :], f_sgn[:, :], -2.0, 1.0, ALU.mult, ALU.add).then_inc(S["s_prep"], 1)
            dve.wait_ge(S["s_prep"], 11)
            dve.wait_ge(S["s_powed"], 1)
            dve.tensor_tensor(f_abs[:, :], f_abs[:, :], f_sgn[:, :], ALU.mult).then_inc(S["s_prep"], 1)
            dve.wait_ge(S["s_prep"], 12)
            dve.wait_ge(S["c_pool"], 9)
            for a in range(2):
                dve.tensor_scalar(eo_diag[:, a], ident[:, :], f_abs[:, a:a + 1], None, ALU.mult)\
                   .then_inc(S["s_diag"], 1)
            dve.wait_ge(S["s_eo_ps"], 1)
            dve.wait_ge(S["ld_w"], 32)
            for a in range(2):
                for f in range(2):
                    dve.scalar_tensor_tensor(out=swn_t[:, a, f], in0=banks[7][:, HID * a:HID * a + HID],
                                             scalar=f_abs[:, 2 + 2 * a + f:3 + 2 * a + f],
                                             in1=swn_t[:, a, f], op0=ALU.mult, op1=ALU.mult).then_inc(S["s_prep"], 1)
            dve.tensor_tensor(sb_eo[:, :], cols[:, 2:4], f_abs[:, 0:2], ALU.mult).then_inc(S["s_prep"], 1)
            dve.wait_ge(S["s_prep"], 17)
            for a in range(2):
                for f in range(2):
                    dve.tensor_tensor(wn_t[:, a, f], swn_t[:, a, f], wn_t[:, a, f], ALU.add).then_inc(S["s_wn"], 1)
            dve.tensor_tensor(bn_col[:, :], sb_eo[:, :], cols[:, 0:2], ALU.add).then_inc(S["s_wn"], 1)
            dve.wait_ge(S["s_wn"], 5)
            dve.tensor_scalar(bn_col[:, 1:2], bn_col[:, 1:2], -1.0, None, ALU.mult).then_inc(S["s_wn"], 1)
            dve.wait_ge(S["ld_rows"], 16 * 3)
            dve.tensor_tensor(base[:, :], base[:, :], bias_b[:, 0], ALU.add).then_inc(S["s_wn"], 1)
            for t in (a_tok, b_tok):
                dve.memset(t[:, :, :, :, :].rearrange("p u t h x -> p (u t h x)"), 0.0).then_inc(S["s_prep"], 1)
            dve.wait_ge(S["s_prep"], 19)
            dve.memset(a_tok[:, :, :, :, HD + 1:HD + 2].rearrange("p u t h x -> p (u t h) x"), 1.0)\
               .then_inc(S["s_prep"], 1)

            def gate_min(n):
                u = n % 2
                dve.wait_ge(S["m_gate"], n + 1)
                dve.tensor_scalar(mish[:, u, 2], mish[:, u, 0], 20.0, None, ALU.min).then_inc(S["m_min"], 1)

            def gate_tanh(n):
                u = n % 2
                dve.wait_ge(S["m_exp"], n + 1)
                if n >= 2:
                    dve.wait_ge(S["m_gin"], n - 1)
                dve.scalar_tensor_tensor(out=mish[:, u, 3], in0=mish[:, u, 2], scalar=2.0, in1=mish[:, u, 2],
                                         op0=ALU.add, op1=ALU.mult).then_inc(S["m_num"], 1)

            def gate_out(n):
                u = n % 2
                dve.wait_ge(S["m_rec0"], n + 1)
                dve.scalar_tensor_tensor(out=mish[:, u, 2], in0=mish[:, u, 3], scalar=2.0, in1=mish[:, u, 4],
                                         op0=ALU.add, op1=ALU.mult).then_inc(S["m_rec"], 1)
                dve.wait_ge(S["m_rec"], 2 * n + 1)
                dve.scalar_tensor_tensor(out=mish[:, u, 4], in0=mish[:, u, 2], scalar=2.0, in1=mish[:, u, 4],
                                         op0=ALU.subtract, op1=ALU.mult).then_inc(S["m_rec"], 1)
                dve.wait_ge(S["m_rec"], 2 * n + 2)
                dve.wait_ge(S["m_gin"], n + 1)
                if n >= 2:
                    dve.wait_ge(S["w3_ps"], n - 1)
                dve.tensor_tensor(mish[:, u, 5], mish[:, u, 1], mish[:, u, 4], ALU.mult).then_inc(S["m_u"], 1)

            def ln1(n):
                u = n % 2
                ts = slice(GT * n, GT * n + GT)
                dve.wait_ge(S["w3_ps"], n + 1)
                dve.tensor_tensor(h[:, ts], banks[6 + u][:, :].rearrange("p (t d) -> p t d", t=GT),
                                  base[:, :].unsqueeze(1).to_broadcast([P, GT, D]), ALU.add).then_inc(S["h_done"], 1)
                dve.wait_ge(S["h_done"], n + 1)
                for t in range(GT):
                    dve.bn_stats(stats[:, t, :], h[:, GT * n + t, :]).then_inc(S["ln_stat"], 1)
                dve.wait_ge(S["ln_stat"], GT * (n + 1))
                for t in range(GT):
                    dve.bn_aggr(all_mv[:, GT * n + t, :], stats[:, t, :]).then_inc(S["ln_mv"], 1)
                dve.wait_ge(S["ln_mv"], GT * (n + 1))
                if n >= 2:
                    dve.wait_ge(S["ln_rstd"], n - 1)
                dve.tensor_scalar(veps[:, u], all_mv[:, ts, 1:2].rearrange("p t a -> p (t a)"), EPS, None, ALU.add)\
                   .then_inc(S["ln_eps"], 1)

            def ln1_apply(n):
                dve.wait_ge(S["ln_rstd"], n + 1)
                for t in range(GT):
                    dve.tensor_scalar(xn[:, GT * n + t], h[:, GT * n + t], all_mv[:, GT * n + t, 0:1],
                                      rstd[:, n % 2, t:t + 1], ALU.subtract, ALU.mult).then_inc(S["ln_xn"], 1)
                dve.wait_ge(S["ln_mv"], GT * (n + 1))
                ts = slice(GT * n, GT * n + GT)
                dve.tensor_tensor(n2[:, ts], all_mv[:, ts, 1:2].rearrange("p t a -> p (t a)"), rstd[:, n % 2],
                                  ALU.mult).then_inc(S["n2_s"], 1)
                dve.wait_ge(S["n2_s"], 2 * n + 1)
                dve.scalar_tensor_tensor(out=n2[:, ts], in0=n2[:, ts], scalar=float(D), in1=rstd[:, n % 2],
                                         op0=ALU.mult, op1=ALU.mult).then_inc(S["n2_s"], 1)
            def d_v(g):
                u = g % 2
                dve.wait_ge(S["q_squared"], 2 * g + 2)
                if g >= 2:
                    dve.wait_ge(S["seq_norm_ps"], g - 1)
                dve.tensor_reduce(v8[:, u], sq[:, :].rearrange("p (x d) -> p x d", d=HD), AX_X, ALU.add)\
                   .then_inc(S["q_norms"], 1)
                dve.wait_ge(S["q_norms"], g + 1)
                if g >= 2:
                    dve.wait_ge(S["aT_in_psum"], 2 * (g - 1))
                dve.tensor_copy(a_tok[:, u, :, :, HD:HD + 1].rearrange("p t h x -> p (t h) x"),
                                v8[:, u].unsqueeze(2)).then_inc(S["q_rows_done"], 1)

            for n in range(GROUPS + 4):
                if n < GROUPS:
                    gate_min(n)
                if 1 <= n <= GROUPS:
                    gate_out(n - 1)
                if n < GROUPS:
                    gate_tanh(n)
                if 3 <= n < GROUPS + 3:
                    ln1(n - 3)
                if n == GROUPS + 3:
                    d_v(0)
                if n >= 4:
                    ln1_apply(n - 4)
            dve.wait_ge(S["n2_ps"], 1)
            dve.tensor_reduce(seqmax[:, :], banks[7][0:TILES, 0:P].rearrange("p (b l) -> p b l", b=2), AX_X, ALU.max)\
               .then_inc(S["bm_s"], 1)
            dve.wait_ge(S["bm_s"], 1)
            dve.tensor_copy(seqmax_b[:, :].rearrange("p (b l) -> p b l", b=2),
                            seqmax[:, :].unsqueeze(2).to_broadcast([TILES, 2, L])).then_inc(S["bm_s"], 1)
            dve.wait_ge(S["bm_ps"], 1)
            dve.wait_ge(S["bm_log"], 2)
            dve.reciprocal(bmaxh[:, :], bmax[:, :]).then_inc(S["bm_dve"], 1)
            dve.wait_ge(S["bm_dve"], 1)
            dve.tensor_tensor(bmaxh[:, :], banks[7][:, 0:TILES], bmaxh[:, :], ALU.mult).then_inc(S["bm_dve"], 1)
            dve.wait_ge(S["bm_dve"], 2)
            dve.tensor_tensor(bmaxh[:, :], bmax[:, :], bmaxh[:, :], ALU.add).then_inc(S["bm_dve"], 1)
            dve.wait_ge(S["bm_dve"], 3)
            dve.tensor_scalar(bmaxh[:, :], bmaxh[:, :], 0.25, None, ALU.mult).then_inc(S["bm_dve"], 1)
            def d_c(g):
                u = g % 2
                a0, ta, tb = c8[:, u, 1], c8[:, u, 0], c8[:, u, 2]
                dve.wait_ge(S["root_first"], 2 * (g + 1))
                dve.reciprocal(tb, a0).then_inc(S["scale_steps"], 1)
                dve.wait_ge(S["scale_steps"], 6 * g + 1)
                dve.tensor_tensor(ta, banks[0][:, 0:GT * HEADS], tb, ALU.mult).then_inc(S["scale_steps"], 1)
                dve.wait_ge(S["scale_steps"], 6 * g + 2)
                dve.tensor_tensor(ta, ta, a0, ALU.add).then_inc(S["scale_steps"], 1)
                dve.wait_ge(S["scale_steps"], 6 * g + 3)
                if g == 0:
                    dve.wait_ge(S["bm_dve"], 4)
                dve.tensor_tensor(ta.rearrange("p (t h) -> p t h", t=GT), ta.rearrange("p (t h) -> p t h", t=GT),
                                  bmaxh[:, GT * g:GT * g + GT].unsqueeze(2).to_broadcast([P, GT, HEADS]),
                                  ALU.mult).then_inc(S["scale_steps"], 1)
                dve.wait_ge(S["scale_steps"], 6 * g + 4)
                dve.tensor_scalar(ta, ta, 1e-10, 0.005, ALU.add, ALU.mult).then_inc(S["scale_steps"], 1)
                dve.wait_ge(S["scale_steps"], 6 * g + 5)
                dve.reciprocal(tb, ta).then_inc(S["scale_steps"], 1)
                dve.wait_ge(S["scale_steps"], 6 * g + 6)
                dve.wait_ge(S["q_copied"], 2 * (g + 1))
                if g >= 2:
                    dve.wait_ge(S["bT_in_psum"], 2 * (g - 1))
                dve.tensor_tensor(b_tok[:, u, :, :, 0:HD].rearrange("p t h d -> p (t h) d"),
                                  a_tok[:, u, :, :, 0:HD].rearrange("p t h d -> p (t h) d"),
                                  c8[:, u, 2].unsqueeze(2).to_broadcast([P, GT * HEADS, HD]), ALU.mult)\
                   .then_inc(S["b_rows_done"], 1)
                dve.tensor_scalar(b_tok[:, u, :, :, HD:HD + 1].rearrange("p t h x -> p (t h) x"),
                                  c8[:, u, 2].unsqueeze(2), -0.5, None, ALU.mult).then_inc(S["b_rows_done"], 1)
                dve.scalar_tensor_tensor(out=b_tok[:, u, :, :, HD + 1:HD + 2].rearrange("p t h x -> p (t h) x"),
                                         in0=c8[:, u, 2].unsqueeze(2), scalar=-0.5, in1=v8[:, u].unsqueeze(2),
                                         op0=ALU.mult, op1=ALU.mult).then_inc(S["b_rows_done"], 1)

            def d_r0(g):
                dve.wait_ge(S["bT_in_psum"], 2 * g + 1)
                if g >= 2:
                    dve.wait_ge(S["scores_ready"], GT * (g - 1))
                dve.tensor_tensor(
                    rdiag[:, g % 2, 0],
                    banks[0][:, :].rearrange("p (s t) -> p s t", s=GSEQ).unsqueeze(2)
                    .to_broadcast([P, GSEQ, GT, L]),
                    head_mask[:, :].unsqueeze(1).unsqueeze(3).to_broadcast([P, GSEQ, GT, L]), ALU.mult)\
                   .then_inc(S["rdiag0_done"], 1)

            def d_o(g, t):
                n = GT * g + t
                dve.wait_ge(S["heads_in_psum"], n + 1)
                src = banks[5 + n % 2][:, :].rearrange("p (x c) -> p x c", c=64)
                for k in range(2):
                    r = slice(L * k, L * k + L)
                    dve.reciprocal(rden[r, n % 2, 0:8], src[r, :, VW * k + HD]).then_inc(S["sums_inverted"], 1)
                dve.wait_ge(S["sums_inverted"], 2 * (n + 1))
                if g >= 2:
                    dve.wait_ge(S["oT_in_psum"], g - 1)
                for k in range(2):
                    r = slice(L * k, L * k + L)
                    dve.tensor_tensor(o_sb[r, g % 2, t].rearrange("p b j d -> p j b d"),
                                      src[r, :, VW * k:VW * k + HD].rearrange("p (j b) d -> p j b d", b=2),
                                      rden[r, n % 2, 0:8].rearrange("p (j b) -> p j b", b=2).unsqueeze(3)
                                      .to_broadcast([L, 4, 2, HD]), ALU.mult).then_inc(S["heads_done"], 1)

            def d_ln2(g):
                u = g % 2
                ts = slice(GT * g, GT * g + GT)
                dve.wait_ge(S["proj_in_psum"], g + 1)
                dve.wait_ge(S["hb_done"], GT * (g + 1))
                dve.tensor_tensor(h[:, ts], banks[7][:, :].rearrange("p (t d) -> p t d", t=GT), h[:, ts], ALU.add)\
                   .then_inc(S["h_added"], 1)
                dve.wait_ge(S["h_added"], g + 1)
                for t in range(GT):
                    dve.bn_stats(stats[:, t, :], h[:, GT * g + t, :]).then_inc(S["ln2_stat"], 1)
                dve.wait_ge(S["ln2_stat"], GT * (g + 1))
                for t in range(GT):
                    dve.bn_aggr(mv[:, u, t, :], stats[:, t, :]).then_inc(S["ln2_mv"], 1)
                dve.wait_ge(S["ln2_mv"], GT * (g + 1))
                dve.tensor_scalar(veps[:, u], mv[:, u, :, 1:2].rearrange("p t a -> p (t a)"), EPS, None, ALU.add)\
                   .then_inc(S["ln2_eps"], 1)

            def d_ln2_apply(g):
                dve.wait_ge(S["ln2_rstd"], g + 1)
                for t in range(GT):
                    dve.tensor_scalar(xn[:, GT * g + t], h[:, GT * g + t], mv[:, g % 2, t, 0:1],
                                      rstd[:, g % 2, t:t + 1], ALU.subtract, ALU.mult).then_inc(S["ln2_xn"], 1)

            def d_top(g):
                dve.wait_ge(S["sel_exp"], g + 1)
                dve.tensor_scalar(sel[:, 1], sel[:, 0], 1.0, None, ALU.add).then_inc(S["sel_plus_one"], 1)
                dve.wait_ge(S["sel_plus_one"], g + 1)
                dve.reciprocal(sel[:, 2], sel[:, 1]).then_inc(S["sel_sigmoid"], 1)
                dve.wait_ge(S["sel_sigmoid"], g + 1)
                for t in range(GT):
                    dve.max(m8[:, t], sel[:, 2, t]).then_inc(S["top_values"], 1)
                dve.wait_ge(S["top_values"], GT * (g + 1))
                for t in range(GT):
                    dve.max_index(i8[:, t], m8[:, t], sel[:, 2, t]).then_inc(S["top_indices"], 1)
                ts = slice(GT * g, GT * g + GT)
                dve.tensor_copy(topw[:, ts], m8[:, :, 0:2]).then_inc(S["hot_done"], 1)
                dve.wait_ge(S["top_indices"], GT * (g + 1))
                dve.tensor_copy(idxf[:, :, :], i8[:, :, 0:2]).then_inc(S["top_indices_f"], 1)
                dve.wait_ge(S["top_indices_f"], g + 1)
                for k in range(2):
                    dve.tensor_tensor(hot[:, k, :, ts], iota_e[:, :].unsqueeze(2).to_broadcast([P, E, GT]),
                                      idxf[:, :, k].unsqueeze(1).to_broadcast([P, E, GT]), ALU.is_equal)\
                       .then_inc(S["hot_done"], 1)

            rd = [0]

            def step(ins):
                rd[0] += 1
                ins.then_inc(S["route_steps"], 1)
                dve.wait_ge(S["route_steps"], rd[0])

            def d_route_mask(b):
                bs = slice(FIRST[b], FIRST[b] + BT[b])
                dve.wait_ge(S["hot_done"], 3 * (RG if b == 0 else GROUPS))
                dve.tensor_tensor(mb_all[:, 0:E * BT[b]].rearrange("p (e t) -> p e t", e=E),
                                  hot[:, 0, :, bs], hot[:, 1, :, bs], ALU.add).then_inc(S["mask_done"], 1)

            def d_route_load(b):
                for i, (k, bank, part) in enumerate(ROUTE_PARTS[b]):
                    dve.wait_ge(S["counts_ps"], len(ROUTE_PARTS[0]) * b + i + 1)
                    dve.tensor_copy(rt_all[:, k, part], banks[bank][:, 0:part.stop - part.start])\
                       .then_inc(S["counts_copied"], 1)

            def d_route(b):
                bt, n = BT[b], E * BT[b]
                flat = [rt_all[:, k, 0:n] for k in range(4)]
                rt = [f.rearrange("p (e t) -> p e t", e=E) for f in flat]
                dve.wait_ge(S["counts_copied"], len(ROUTE_PARTS[0]) + len(ROUTE_PARTS[1]) * b)
                step(dve.tensor_tensor_scan(flat[2], scan_keep[:, E * FIRST[b]:E * FIRST[b] + n], flat[0], 0.0,
                                            ALU.mult, ALU.add))
                step(dve.tensor_tensor(flat[0], flat[2], flat[0], ALU.subtract))
                step(dve.tensor_tensor(rt[3], rt[2][:, :, bt - 1:bt].to_broadcast([P, E, bt]),
                                       thr[:, 0:bt].unsqueeze(1).to_broadcast([P, E, bt]), ALU.is_gt))
                step(dve.tensor_reduce(cnt[:, 0], rt[3], AX_X, ALU.add))
                step(dve.tensor_tensor_scan(cnt[:, 1], onesE[:, :], cnt[:, 0], 0.0, ALU.mult, ALU.add))
                step(dve.tensor_tensor(cnt[:, 2], cnt[:, 1], cnt[:, 0], ALU.subtract))
                step(dve.tensor_scalar(cnt[:, 3], cnt[:, 1], part_no[:, 0:1], None, ALU.is_le))
                dve.tensor_reduce(ecol[:, :], cnt[:, 3], AX_X, ALU.add).then_inc(S["tile_expert_col"], 1)
                step(dve.scalar_tensor_tensor(out=rt[0], in0=cnt[:, 2].unsqueeze(2).to_broadcast([P, E, bt]),
                                              scalar=float(P), in1=rt[0], op0=ALU.mult, op1=ALU.add))
                step(dve.tensor_tensor(flat[0], flat[1], flat[0], ALU.add))
                bs = slice(FIRST[b], FIRST[b] + bt)
                for k in range(2):
                    step(dve.tensor_tensor(rt[2], rt[0], hot[:, k, :, bs], ALU.mult))
                    step(dve.tensor_reduce(posf[:, k, 0:bt], rt[2].rearrange("p e t -> p t e"), AX_X, ALU.add))
                dve.tensor_copy(pos_u[:, :, bs], posf[:, :, 0:bt]).then_inc(S["slots_done"], 1)

            def d_etab(b):
                dve.wait_ge(S["tile_expert_ps"], b + 1)
                dve.tensor_scalar(etab[0:1, b, :], banks[7][0:1, 0:P], float(E - 1), None, ALU.min)\
                   .then_inc(S["tile_expert_done"], 1)
            d_c(0)
            d_r0(0)
            for g in range(GROUPS):
                nxt, old = g + 1 < GROUPS, g >= 1
                if g == RG + 2:
                    d_etab(0)
                if g == RG + 1:
                    d_route_load(0)
                    d_route(0)
                if nxt:
                    d_v(g + 1)
                d_o(g, 0)
                if old:
                    d_ln2(g - 1)
                if nxt:
                    d_c(g + 1)
                if old:
                    d_ln2_apply(g - 1)
                d_o(g, 1)
                if nxt:
                    d_r0(g + 1)
                d_o(g, 2)
                d_o(g, 3)
                if old:
                    d_top(g - 1)
                if g == RG:
                    d_route_mask(0)

            def key_copy(n):
                b, c = block_chunk(n)
                if n >= 2:
                    dve.wait_ge(S["hidden_ps"], n - 1)
                _, experts = nc.values_load_multi_w_load_instructions(
                    etab[0:1, b, c * GT:c * GT + GT], engines=[mybir.EngineType.DVE], min_val=0, max_val=E - 1)
                for t, e in enumerate(experts):
                    dve.tensor_copy(keyc[:, n % 2, t:t + 1, :], keys_sb[:, bass.ds(e, 1), :]).then_inc(S["keys_copied"], 1)

            def combine(t):
                g = t // GT
                dve.wait_ge(S[f"gat{t % YR}"], 32 * (t // YR + 1))
                if t % GT == 0 and g >= OR:
                    dve.wait_ge(S[f"out_st{g % OR}"], 16 * (g // OR))
                dve.scalar_tensor_tensor(out=h[:, t], in0=yg[:, t % YR, 0], scalar=topw[:, t, 0:1], in1=h[:, t],
                                         op0=ALU.mult, op1=ALU.add).then_inc(S["first_added"], 1)
                dve.wait_ge(S["first_added"], t + 1)
                dve.scalar_tensor_tensor(out=ob[:, g % OR, t % GT], in0=yg[:, t % YR, 1], scalar=topw[:, t, 1:2],
                                         in1=h[:, t], op0=ALU.mult, op1=ALU.add).then_inc(S["result_done"], 1)

            d_ln2(GROUPS - 1)
            d_ln2_apply(GROUPS - 1)
            dve.wait_ge(S["ld_exp"], 32)
            dve.wait_ge(S["heads_in_psum"], TILES)
            key_copy(0)
            key_copy(1)
            d_top(GROUPS - 1)
            d_route_mask(1)
            d_route_load(1)
            d_route(1)
            for n in range(CHUNKS):
                if n == ROW_AT:
                    d_etab(1)
                if n + 2 < CHUNKS:
                    key_copy(n + 2)
                if n >= SCH[0] + 2:
                    combine(n - SCH[0] - 2)
            for t in range(SCH[1] - 2, TILES):
                combine(t)

        @block.tensor
        def _(pe):
            def linear(n):
                u = n % 2
                pe.wait_ge(S[f"ld_x{n}"], 16)
                for a in range(2):
                    if n >= 2:
                        pe.wait_ge(S["m_gate" if a == 0 else "m_inner"], n - 1)
                    for f in range(2):
                        mm = pe.matmul(banks[2 + 2 * u + a][:, :], wn_t[:, a, f, :],
                                       xT[:, f, GTOK * n:GTOK * n + GTOK], start=(f == 0), stop=(f == 1))
                    mm.then_inc(S["lin_ps"], 1)

            def embed(n):
                u = n % 2
                pe.wait_ge(S["m_u"], n + 1)
                if n >= 2:
                    pe.wait_ge(S["h_done"], n - 1)
                for t in range(GT):
                    mm = pe.matmul(banks[6 + u][:, D * t:D * t + D], mish[:, u, 5, P * t:P * t + P], w3T[:, :],
                                   start=True, stop=True)
                mm.then_inc(S["w3_ps"], 1)
            pe.wait_ge(S["c_pool"], 9)
            pe.wait_ge(S["s_ones"], 6)
            pe.wait_ge(S["s_diag"], 2)
            pe.matmul(banks[7][:, 0:2 * HID], ones_f[:, :], eo_diag[:, :, :].rearrange("p a o -> p (a o)"),
                      start=True, stop=True).then_inc(S["s_eo_ps"], 1)
            pe.wait_ge(S["s_wn"], 7)
            def t_x(g):
                pe.wait_ge(S["ln_xn"], GT * (g + 1))
                if g >= 1:
                    pe.wait_ge(S["rdiag0_done"], g)
                for t in range(GT):
                    mm = pe.transpose(banks[0][:, P * t:P * t + P], xn[:, GT * g + t], ident[:, :])
                mm.then_inc(S["xT_in_psum"], 1)

            def t_qv(g):
                pe.wait_ge(S["xT_copied"], g + 1)
                pe.wait_ge(S["ld_attn"], 16 * 4)
                if g >= 1:
                    pe.wait_ge(S["rdiag1_done"], GT * g)
                    pe.wait_ge(S["aT_copied"], 2 * g)
                for t in range(GT):
                    pe.matmul(banks[1 + t // 2][:, 256 * (t % 2):256 * (t % 2) + 256], xnT[:, g % 2, P * t:P * t + P],
                              wqv[:, :], start=True, stop=True)\
                      .then_inc(S["qv_in_psum"], 1)

            def t_a2(g):
                pe.wait_ge(S["q_norms"], g + 1)
                pe.wait_ge(S["xT_copied"], g + 1)
                pe.matmul(banks[0][:, 0:GT * HEADS], seq_ones[:, :], v8[:, g % 2], start=True, stop=True)\
                  .then_inc(S["seq_norm_ps"], 1)

            def t_at(g):
                pe.wait_ge(S["q_rows_done"], g + 1)
                pe.wait_ge(S["q_copied"], 2 * (g + 1))
                pe.wait_ge(S["v_copied"], GT * (g + 1))
                for f in range(2):
                    for t in range(GT):
                        mm = pe.transpose(banks[1 + f][:, P * t:P * t + P],
                                          a_tok[:, g % 2, t, 4 * f:4 * f + 4, :].rearrange("p h x -> p (h x)"),
                                          ident[:, :])
                    mm.then_inc(S["aT_in_psum"], 1)

            def t_bt(g):
                pe.wait_ge(S["b_rows_done"], 3 * (g + 1))
                for f in range(2):
                    pe.wait_ge(S["aT_copied"], 2 * g + 1)
                    for t in range(GT):
                        mm = pe.transpose(banks[f][:, P * t:P * t + P],
                                          b_tok[:, g % 2, t, 4 * f:4 * f + 4, :].rearrange("p h x -> p (h x)"),
                                          ident[:, :])
                    mm.then_inc(S["bT_in_psum"], 1)

            def t_s(g, t):
                n = GT * g + t
                if t == 0:
                    pe.wait_ge(S["rdiag0_done"], g + 1)
                    pe.wait_ge(S["rdiag1_done"], GT * (g + 1))
                    pe.wait_ge(S["aT_copied"], 2 * (g + 1))
                if n >= 2:
                    pe.wait_ge(S["probs_ready"], n - 1)
                for f in range(2):
                    for b in range(2):
                        s = 2 * t + b
                        mm = pe.matmul(banks[3 + n % 2][L * b:L * b + L, 256 * f:256 * f + 256],
                                       aT[:, g % 2, f, L * s:L * s + L],
                                       rdiag[:, g % 2, f, s].rearrange("p h t -> p (h t)"), start=True, stop=True)
                mm.then_inc(S["scores_ready"], 1)

            def t_o(g, t):
                n = GT * g + t
                pe.wait_ge(S["probs_ready"], n + 1)
                if t == 0:
                    pe.wait_ge(S["v_copied"], GT * (g + 1))
                if n >= 2:
                    pe.wait_ge(S["heads_done"], 2 * (n - 1))
                for j in range(4):
                    mm = pe.matmul(banks[5 + n % 2][:, P * j:P * j + P], probs[:, n % 2, P * j:P * j + P],
                                   vbd[:, g % 2, t, :, 2 * VW * j:2 * VW * j + 64], start=True, stop=True)
                mm.then_inc(S["heads_in_psum"], 1)

            def t_ot(g):
                pe.wait_ge(S["heads_done"], 2 * GT * (g + 1))
                if g >= 1:
                    pe.wait_ge(S["sel_exp"], g)
                if g == RG:
                    pe.wait_ge(S["counts_copied"], len(ROUTE_PARTS[0]))
                if g == RG + 1:
                    pe.wait_ge(S["tile_expert_done"], 1)
                for t in range(GT):
                    mm = pe.transpose(banks[7][:, P * t:P * t + P],
                                      o_sb[:, g % 2, t].rearrange("p b j d -> p (b j d)"), ident[:, :])
                mm.then_inc(S["oT_in_psum"], 1)

            def t_y(g):
                pe.wait_ge(S["oT_copied"], g + 1)
                for t in range(GT):
                    for k in range(2):
                        for b in range(2):
                            r = slice(L * b, L * b + L)
                            c = P * t + L * k
                            mm = pe.matmul(banks[7][r, D * t:D * t + D], oT[r, 0, c:c + L], wp2[r, k, :],
                                           start=(k == 0), stop=(k == 1))
                mm.then_inc(S["proj_in_psum"], 1)

            def t_x2(g):
                pe.wait_ge(S["ln2_xn"], GT * (g + 1))
                for t in range(GT):
                    mm = pe.transpose(banks[7][:, P * t:P * t + P], xn[:, GT * g + t], ident[:, :])
                mm.then_inc(S["x2T_in_psum"], 1)

            def t_l(g):
                pe.wait_ge(S["x2T_copied"], g + 1)
                for t in range(GT):
                    mm = pe.matmul(banks[7][:, E * t:E * t + E], x2T[:, 1, P * t:P * t + P], selT[:, :],
                                   start=True, stop=True)
                mm.then_inc(S["logits_ready"], 1)

            def t_tt(b, i):
                k, bank, part = ROUTE_PARTS[b][i]
                if i == 0:
                    pe.wait_ge(S["mask_done"], b + 1)
                    pe.wait_ge(S["sel_exp"], RG if b == 0 else GROUPS)
                if i >= 2:
                    pe.wait_ge(S["counts_copied"], i - 1)
                pe.matmul(banks[bank][:, 0:part.stop - part.start], (ones_bf, tri)[k][:, :], mb_all[:, part],
                          start=True, stop=True).then_inc(S["counts_ps"], 1)

            def t_row(b):
                pe.wait_ge(S["tile_expert_col"], b + 1)
                pe.wait_ge(S["sel_exp"], RG + 1 if b == 0 else GROUPS)
                pe.matmul(banks[7][0:1, 0:P], ecol[:, 0:1], ident[:, :], start=True, stop=True)\
                  .then_inc(S["tile_expert_ps"], 1)
            for n in range(GROUPS + 2):
                if n < GROUPS:
                    linear(n)
                if n == GROUPS + 1:
                    t_x(0)
                if n >= 2:
                    embed(n - 2)
            pe.wait_ge(S["m_gate"], GROUPS - 1)
            t_qv(0)
            t_a2(0)
            t_at(0)
            pe.wait_ge(S["n2_s"], 2 * GROUPS)
            pe.wait_ge(S["h_done"], GROUPS)
            pe.transpose(banks[7][0:TILES, 0:P], n2[:, :], ident[:, :]).then_inc(S["n2_ps"], 1)
            pe.wait_ge(S["bm_s"], 2)
            pe.transpose(banks[7][:, 0:TILES], seqmax_b[:, :], ident[0:TILES, 0:TILES]).then_inc(S["bm_ps"], 1)
            t_bt(0)
            for g in range(GROUPS):
                nxt, old = g + 1 < GROUPS, g >= 1
                if nxt:
                    t_x(g + 1)
                t_s(g, 0)
                if g == RG + 1:
                    t_tt(0, 0)
                    t_tt(0, 1)
                    t_s(g, 1)
                    t_tt(0, 2)
                    t_tt(0, 3)
                    pe.wait_ge(S["counts_copied"], len(ROUTE_PARTS[0]))
                    t_qv(g + 1)
                    t_ot(g - 1)
                else:
                    if old:
                        t_ot(g - 1)
                    if nxt:
                        t_qv(g + 1)
                    t_s(g, 1)
                t_o(g, 0)
                if old:
                    t_y(g - 1)
                if nxt:
                    t_a2(g + 1)
                t_s(g, 2)
                if nxt:
                    t_at(g + 1)
                t_o(g, 1)
                t_s(g, 3)
                if nxt:
                    t_bt(g + 1)
                t_o(g, 2)
                if old:
                    t_x2(g - 1)
                t_o(g, 3)
                if old:
                    t_l(g - 1)
                if g == RG + 1:
                    t_row(0)

            def f_tp(n):
                pe.wait_ge(S[f"xg_l{n % XR}"], 16 * (n // XR + 1))
                if n >= 2:
                    pe.wait_ge(S["rowsT_copied"], n - 1)
                for t in range(GT):
                    mm = pe.transpose(banks[n % 2][:, P * t:P * t + P], xg[:, n % XR, t], ident[:, :])
                mm.then_inc(S["rowsT_in_psum"], 1)

            def f_m1(n):
                pe.wait_ge(S["rowsT_copied"], n + 1)
                pe.wait_ge(S["keys_copied"], GT * (n + 1))
                if n < 2:
                    pe.wait_ge(S["probs_ready"], TILES)
                    pe.wait_ge(S["heads_done"], 2 * TILES)
                if n >= 2:
                    pe.wait_ge(S["hidden_done"], n - 1)
                for t in range(GT):
                    mm = pe.matmul(banks[2 + n % 2][:, P * t:P * t + P], keyc[:, n % 2, t], xgT[:, n % 2, P * t:P * t + P],
                                   start=True, stop=True)
                mm.then_inc(S["hidden_ps"], 1)

            held = {}

            def m2_experts(n):
                b, c = block_chunk(n)
                _, held[n] = nc.values_load_multi_w_load_instructions(
                    etab[0:1, b, c * GT:c * GT + GT], engines=[mybir.EngineType.PE], min_val=0, max_val=E - 1)

            def f_m2(n):
                experts = held.pop(n)
                pe.wait_ge(S["hidden_done"], n + 1)
                if n >= 2:
                    pe.wait_ge(S["y_copied"], n - 1)
                for t, e in enumerate(experts):
                    mm = pe.matmul(banks[4 + n % 2][:, P * t:P * t + P], hexT[:, n % 2, P * t:P * t + P],
                                   values_sb[:, bass.ds(e, 1), :].rearrange("p a d -> p (a d)"),
                                   start=True, stop=True)
                mm.then_inc(S["y_in_psum"], 1)
            pe.wait_ge(S["ld_exp"], 32)
            t_ot(GROUPS - 1)
            t_y(GROUPS - 1)
            t_x2(GROUPS - 1)
            t_l(GROUPS - 1)
            pe.wait_ge(S["heads_done"], 2 * TILES)
            for i in range(len(ROUTE_PARTS[1])):
                t_tt(1, i)
            f_tp(0)
            for n in range(CHUNKS):
                if n + 1 < CHUNKS:
                    f_tp(n + 1)
                if n == ROW_AT:
                    t_row(1)
                if n == SCH[0]:
                    pe.wait_ge(S["tile_expert_done"], 2)
                if n >= 1:
                    m2_experts(n - 1)
                f_m1(n)
                if n >= 1:
                    f_m2(n - 1)
            m2_experts(CHUNKS - 1)
            f_m2(CHUNKS - 1)


def kernel(**inputs):
    import numpy as np
    import concourse.bacc as bacc
    from concourse.bass_utils import run_bass_kernel_spmd

    a = {k.removeprefix("L0_"): np.asarray(v) for k, v in inputs.items()}
    seqs, _, high, wide = a["x"].shape
    emb = a["tok_W3_w"].shape[0]
    patch, heads = 16, 8
    hi, wi = high // patch, wide // patch
    tokens, hd, part = hi * wi, emb // heads, 128
    halves = patch * patch // part

    def layer(n, what):
        return a[f"tok_W{n}_{what}"].T.reshape(halves, part, -1)

    qkv = a["attn_W_qkv"].reshape(emb, hd, 2, heads)
    arrays = {
        "patches_t": a["x"].reshape(seqs, hi, patch, wi, patch).transpose(2, 4, 0, 1, 3)
        .reshape(halves, part, seqs * tokens),
        "noisy_w_t": np.stack([layer(1, "w"), layer(2, "w")]),
        "noisy_sw_t": np.stack([layer(1, "sw"), layer(2, "sw")]),
        "noisy_cols": np.stack([a["tok_W1_b"], a["tok_W2_b"], a["tok_W1_sb"], a["tok_W2_sb"],
                                a["tok_eps_out1"], a["tok_eps_out2"],
                                *a["tok_eps_in1"].reshape(halves, part), *a["tok_eps_in2"].reshape(halves, part)],
                               axis=1),
        "w3_t": a["tok_W3_w"].T,
        "bias_rows": np.stack([a["tok_W3_b"], a["attn_b_proj"]]),
        "w_qv": qkv.transpose(0, 2, 3, 1).reshape(emb, 2 * emb),
        "w_out": a["attn_W_proj"].reshape(heads // 2, 2, hd, emb).transpose(0, 2, 1, 3).reshape(emb // 2, 2, emb),
        "sel_t": a["ffn_expert_sel"].T,
        "keys_t": a["ffn_keys"].transpose(1, 0, 2),
        "values_t": a["ffn_values"].transpose(1, 0, 2),
    }
    at = np.arange(tokens, dtype=np.float32)[:, None]
    div = np.exp(np.arange(0, emb, 2, dtype=np.float32) * np.float32(-np.log(10000.0) / emb))
    ang = (at * div).astype(np.float32)
    code = np.stack([np.sin(ang), np.cos(ang)], axis=-1).reshape(tokens, emb).astype(np.float32)
    arrays["position_code"] = np.concatenate([code, code], axis=0)
    arrays = {k: np.ascontiguousarray(v) for k, v in arrays.items()}

    nc = bacc.Bacc("TRN2", target_bir_lowering=False, num_devices=1)
    args = [nc.dram_tensor(k, v.shape, mybir.dt.from_np(v.dtype), kind="ExternalInput").ap()
            for k, v in arrays.items()]
    args.append(nc.dram_tensor("tokens_out", (seqs, tokens, emb), F32, kind="ExternalOutput").ap())
    vit_tower_kernel(nc, *args)
    r = run_bass_kernel_spmd(nc, [arrays], core_ids=[0])
    return r.results[0]["tokens_out"]
```
